# Optimizing a Trainium2 kernel written in Bass

```python
import numpy as np
import jax
import jax.numpy as jnp

def _softmax(x, axis=-1):
    return jax.nn.softmax(x, axis=axis)

def _gelu(x):
    return jax.nn.gelu(x, approximate=True)

def _silu(x):
    return jax.nn.silu(x)

def _sigmoid(x):
    return jax.nn.sigmoid(x)

def _layernorm(x, axis=-1, eps=1e-05):
    m = jnp.mean(x, axis=axis, keepdims=True)
    v = jnp.var(x, axis=axis, keepdims=True)
    return (x - m) / jnp.sqrt(v + eps)

def _scatter_add(tgt, idx, src, axis=0):
    return tgt.at[idx].add(src)

def _segment_sum(src, seg, n):
    return jax.ops.segment_sum(src, seg, n)
kernel_name = 'mk_flamingo_gated_d1_seqx_r4_16366f'

def setup_inputs(seed: int=0):
    np.random.seed(seed)
    _w = jnp.asarray

    def _rec_inputs():
        import jax
        import jax.numpy as jnp
        _rk = jax.random.key(seed)
        x = 7.22e-05 + 1 * jax.random.normal(jax.random.fold_in(_rk, 1), (8, 256, 1024), jnp.float32)
        _lenS = 256 - jax.random.randint(jax.random.fold_in(_rk, 7), (8,), 0, max(1, 256 // 4) + 1, jnp.int32)
        _lenS2 = 256 - jax.random.randint(jax.random.fold_in(_rk, 8), (8,), 0, max(1, 256 // 4) + 1, jnp.int32)
        _ctx_4096P = jax.random.normal(jax.random.fold_in(_rk, 11), (8, 16, 1024), jnp.float32)
        _ctx_4096c = jax.random.dirichlet(jax.random.fold_in(_rk, 511), 0.3 * jnp.ones((16,), jnp.float32), (8, 256))
        _ctx_4096t = jnp.einsum('bsk,bkd->bsd', _ctx_4096c, _ctx_4096P)
        _ctx_4096t = _ctx_4096t * jax.lax.rsqrt(jnp.mean(jnp.square(_ctx_4096t)) + 1e-12) * 0.953939
        ctx_4096 = 4.13588e-05 + 0.999923 * (_ctx_4096t + 0.3 * jax.random.normal(jax.random.fold_in(_rk, 611), (8, 256, 1024), jnp.float32))
        _validS = jnp.arange(256)[None, :] < _lenS[:, None]
        _validS2 = jnp.arange(256)[None, :] < _lenS2[:, None]
        _causal = jnp.tril(jnp.ones((256, 256), dtype=bool))
        mask_1x1xSxS2_bk0 = jnp.logical_not(jnp.broadcast_to(_validS2[0:1, None, None, :], (1, 1, 256, 256)))
        _g = jax.random.normal(jax.random.fold_in(_rk, 9001), (2, 1), jnp.float32)
        _g = jnp.sign(_g) * jnp.maximum(jnp.abs(_g), 1.0) + (_g == 0) * 1.0
        g_xattn = _g[0]
        g_ffn = _g[1]
        return (x, ctx_4096, mask_1x1xSxS2_bk0, g_xattn, g_ffn)
    x, ctx_4096, mask_1x1xSxS2_bk0, g_xattn, g_ffn = _rec_inputs()

    def _L0_xattn_setup():
        import jax, jax.numpy as jnp
        import numpy as np
        B, T, D_MODEL = (1, 512, 1024)
        NUM_Q_HEADS, NUM_KV_HEADS, KEY_SIZE = (32, 8, 128)
        ATTN_MULT = 0.08838834764831845
        MAX_ATTN_VAL = 30.0

        def rotate_half(x):
            x1, x2 = jnp.split(x, 2, axis=-1)
            return jnp.concatenate((-x2, x1), axis=-1)

        def apply_rope(x):
            b, t, h, d = x.shape
            exponents = jnp.arange(0, d, 2, dtype=jnp.float32)
            inv_freq = 1.0 / 10000.0 ** (exponents / d)
            pos = jnp.arange(t, dtype=jnp.float32)
            phase = pos[:, None] * inv_freq[None, :]
            phase = jnp.tile(phase, (1, 2))[None, :, None, :]
            return (x * jnp.cos(phase) + rotate_half(x) * jnp.sin(phase)).astype(x.dtype)
        key = jax.random.key(seed)
        ks = jax.random.split(key, 8)
        query = jax.random.normal(ks[0], (B, T, D_MODEL), dtype=jnp.float32)
        kk = jax.random.normal(ks[1], (B, T, D_MODEL), dtype=jnp.float32)
        vv = jax.random.normal(ks[2], (B, T, D_MODEL), dtype=jnp.float32)
        mask = jnp.tril(jnp.ones((T, T), dtype=bool))[None, None, :, :]
        s = 0.02
        Wq = jax.random.normal(ks[3], (D_MODEL, NUM_Q_HEADS * KEY_SIZE), dtype=jnp.float32) * s
        Wk = jax.random.normal(ks[4], (D_MODEL, NUM_KV_HEADS * KEY_SIZE), dtype=jnp.float32) * s
        Wv = jax.random.normal(ks[5], (D_MODEL, NUM_KV_HEADS * KEY_SIZE), dtype=jnp.float32) * s
        Wo = jax.random.normal(ks[6], (NUM_Q_HEADS * KEY_SIZE, D_MODEL), dtype=jnp.float32) * s
        return {'query': query, 'key': kk, 'value': vv, 'mask': mask, 'Wq': Wq, 'Wk': Wk, 'Wv': Wv, 'Wo': Wo}
    _L0_xattn_all = _L0_xattn_setup()
    _L0_xattn_in = {k: v for k, v in _L0_xattn_all.items() if k in ('Wq', 'Wk', 'Wv', 'Wo')}
    del _L0_xattn_all

    def _L0_ffn_setup():
        import jax, jax.numpy as jnp
        import numpy as np
        MAX_THRESHOLD = 1.0 / 8.0
        SCALING = 32.0 / 16.0
        key = jax.random.key(seed)
        ks = jax.random.split(key, 8)
        B_, S, D, O, E, R = (4, 512, 1024, 1024, 8, 16)
        sd = 1.0 / np.sqrt(D)
        return {'x': jax.random.normal(ks[0], (B_, S, D), jnp.float32), 'W_base': jax.random.normal(ks[1], (O, D), jnp.float32) * sd, 'b_base': jax.random.normal(ks[2], (O,), jnp.float32) * 0.01, 'W_gate': jax.random.normal(ks[3], (E, D), jnp.float32) * sd, 'W_thr': jax.random.normal(ks[4], (1, D), jnp.float32) * sd, 'b_thr': jax.random.normal(ks[5], (1,), jnp.float32) * 0.01, 'A': jax.random.normal(ks[6], (E, R, D), jnp.float32) * sd, 'B': jax.random.normal(ks[7], (O,), jnp.float32)[None, :, None] * jnp.zeros((E, O, R), jnp.float32) + jax.random.normal(jax.random.fold_in(key, 7), (E, O, R), jnp.float32) * (1.0 / np.sqrt(R))}
    _L0_ffn_all = _L0_ffn_setup()
    _L0_ffn_in = {k: v for k, v in _L0_ffn_all.items() if k in ('W_base', 'b_base', 'W_gate', 'W_thr', 'b_thr', 'A', 'B')}
    del _L0_ffn_all
    return {'x': x, 'ctx_4096': ctx_4096, 'mask_1x1xSxS2_bk0': mask_1x1xSxS2_bk0, 'g_xattn': g_xattn, 'g_ffn': g_ffn, 'L0_xattn_Wq': _L0_xattn_in['Wq'], 'L0_xattn_Wk': _L0_xattn_in['Wk'], 'L0_xattn_Wv': _L0_xattn_in['Wv'], 'L0_xattn_Wo': _L0_xattn_in['Wo'], 'L0_ffn_W_base': _L0_ffn_in['W_base'], 'L0_ffn_b_base': _L0_ffn_in['b_base'], 'L0_ffn_W_gate': _L0_ffn_in['W_gate'], 'L0_ffn_W_thr': _L0_ffn_in['W_thr'], 'L0_ffn_b_thr': _L0_ffn_in['b_thr'], 'L0_ffn_A': _L0_ffn_in['A'], 'L0_ffn_B': _L0_ffn_in['B']}

def reference(x, ctx_4096, mask_1x1xSxS2_bk0, g_xattn, g_ffn, L0_xattn_Wq, L0_xattn_Wk, L0_xattn_Wv, L0_xattn_Wo, L0_ffn_W_base, L0_ffn_b_base, L0_ffn_W_gate, L0_ffn_W_thr, L0_ffn_b_thr, L0_ffn_A, L0_ffn_B):
    import jax
    import jax.numpy as jnp

    def _L0_xattn_ref(query, key, value, mask, Wq, Wk, Wv, Wo):
        import jax, jax.numpy as jnp
        import numpy as np
        B, T, D_MODEL = (1, 512, 1024)
        NUM_Q_HEADS, NUM_KV_HEADS, KEY_SIZE = (32, 8, 128)
        ATTN_MULT = 0.08838834764831845
        MAX_ATTN_VAL = 30.0

        def rotate_half(x):
            x1, x2 = jnp.split(x, 2, axis=-1)
            return jnp.concatenate((-x2, x1), axis=-1)

        def apply_rope(x):
            b, t, h, d = x.shape
            exponents = jnp.arange(0, d, 2, dtype=jnp.float32)
            inv_freq = 1.0 / 10000.0 ** (exponents / d)
            pos = jnp.arange(t, dtype=jnp.float32)
            phase = pos[:, None] * inv_freq[None, :]
            phase = jnp.tile(phase, (1, 2))[None, :, None, :]
            return (x * jnp.cos(phase) + rotate_half(x) * jnp.sin(phase)).astype(x.dtype)
        b, t, _ = query.shape
        d = KEY_SIZE
        h, kv_h = (NUM_Q_HEADS, NUM_KV_HEADS)
        g = h // kv_h
        q = (query @ Wq).reshape(b, t, h, d)
        k = (key @ Wk).reshape(b, t, kv_h, d)
        v = (value @ Wv).reshape(b, t, kv_h, d)
        q = apply_rope(q)
        k = apply_rope(k)
        q = q.reshape(b, t, kv_h, g, d)
        logits = jnp.einsum('btkgd,bTkd->bkgtT', q, k).astype(jnp.float32)
        logits = logits * ATTN_MULT
        logits = MAX_ATTN_VAL * jnp.tanh(logits / MAX_ATTN_VAL)
        m = mask[:, :, None, :, :]
        logits = jnp.where(m, logits, -1e+30)
        weights = jax.nn.softmax(logits, axis=-1).astype(query.dtype)
        attn = jnp.einsum('bkgtT,bTkd->btkgd', weights, v)
        attn = attn.reshape(b, t, h * d)
        return attn @ Wo

    def _L0_ffn_ref(x, W_base, b_base, W_gate, W_thr, b_thr, A, B):
        import jax, jax.numpy as jnp
        import numpy as np
        MAX_THRESHOLD = 1.0 / 8.0
        SCALING = 32.0 / 16.0
        base = jnp.einsum('bsd,od->bso', x, W_base) + b_base
        D = x.shape[-1]
        xf = x.reshape(-1, D)
        gate_logits = jax.nn.softmax(xf @ W_gate.T, axis=-1)
        thresholds = jax.nn.sigmoid(xf @ W_thr.T + b_thr) * MAX_THRESHOLD
        adapted = gate_logits - thresholds
        selected = (adapted >= 0).astype(x.dtype)
        weights = adapted * selected
        wsum = jnp.sum(weights, axis=-1, keepdims=True)
        wsum = jnp.where(wsum == 0, jnp.ones_like(wsum), wsum)
        weights = weights / wsum
        h = jnp.einsum('nd,erd->ner', xf, A)
        moe = jnp.einsum('ner,ne,eor->no', h, weights, B) * SCALING
        out = base + moe.reshape(base.shape)
        return out
    x = x + jnp.tanh(g_xattn[0]) * _L0_xattn_ref(_layernorm(x, axis=-1), ctx_4096, ctx_4096, mask_1x1xSxS2_bk0, L0_xattn_Wq, L0_xattn_Wk, L0_xattn_Wv, L0_xattn_Wo)
    x = x + jnp.tanh(g_ffn[0]) * _L0_ffn_ref(_layernorm(x, axis=-1), L0_ffn_W_base, L0_ffn_b_base, L0_ffn_W_gate, L0_ffn_W_thr, L0_ffn_b_thr, L0_ffn_A, L0_ffn_B)
    return x

_drawn_inputs = setup_inputs


def setup_inputs(seed=0):
    import zlib

    import numpy as np

    out = dict(_drawn_inputs(seed))
    spreads = {}
    factors = {'L0_ffn_b_base': 8.0}
    for name, (base, spread) in spreads.items():
        noise = np.random.default_rng([zlib.crc32(name.encode()), seed]).standard_normal(out[name].shape)
        drawn = base * np.exp(spread * noise) if base else spread * noise
        out[name] = jnp.asarray(drawn.astype(out[name].dtype))
    for name, factor in factors.items():
        out[name] = (out[name] * factor).astype(out[name].dtype)
    return out
```

```python
import concourse.bass as bass
from concourse import mybir
from contextlib import ExitStack

F32 = mybir.dt.float32
F32R = mybir.dt.float32r
F16 = mybir.dt.float16
U8 = mybir.dt.uint8
ALU = mybir.AluOpType
ACT = mybir.ActivationFunctionType
AX = mybir.AxisListType.X

P = 128
NB, S, D = 8, 256, 1024
HQ, HK, DH = 32, 8, 128
GQ = HQ // HK
ROWS = NB * S
PAIR = 2 * S
NP = ROWS // PAIR
TP = PAIR // P
DC = D // P
E, R = 8, 16
NG = E + 1
HGW = E * R + NG
NT = ROWS // P
EPS = 1e-5
ATTN_MULT = 0.08838834764831845
MAX_ATTN = 30.0

WS = 64.0
QS = 4.0
VS = 4.0
PS = 1024.0
OS = 4.0
HS = 16.0
BS = 8.0

PAIRS_PER_HALF = 2
NIT = 2 * HK
SPI = PAIRS_PER_HALF * GQ
NSTEP = NIT * SPI
LAG = GQ


def at_least(eng, sem, value):
    if isinstance(value, int) and value <= 0:
        return
    eng.wait_ge(sem, value)


def build(nc, x, ctx, mask, g_xattn, g_ffn, wq, wk, wv, wo, w_base, b_base, w_gate, w_thr, b_thr, a_dn, b_up,
          tables, out):
    x_rows = x.rearrange("b s d -> (b s) d")
    ctx_rows = ctx.rearrange("b s d -> (b s) d")
    out_rows = out.rearrange("b s d -> (b s) d")
    mask_rows = mask.rearrange("a b t s -> (a b t) s").rearrange("(k p) s -> p k s", p=P)

    k_scr = nc.dram_tensor("k_scr", (HK, NP, P, 2 * PAIR), F16, kind="Internal").ap()
    v_scr = nc.dram_tensor("v_scr", (HK, NP, P, TP * 2 * DH), F16, kind="Internal").ap()
    xn_scr = nc.dram_tensor("xn_scr", (NP, P, 2 * DC * PAIR), F16, kind="Internal").ap()
    x1_scr = nc.dram_tensor("x1_scr", (ROWS, D), F32, kind="Internal").ap()

    with ExitStack() as whole:
        def sem(name):
            return whole.enter_context(nc.semaphore(name))

        def sb(stack, name, shape, dt):
            return stack.enter_context(nc.sbuf_tensor(name, shape, dt))

        bank = [whole.enter_context(nc.psum_tensor(f"bank{i}", [P, 512], F32)) for i in range(8)]

        tab = sb(whole, "tab", [P, 2 * S + P], F32)
        cos_k, sin_k, ident = tab[:, 0:S], tab[:, S:2 * S], tab[:, 2 * S:2 * S + P]
        cos_q = sb(whole, "cos_q", [P, S], F32)
        sin_q = sb(whole, "sin_q", [P, S], F32)
        mask_t = sb(whole, "mask_t", [P, 2 * S], F32)
        gates = sb(whole, "gates", [P, 8], F32)
        ones_r = sb(whole, "ones_r", [P, P], F32R)
        mhalf = sb(whole, "mhalf", [P, 1], F32)

        ph1 = ExitStack()
        wk_hi = sb(ph1, "wk_hi", [P, DC, D], F16)
        wk_lo = sb(ph1, "wk_lo", [P, DC, D], F16)
        wv_hi = sb(ph1, "wv_hi", [P, DC, D], F16)
        wv_lo = sb(ph1, "wv_lo", [P, DC, D], F16)
        NST1 = 4
        wst1 = sb(ph1, "wst1", [P, NST1, D], F32)
        ctx_raw = sb(ph1, "ctx_raw", [P, TP, D], F32)
        x_raw = sb(ph1, "x_raw", [P, TP, D], F32)
        ct_hi = sb(ph1, "ct_hi", [P, DC, PAIR], F16)
        ct_lo = sb(ph1, "ct_lo", [P, DC, PAIR], F16)
        xst = sb(ph1, "xst", [P, 2, DC, PAIR], F16)
        kst = sb(ph1, "kst", [P, 2, 2, PAIR], F16)
        vst = sb(ph1, "vst", [P, HK, TP, 2, DH], F16)
        ka = sb(ph1, "ka", [P, PAIR], F32)
        kb = sb(ph1, "kb", [P, PAIR], F32)
        stats = sb(ph1, "stats", [P, TP, 12], F32)
        mv = sb(ph1, "mv", [P, TP, 16], F32)
        mask_u8 = sb(ph1, "mask_u8", [P, 2, S], U8)
        mask_f = sb(ph1, "mask_f", [P, 2, S], F32)
        row_any = sb(ph1, "row_any", [P, 2, 2], F32)
        row_wide = sb(ph1, "row_wide", [P, 2, P], F32)
        ones_w = sb(ph1, "ones_w", [P, P], F32)
        ph1.close()

        ph2 = ExitStack()
        HALF = PAIRS_PER_HALF * PAIR
        xn = sb(ph2, "xn", [P, PAIRS_PER_HALF, 2, DC, PAIR], F16)
        y = sb(ph2, "y", [P, PAIRS_PER_HALF, TP, D], F32)
        wq_s = sb(ph2, "wq_s", [P, 2, 2, DC, GQ * DH], F16)
        wo_s = sb(ph2, "wo_s", [P, 2, 2, GQ, D], F16)
        wst2 = sb(ph2, "wst2", [P, 2, D], F32)
        kt = sb(ph2, "kt", [P, PAIRS_PER_HALF, 2, PAIR], F16)
        vt = sb(ph2, "vt", [P, PAIRS_PER_HALF, TP, 2, DH], F16)
        q_s = sb(ph2, "q_s", [P, 2, PAIR], F16)
        qa = sb(ph2, "qa", [P, PAIR], F32)
        qb = sb(ph2, "qb", [P, PAIR], F32)
        e_t = sb(ph2, "e_t", [P, 2, 2, S], F32)
        w_s = sb(ph2, "w_s", [P, 2, 2, 2, S], F16)
        esum = sb(ph2, "esum", [P, PAIR], F32)
        esum_r = sb(ph2, "esum_r", [P, 2, PAIR], F32R)
        den_t = sb(ph2, "den_t", [P, PAIR], F32)
        rden_t = sb(ph2, "rden_t", [P, PAIR // 32], F32)
        rden = sb(ph2, "rden", [P, PAIR], F32)
        o_s = sb(ph2, "o_s", [P, PAIRS_PER_HALF, GQ, 2, PAIR], F16)
        ph2.close()

        ph3 = ExitStack()
        wb_raw = sb(ph3, "wb_raw", [P, DC, D], F32)
        a_raw = sb(ph3, "a_raw", [P, D], F32)
        gt_raw = sb(ph3, "gt_raw", [P, D], F32)
        b_raw = sb(ph3, "b_raw", [P, DC, E, R], F32)
        wb_hi = sb(ph3, "wb_hi", [P, DC, D], F16)
        wb_lo = sb(ph3, "wb_lo", [P, DC, D], F16)
        ag_hi = sb(ph3, "ag_hi", [P, DC, HGW + 1], F16)
        ag_lo = sb(ph3, "ag_lo", [P, DC, HGW + 1], F16)
        bt_hi = sb(ph3, "bt_hi", [P, D], F16)
        bt_lo = sb(ph3, "bt_lo", [P, D], F16)
        bias_row = sb(ph3, "bias_row", [P, D], F32)
        thr_bias = sb(ph3, "thr_bias", [P, 2], F32)
        NX = 4
        x1t = sb(ph3, "x1t", [P, NX, D], F32)
        xn2 = sb(ph3, "xn2", [P, 2, D], F32)
        xt_hi = sb(ph3, "xt_hi", [P, 2, DC, P], F16)
        xt_lo = sb(ph3, "xt_lo", [P, 2, DC, P], F16)
        out_t = sb(ph3, "out_t", [P, 2, D], F32)
        stats3 = sb(ph3, "stats3", [P, 12], F32)
        mv3 = sb(ph3, "mv3", [P, 16], F32)
        gsm = sb(ph3, "gsm", [P, 2, 64], F32)
        hw = sb(ph3, "hw", [P, E * R], F32)
        hwt = sb(ph3, "hwt", [P, 2, P], F16)
        ph3.close()

        tab_in = sem("tab_in")
        mask_in = sem("mask_in")
        g_in = sem("g_in")
        setup_dve = sem("setup_dve")
        ones_set = sem("ones_set")
        mask_tr = sem("mask_tr")
        tanh_g = sem("tanh_g")
        ctx_in = [sem(f"ctx_in{t}") for t in range(TP)]
        x_in = [sem(f"x_in{t}") for t in range(TP)]
        wst1_in = [sem(f"wst1_in{t}") for t in range(NST1)]
        wk_hi_set = sem("wk_hi_set")
        wk_lo_set = sem("wk_lo_set")
        wv_scaled = sem("wv_scaled")
        wv_hi_set = sem("wv_hi_set")
        wv_lo_set = sem("wv_lo_set")
        tr_done = sem("tr_done")
        tr_hi = sem("tr_hi")
        tr_lo = sem("tr_lo")
        k_done = sem("k_done")
        v_done = sem("v_done")
        kr_a = sem("kr_a")
        kr_read = sem("kr_read")
        k_roped = sem("k_roped")
        k_hi = sem("k_hi")
        k_lo = sem("k_lo")
        v_hi = sem("v_hi")
        v_lo = sem("v_lo")
        ln1_stat = sem("ln1_stat")
        ln1_rstd = sem("ln1_rstd")
        ln1 = sem("ln1")
        mhalf_set = sem("mhalf_set")
        k_out = [sem("k_out0"), sem("k_out1")]
        v_out = sem("v_out")
        xn_out = sem("xn_out")

        wst2_in = [sem("wst2_in0"), sem("wst2_in1")]
        w_hi = sem("w_hi")
        w_lo = sem("w_lo")
        kv_in = [sem("kv_in0"), sem("kv_in1")]
        xn_in = [sem("xn_in0"), sem("xn_in1")]
        y_in = [sem("y_in0"), sem("y_in1")]
        y_out = [sem("y_out0"), sem("y_out1")]
        q_done = sem("q_done")
        q_a = sem("q_a")
        q_read = sem("q_read")
        q_roped = sem("q_roped")
        q_hi = sem("q_hi")
        q_lo = sem("q_lo")
        logits_done = sem("logits_done")
        tanh_done = sem("tanh_done")
        exp_done = sem("exp_done")
        masked = sem("masked")
        esum_done = sem("esum_done")
        esum_hi = sem("esum_hi")
        esum_lo = sem("esum_lo")
        den_done = sem("den_done")
        den_read = sem("den_read")
        rden_t_done = sem("rden_t_done")
        rden_done = sem("rden_done")
        weighted = sem("weighted")
        p_hi = sem("p_hi")
        p_lo = sem("p_lo")
        av_done = sem("av_done")
        o_hi = sem("o_hi")
        o_lo = sem("o_lo")
        y_done = [sem("y_done0"), sem("y_done1")]
        y_added = [sem("y_added0"), sem("y_added1")]

        w3_in = sem("w3_in")
        g3_in = sem("g3_in")
        b3_in = sem("b3_in")
        x1_in = [sem(f"x1_in{t}") for t in range(NX)]
        tr3_done = sem("tr3_done")
        tr3_hi = sem("tr3_hi")
        tr3_lo = sem("tr3_lo")
        bias_set = sem("bias_set")
        ln3_stat = sem("ln3_stat")
        ln3_rstd = sem("ln3_rstd")
        ln3 = sem("ln3")
        x1_biased = sem("x1_biased")
        hg_done = sem("hg_done")
        gmax = sem("gmax")
        gexp = sem("gexp")
        gate_step = sem("gate_step")
        wsum_step = sem("wsum_step")
        hw_set = sem("hw_set")
        hwt_done = sem("hwt_done")
        hwt_hi = sem("hwt_hi")
        hwt_lo = sem("hwt_lo")
        ffn_done = sem("ffn_done")
        out_set = sem("out_set")
        out_out = [sem("out_out0"), sem("out_out1")]

        NTR1 = DC + 2 * DC * NP

        def wait_phase1(eng):
            eng.wait_ge(k_lo, HK * NP)
            eng.wait_ge(v_lo, 2 * TP * NP)
            eng.wait_ge(tr_lo, NTR1 - DC)
            eng.wait_ge(k_out[0], 16 * HK * NP // 2)
            eng.wait_ge(k_out[1], 16 * HK * NP // 2)
            eng.wait_ge(v_out, 16 * NP)
            eng.wait_ge(xn_out, 16 * NP)
            eng.wait_ge(tanh_g, 3)

        def wait_phase2(eng):
            eng.wait_ge(y_added[0], NSTEP)
            eng.wait_ge(y_added[1], NSTEP)
            eng.wait_ge(y_out[0], 32)
            eng.wait_ge(y_out[1], 32)

        NTR3W = 2 * DC + DC + 2

        def weight_banks():
            n = 0
            for c in range(DC):
                for f in range(2):
                    yield (n, wb_hi[:, c, f * 512:(f + 1) * 512], wb_lo[:, c, f * 512:(f + 1) * 512],
                           bank[4 + n % 2][:, :], WS)
                    n += 1
            for c in range(DC):
                yield n, ag_hi[:, c, 0:HGW], ag_lo[:, c, 0:HGW], bank[4 + n % 2][:, 0:HGW], WS
                n += 1
            for f in range(2):
                yield (n, bt_hi[:, f * 512:(f + 1) * 512], bt_lo[:, f * 512:(f + 1) * 512],
                       bank[4 + n % 2][:, :], BS)
                n += 1

        block = whole.enter_context(nc.Block())

        @block.sync
        def _(sp):
            sp.dma_start(tab[:, :], tables).then_inc(tab_in, 16)
            for t in range(TP):
                sp.dma_start(ctx_raw[:, t, :], ctx_rows[t * P:(t + 1) * P, :]).then_inc(ctx_in[t], 16)
            sp.dma_start(mask_u8[:, :, :], mask_rows).then_inc(mask_in, 16)
            sp.dma_start(gates[:, 0:1], g_xattn.partition_broadcast(P)).then_inc(g_in, 16)
            sp.dma_start(gates[:, 1:2], g_ffn.partition_broadcast(P)).then_inc(g_in, 16)

            def load_w(n, src, c):
                if n >= NST1:
                    if n - NST1 < DC:
                        sp.wait_ge(wk_lo_set, n - NST1 + 1)
                    else:
                        sp.wait_ge(wv_lo_set, n - NST1 - DC + 1)
                sp.dma_start(wst1[:, n % NST1, :], src[c * P:(c + 1) * P, :]).then_inc(wst1_in[n % NST1], 16)

            for c in range(DC):
                load_w(c, wk, c)
            for t in range(TP):
                sp.dma_start(x_raw[:, t, :], x_rows[t * P:(t + 1) * P, :]).then_inc(x_in[t], 16)
            for t in range(TP):
                sp.wait_ge(tr_done, 2 * (t + 1))
                sp.dma_start(ctx_raw[:, t, :], ctx_rows[PAIR + t * P:PAIR + (t + 1) * P, :]).then_inc(ctx_in[t], 16)
            for c in range(DC):
                load_w(DC + c, wv, c)

            def pair_io(q, more_x, more_ctx):
                for g in range(HK):
                    sp.wait_ge(k_hi, q * HK + g + 1)
                    sp.wait_ge(k_lo, q * HK + g + 1)
                    sp.dma_start(k_scr[g, q, :, :], kst[:, g % 2, :, :].rearrange("p a t -> p (a t)")
                                 ).then_inc(k_out[g % 2], 16)
                sp.wait_ge(tr_lo, DC + 16 * q + DC)
                sp.dma_start(xn_scr[q, :, :], xst[:, :, :, :].rearrange("p a c t -> p (a c t)")).then_inc(xn_out, 16)
                if more_x:
                    for t in range(TP):
                        sp.wait_ge(tr_done, DC + 16 * q + DC)
                        sp.dma_start(x_raw[:, t, :], x_rows[bass.ds(q * PAIR + PAIR + t * P, P), :]
                                     ).then_inc(x_in[t], 16)
                if more_ctx:
                    for t in range(TP):
                        sp.wait_ge(tr_done, DC + 16 * q + DC + 2 * (t + 1))
                        sp.dma_start(ctx_raw[:, t, :], ctx_rows[bass.ds(q * PAIR + 2 * PAIR + t * P, P), :]
                                     ).then_inc(ctx_in[t], 16)
                sp.wait_ge(v_lo, (q + 1) * 2 * TP)
                sp.dma_start(v_scr[:, q, :, :].rearrange("g p n -> p g n"),
                             vst[:, :, :, :, :].rearrange("p g t a d -> p g (t a d)")).then_inc(v_out, 16)

            with sp.Fori(0, NP - 2) as q:
                pair_io(q, True, True)
            pair_io(NP - 2, True, False)
            pair_io(NP - 1, False, False)

            wait_phase1(sp)

            def load_piece(n_first, n, g):
                j = n_first
                at_least(sp, w_lo, n - 1)
                if j < 4:
                    src = wq[2 * j * P:(2 * j + 2) * P, bass.ds(g * GQ * DH, GQ * DH)].rearrange(
                        "(c p) n -> p c n", p=P)
                    dst = wst2[:, j % 2, :].rearrange("p (c n) -> p c n", c=2)
                else:
                    src = wo[bass.ds(g * GQ * DH + (j - 4) * DH, P), :]
                    dst = wst2[:, j % 2, :]
                sp.dma_start(dst, src).then_inc(wst2_in[j % 2], 16)

            def load_kv(b, g, half):
                q = half * PAIRS_PER_HALF + b
                sp.dma_start(kt[:, b, :, :].rearrange("p a t -> p (a t)"), k_scr[g, q, :, :]).then_inc(kv_in[b], 16)
                sp.dma_start(vt[:, b, :, :, :].rearrange("p t a d -> p (t a d)"), v_scr[g, q, :, :]
                             ).then_inc(kv_in[b], 16)

            def load_xn(b, half):
                sp.dma_start(xn[:, b, :, :, :].rearrange("p a c t -> p (a c t)"),
                             xn_scr[half * PAIRS_PER_HALF + b, :, :]).then_inc(xn_in[b], 16)

            def y_rows(dram, b, half):
                r0 = (half * PAIRS_PER_HALF + b) * PAIR
                return dram[r0:r0 + PAIR, :].rearrange("(t p) d -> p t d", p=P)

            def load_y(b, half):
                sp.dma_start(y[:, b, :, :], y_rows(x_rows, b, half)).then_inc(y_in[b], 16)

            def store_y(b, half):
                sp.dma_start(y_rows(x1_scr, b, half), y[:, b, :, :]).then_inc(y_out[b], 16)

            load_piece(0, 0, 0)
            load_piece(1, 1, 0)
            load_xn(0, 0)
            for j in range(2, 8):
                load_piece(j, j, 0)
            load_kv(0, 0, 0)
            load_kv(1, 0, 0)
            load_xn(1, 0)
            load_y(0, 0)
            load_y(1, 0)

            def loads(it, half, g, turn=False, last=False):
                for u in range(SPI):
                    if not last:
                        load_piece(u, 8 * it + 8 + u, (g + 1) if not turn else 0)
                    if u == 1 and not (isinstance(it, int) and it == 0):
                        sp.wait_ge(av_done, 8 * it)
                        load_kv(1, g, half)
                    if u == 5 and not last:
                        sp.wait_ge(av_done, 8 * it + 4)
                        if turn:
                            load_kv(0, 0, 1)
                        else:
                            load_kv(0, g + 1, half)
                    if turn and u == 5:
                        sp.wait_ge(q_done, 8 * it + 4)
                        load_xn(0, 1)
                    if isinstance(it, int) and it == HK:
                        if u == 1:
                            sp.wait_ge(q_done, 8 * it)
                            load_xn(1, 1)
                            for k in range(2):
                                sp.wait_ge(y_added[k], 8 * it - LAG)
                            store_y(0, 0)
                        if u == 2:
                            sp.wait_ge(y_out[0], 16)
                            load_y(0, 1)
                        if u == 5:
                            for k in range(2):
                                sp.wait_ge(y_added[k], 8 * it)
                            store_y(1, 0)
                        if u == 6:
                            sp.wait_ge(y_out[1], 16)
                            load_y(1, 1)

            loads(0, 0, 0)
            with sp.Fori(1, HK - 1) as it:
                loads(it, 0, it)
            loads(HK - 1, 0, HK - 1, turn=True)
            loads(HK, 1, 0)
            with sp.Fori(HK + 1, NIT - 1) as it:
                loads(it, 1, it - HK)
            loads(NIT - 1, 1, HK - 1, last=True)
            for k in range(2):
                sp.wait_ge(y_added[k], NSTEP - LAG)
            store_y(0, 1)
            for k in range(2):
                sp.wait_ge(y_added[k], NSTEP)
            store_y(1, 1)

            wait_phase2(sp)
            for o in range(DC):
                sp.dma_start(wb_raw[:, o, :], w_base[o * P:(o + 1) * P, :]).then_inc(w3_in, 16)

            def load_x1(i, slot):
                sp.dma_start(x1t[:, slot, :], x1_scr[bass.ds(i * P, P), :]).then_inc(x1_in[slot], 16)

            for i in range(NX):
                load_x1(i, i)
            sp.dma_start(a_raw[:, :], a_dn.rearrange("e r d -> (e r) d")).then_inc(g3_in, 16)
            sp.dma_start(gt_raw[0:E, :], w_gate).then_inc(g3_in, 16)
            sp.dma_start(gt_raw[E:NG, :], w_thr).then_inc(g3_in, 16)
            sp.dma_start(bias_row[:, :], b_base.partition_broadcast(P)).then_inc(b3_in, 16)
            sp.dma_start(thr_bias[:, 0:1], b_thr.partition_broadcast(P)).then_inc(b3_in, 16)
            b_by_o = b_up.rearrange("e (k p) r -> k p e r", p=P)
            for o in range(DC):
                sp.dma_start(b_raw[:, o, :, :], b_by_o[o, :, :, :]).then_inc(g3_in, 16)

            def rows_io(i, u, more):
                if more:
                    sp.wait_ge(out_set, 2 * i + 2)
                    load_x1(i + NX, u)
                sp.wait_ge(out_set, 2 * i + 2)
                sp.dma_start(out_rows[bass.ds(i * P, P), :], out_t[:, u % 2, :]).then_inc(out_out[u % 2], 16)

            with sp.Fori(0, NT // NX - 1) as j:
                for u in range(NX):
                    rows_io(j * NX + u, u, True)
            for u in range(NX):
                rows_io(NT - NX + u, u, False)
            for k in range(2):
                sp.wait_ge(out_out[k], 16 * NT // 2)

        @block.gpsimd
        def _(pool):
            nc.gpsimd.memset(mhalf[:, :], -0.5).then_inc(mhalf_set, 1)
            pool.wait_ge(mhalf_set, 1)

            def inverse_std(stat, rstd, n, m):
                pool.wait_ge(stat, 8 * n + 8)
                nc.gpsimd.tensor_tensor(m[:, 3:4], m[:, 2:3], mhalf[:, :], ALU.pow).then_inc(rstd, 1)

            for t in range(TP):
                inverse_std(ln1_stat, ln1_rstd, t, mv[:, t, :])

            for c in range(DC):
                n = DC + c
                w = wst1[:, n % NST1, :]
                pool.wait_ge(wst1_in[n % NST1], 16 * (n // NST1 + 1))
                nc.gpsimd.tensor_scalar(w, w, WS, 1.0, ALU.mult, ALU.mult).then_inc(wv_scaled, 1)
                pool.wait_ge(wv_scaled, c + 1)
                nc.gpsimd.tensor_copy(wv_hi[:, c, :], w).then_inc(wv_hi_set, 1)
                pool.wait_ge(wv_hi_set, c + 1)
                nc.gpsimd.tensor_tensor(wv_lo[:, c, :], w, wv_hi[:, c, :], ALU.subtract).then_inc(wv_lo_set, 1)

            with pool.Fori(1, NP) as q:
                for t in range(TP):
                    inverse_std(ln1_stat, ln1_rstd, TP * q + t, mv[:, t, :])

            wait_phase1(pool)

            def step(s):
                for b in range(2):
                    pool.wait_ge(exp_done, 2 * s + b + 1)
                    e_b = e_t[:, b, :, :].rearrange("p k t -> p (k t)")
                    nc.gpsimd.tensor_tensor(e_b, e_b, mask_t[:, :], ALU.mult).then_inc(masked, 1)
                    pool.wait_ge(masked, 2 * s + b + 1)
                    at_least(pool, esum_lo, s)
                    nc.gpsimd.tensor_tensor(esum[:, b * S:(b + 1) * S], e_t[:, b, 0, :], e_t[:, b, 1, :],
                                            ALU.add).then_inc(esum_done, 1)
                pool.wait_ge(esum_hi, s + 1)
                at_least(pool, den_done, s)
                nc.gpsimd.tensor_tensor(esum_r[:, 1, :], esum[:, :], esum_r[:, 0, :].bitcast(F32), ALU.subtract
                                        ).then_inc(esum_lo, 1)

            step(0)
            with pool.Fori(1, NSTEP) as s:
                step(s)

            wait_phase2(pool)
            for i in range(2):
                inverse_std(ln3_stat, ln3_rstd, i, mv3[:, :])
            pool.wait_ge(b3_in, 32)
            pool.wait_ge(bias_set, 2)

            def biased(i, u):
                pool.wait_ge(ln3, i + 1)
                nc.gpsimd.tensor_tensor(x1t[:, u, :], x1t[:, u, :], bias_row[:, :], ALU.add).then_inc(x1_biased, 1)

            with pool.Fori(0, NT // NX - 1) as j:
                for u in range(NX):
                    biased(j * NX + u, u)
                    inverse_std(ln3_stat, ln3_rstd, j * NX + u + 2, mv3[:, :])
            for u in range(NX):
                biased(NT - NX + u, u)
                if u < NX - 2:
                    inverse_std(ln3_stat, ln3_rstd, NT - NX + u + 2, mv3[:, :])

        @block.scalar
        def _(act):
            act.wait_ge(g_in, 32)
            nc.scalar.activation(gates[:, 2:4], gates[:, 0:2], ACT.Tanh).then_inc(tanh_g, 1)

            def bank_hi(n, par, dst):
                act.wait_ge(tr_done, n + 1)
                src = bank[par][:, :]
                if len(dst.shape) == 3:
                    src = src.rearrange("p (a b) -> p a b", a=dst.shape[1])
                nc.scalar.activation(dst, src, ACT.Copy).then_inc(tr_hi, 1)

            for m in range(DC):
                t, f = divmod(m, 2)
                bank_hi(m, m % 2, ct_hi[:, 4 * f:4 * f + 4, t * P:(t + 1) * P])
            for c in range(DC):
                act.wait_ge(wst1_in[c % NST1], 16 * (c // NST1 + 1))
                nc.scalar.activation(wk_hi[:, c, :], wst1[:, c % NST1, :], ACT.Copy, scale=WS).then_inc(wk_hi_set, 1)

            def pair(q, more):
                for g in range(HK):
                    at_least(act, xn_out, 16 * q)
                    bank_hi(DC + 16 * q + g, g % 2, xst[:, 0, g, :])
                    act.wait_ge(k_roped, HK * q + g + 1)
                    at_least(act, k_out[g % 2], 16 * (4 * q + g // 2))
                    nc.scalar.activation(kst[:, g % 2, 0, :], ka[:, :], ACT.Copy).then_inc(k_hi, 1)
                for v in range(2 * TP):
                    t, f = divmod(v, 2)
                    if more and t >= 1:
                        act.wait_ge(v_done, 2 * TP * q + 2 * t)
                        bank_hi(DC + 16 * q + DC + v - 2, v % 2, ct_hi[:, 4 * f:4 * f + 4, (t - 1) * P:t * P])
                    act.wait_ge(v_done, 2 * TP * q + v + 1)
                    at_least(act, v_out, 16 * q)
                    nc.scalar.activation(vst[:, 4 * f:4 * f + 4, t, 0, :],
                                         bank[4 + v % 2][:, :].rearrange("p (g d) -> p g d", g=4),
                                         ACT.Copy, scale=VS / WS).then_inc(v_hi, 1)
                if more:
                    for f in range(2):
                        act.wait_ge(v_done, 2 * TP * (q + 1))
                        bank_hi(DC + 16 * q + DC + 6 + f, f, ct_hi[:, 4 * f:4 * f + 4, 3 * P:4 * P])

            pair(0, True)
            with act.Fori(1, NP - 1) as q:
                pair(q, True)
            pair(NP - 1, False)

            wait_phase1(act)

            def split_piece(n, j, par, it):
                act.wait_ge(wst2_in[j % 2], 16 * (n // 2 + 1))
                if j < 4:
                    at_least(act, q_done, 8 * it if not isinstance(it, int) or it > 0 else 0)
                    dst = wq_s[:, par, 0, 2 * j:2 * j + 2, :].rearrange("p c n -> p (c n)")
                else:
                    at_least(act, y_done[1], 8 * it if not isinstance(it, int) or it > 0 else 0)
                    dst = wo_s[:, par, 0, j - 4, :]
                nc.scalar.activation(dst, wst2[:, j % 2, :], ACT.Copy, scale=WS).then_inc(w_hi, 1)

            def q_high(n):
                act.wait_ge(q_roped, n + 1)
                at_least(act, logits_done, 2 * n)
                nc.scalar.activation(q_s[:, 0, :], qa[:, :], ACT.Copy).then_inc(q_hi, 1)

            def o_high(p, pb, ph):
                act.wait_ge(av_done, p + 1)
                at_least(act, y_done[1], p + 1 - LAG)
                nc.scalar.activation(o_s[:, pb, ph, 0, :], bank[5][:, :], ACT.Copy, scale=OS / (PS * VS)
                                     ).then_inc(o_hi, 1)

            for j in range(8):
                split_piece(j, j, 0, 0)
            q_high(0)

            def steps(it, par, first=False, last=False):
                for u in range(SPI):
                    s = SPI * it + u
                    for b in range(2):
                        act.wait_ge(logits_done, 2 * s + b + 1)
                        at_least(act, p_lo, 2 * s - 1 + b if not (first and u == 0) else 0)
                        e_b = e_t[:, b, :, :].rearrange("p k t -> p (k t)")
                        nc.scalar.activation(e_b, bank[b][:, :], ACT.Tanh,
                                             scale=ATTN_MULT / (MAX_ATTN * QS * QS)).then_inc(tanh_done, 1)
                    for b in range(2):
                        act.wait_ge(tanh_done, 2 * s + b + 1)
                        e_b = e_t[:, b, :, :].rearrange("p k t -> p (k t)")
                        nc.scalar.activation(e_b, e_b, ACT.Exp, scale=MAX_ATTN).then_inc(exp_done, 1)
                    if not last:
                        split_piece(8 * it + 8 + u, u, 1 - par, it)
                    if not (first and u == 0):
                        o_high(s - 1, ((u - 1) % SPI) // GQ, (u - 1) % GQ)
                    act.wait_ge(esum_done, 2 * s + 2)
                    at_least(act, den_done, s)
                    nc.scalar.activation(esum_r[:, 0, :], esum[:, :], ACT.Copy).then_inc(esum_hi, 1)
                    if not (last and u == SPI - 1):
                        q_high(s + 1)
                    for b in range(2):
                        act.wait_ge(weighted, 2 * s + b + 1)
                        at_least(act, av_done, s)
                        nc.scalar.activation(w_s[:, 0, b, :, :], e_t[:, b, :, :], ACT.Copy).then_inc(p_hi, 1)

            steps(0, 0, first=True)
            with act.Fori(0, NIT // 2 - 1) as j:
                steps(2 * j + 1, 1)
                steps(2 * j + 2, 0)
            steps(NIT - 1, 1, last=True)
            o_high(NSTEP - 1, PAIRS_PER_HALF - 1, GQ - 1)

            wait_phase2(act)

            def bank3_hi(n, dst, src, scale=1.0):
                act.wait_ge(tr3_done, n + 1)
                nc.scalar.activation(dst, src, ACT.Copy, scale=scale).then_inc(tr3_hi, 1)

            for n, dst, _, src, scale in weight_banks():
                bank3_hi(n, dst, src, scale)

            def xt_high(i, par):
                for f in range(2):
                    at_least(act, hg_done, i - 1)
                    at_least(act, ffn_done, 2 * i - 2)
                    bank3_hi(NTR3W + 2 * i + f, xt_hi[:, par, 4 * f:4 * f + 4, :],
                             bank[4 + f][:, :].rearrange("p (c t) -> p c t", c=4))

            xt_high(0, 0)

            def tile(i, par, more):
                if more:
                    xt_high(i + 1, 1 - par)
                act.wait_ge(gmax, i + 1)
                nc.scalar.activation(gsm[:, par, 0:E], bank[6][:, E * R:E * R + E], ACT.Exp,
                                     bias=gsm[:, par, 9:10], scale=1.0 / WS).then_inc(gexp, 1)
                nc.scalar.activation(gsm[:, par, 10:11], bank[6][:, E * R + E:HGW], ACT.Tanh,
                                     bias=thr_bias[:, 1:2], scale=0.5 / WS).then_inc(gexp, 1)
                act.wait_ge(hwt_done, i + 1)
                at_least(act, ffn_done, 2 * i)
                nc.scalar.activation(hwt[:, 0, :], bank[7][:, 0:P], ACT.Copy).then_inc(hwt_hi, 1)

            tile(0, 0, True)
            tile(1, 1, True)
            with act.Fori(1, NT // 2 - 1) as j:
                tile(2 * j, 0, True)
                tile(2 * j + 1, 1, True)
            tile(NT - 2, 0, True)
            tile(NT - 1, 1, False)

        @block.vector
        def _(dve):
            setup = [0]

            def link(ins):
                setup[0] += 1
                ins.then_inc(setup_dve, 1)
                dve.wait_ge(setup_dve, setup[0])

            link(nc.vector.memset(ones_w[:, :], 1.0))
            nc.vector.tensor_scalar(ones_r[:, :], ones_w[:, :], 1.0 / PS, None, ALU.mult).then_inc(ones_set, 1)

            def bank_lo(n, par, dst, hi):
                dve.wait_ge(tr_hi, n + 1)
                src = bank[par][:, :]
                if len(dst.shape) == 3:
                    src = src.rearrange("p (a b) -> p a b", a=dst.shape[1])
                nc.vector.tensor_tensor(dst, src, hi, ALU.subtract).then_inc(tr_lo, 1)

            for m in range(DC):
                t, f = divmod(m, 2)
                cols = (slice(None), slice(4 * f, 4 * f + 4), slice(t * P, (t + 1) * P))
                bank_lo(m, m % 2, ct_lo[cols], ct_hi[cols])

            dve.wait_ge(mask_in, 16)
            link(nc.vector.tensor_copy(mask_f[:, :, :], mask_u8[:, :, :]))
            for k in range(2):
                link(nc.vector.tensor_reduce(row_any[:, k, 0:1], mask_f[:, k, :], AX, ALU.max))
                link(nc.vector.tensor_scalar(row_any[:, k, 1:2], row_any[:, k, 0:1], -1.0, 1.0, ALU.mult, ALU.add))
                link(nc.vector.tensor_scalar(mask_f[:, k, :], mask_f[:, k, :], row_any[:, k, 1:2], None, ALU.max))
                link(nc.vector.tensor_scalar(row_wide[:, k, :], ones_w[:, :], row_any[:, k, 0:1], None, ALU.mult))
            dve.wait_ge(mask_tr, 1)
            link(nc.vector.tensor_copy(mask_t[:, :], bank[6][:, :]))
            dve.wait_ge(mask_tr, 2)
            dve.wait_ge(tab_in, 16)
            link(nc.vector.tensor_tensor(cos_q[:, :], bank[7][:, 0:S], cos_k, ALU.mult))
            link(nc.vector.tensor_tensor(sin_q[:, :], bank[7][:, 0:S], sin_k, ALU.mult))
            dve.wait_ge(tanh_g, 1)
            nc.vector.tensor_scalar(gates[:, 4:5], gates[:, 2:3], 1.0 / (OS * WS), None, ALU.mult).then_inc(tanh_g, 1)
            nc.vector.tensor_scalar(gates[:, 5:6], gates[:, 3:4], 1.0 / WS, None, ALU.mult).then_inc(tanh_g, 1)

            for c in range(DC):
                dve.wait_ge(wk_hi_set, c + 1)
                nc.vector.scalar_tensor_tensor(wk_lo[:, c, :], wst1[:, c % NST1, :], WS, wk_hi[:, c, :],
                                               ALU.mult, ALU.subtract).then_inc(wk_lo_set, 1)

            def layernorm(stat, rstd, done, n, src, dst, st, m):
                for k in range(2):
                    i = nc.vector.bn_stats(st[:, 6 * k:6 * k + 6], src[:, 512 * k:512 * k + 512])
                i.then_inc(stat, 1)
                groups = st.rearrange("p (g k) -> p g k", k=3)
                dve.wait_ge(stat, 8 * n + 1)
                nc.vector.tensor_reduce(m[:, 1:2], groups[:, :, 1], AX, ALU.add).then_inc(stat, 1)
                dve.wait_ge(stat, 8 * n + 2)
                nc.vector.tensor_scalar(m[:, 0:1], m[:, 1:2], 0.25, None, ALU.mult).then_inc(stat, 1)
                dve.wait_ge(stat, 8 * n + 3)
                nc.vector.tensor_scalar(m[:, 4:8], groups[:, :, 1], m[:, 0:1], None, ALU.subtract).then_inc(stat, 1)
                dve.wait_ge(stat, 8 * n + 4)
                nc.vector.scalar_tensor_tensor(m[:, 8:12], m[:, 4:8], D / 4.0, m[:, 4:8], ALU.mult, ALU.mult
                                               ).then_inc(stat, 1)
                dve.wait_ge(stat, 8 * n + 5)
                nc.vector.tensor_tensor(m[:, 12:16], m[:, 8:12], groups[:, :, 2], ALU.add).then_inc(stat, 1)
                dve.wait_ge(stat, 8 * n + 6)
                nc.vector.tensor_reduce(m[:, 1:2], m[:, 12:16], AX, ALU.add).then_inc(stat, 1)
                dve.wait_ge(stat, 8 * n + 7)
                nc.vector.tensor_scalar(m[:, 2:3], m[:, 1:2], 1.0 / D, EPS, ALU.mult, ALU.add).then_inc(stat, 1)
                dve.wait_ge(rstd, n + 1)
                nc.vector.tensor_scalar(dst, src, m[:, 0:1], m[:, 3:4], ALU.subtract, ALU.mult).then_inc(done, 1)

            def norm_x(q, t):
                dve.wait_ge(x_in[t], 16 * (q + 1))
                layernorm(ln1_stat, ln1_rstd, ln1, TP * q + t, x_raw[:, t, :], x_raw[:, t, :], stats[:, t, :], mv[:, t, :])

            for t in range(TP):
                norm_x(0, t)

            def rope(src, ra, rb, cos, sin, a_set, b_set, summed, n):
                two = "p (b t) -> p b t"
                wide = [P, 2, S]
                half = [P // 2, 2, S]
                lo, hi = slice(0, P // 2), slice(P // 2, P)
                nc.vector.tensor_tensor(ra[:, :].rearrange(two, b=2), src[:, :].rearrange(two, b=2),
                                        cos.unsqueeze(1).broadcast_to(wide), ALU.mult).then_inc(a_set, 1)
                nc.vector.tensor_tensor(rb[lo, :].rearrange(two, b=2), src[hi, :].rearrange(two, b=2),
                                        sin[hi, :].unsqueeze(1).broadcast_to(half), ALU.mult)
                nc.vector.tensor_tensor(rb[hi, :].rearrange(two, b=2), src[lo, :].rearrange(two, b=2),
                                        sin[lo, :].unsqueeze(1).broadcast_to(half), ALU.mult).then_inc(b_set, 1)
                dve.wait_ge(a_set, n + 1)
                dve.wait_ge(b_set, n + 1)
                nc.vector.tensor_tensor(ra[:, :], ra[:, :], rb[:, :], ALU.add).then_inc(summed, 1)

            def pair(q, more):
                for g in range(HK):
                    at_least(dve, xn_out, 16 * q)
                    bank_lo(DC + 16 * q + g, g % 2, xst[:, 1, g, :], xst[:, 0, g, :])
                    n = HK * q + g
                    dve.wait_ge(k_done, n + 1)
                    at_least(dve, k_lo, n)
                    rope(bank[2 + g % 2], ka, kb, cos_k, sin_k, kr_a, kr_read, k_roped, n)
                    dve.wait_ge(k_hi, n + 1)
                    at_least(dve, k_out[g % 2], 16 * (4 * q + g // 2))
                    nc.vector.tensor_tensor(kst[:, g % 2, 1, :], ka[:, :], kst[:, g % 2, 0, :], ALU.subtract
                                            ).then_inc(k_lo, 1)
                for v in range(2 * TP):
                    t, f = divmod(v, 2)
                    if more and t >= 1:
                        cols = (slice(None), slice(4 * f, 4 * f + 4), slice((t - 1) * P, t * P))
                        bank_lo(DC + 16 * q + DC + v - 2, v % 2, ct_lo[cols], ct_hi[cols])
                    dve.wait_ge(v_hi, 2 * TP * q + v + 1)
                    nc.vector.scalar_tensor_tensor(
                        vst[:, 4 * f:4 * f + 4, t, 1, :], bank[4 + v % 2][:, :].rearrange("p (g d) -> p g d", g=4),
                        VS / WS, vst[:, 4 * f:4 * f + 4, t, 0, :], ALU.mult, ALU.subtract).then_inc(v_lo, 1)
                    if more and f == 1:
                        norm_x(q + 1, t)
                if more:
                    for f in range(2):
                        cols = (slice(None), slice(4 * f, 4 * f + 4), slice(3 * P, 4 * P))
                        bank_lo(DC + 16 * q + DC + 6 + f, f, ct_lo[cols], ct_hi[cols])

            pair(0, True)
            with dve.Fori(1, NP - 1) as q:
                pair(q, True)
            pair(NP - 1, False)

            wait_phase1(dve)

            def split_piece(n, j, par):
                dve.wait_ge(w_hi, n + 1)
                if j < 4:
                    hi, lo = (wq_s[:, par, k, 2 * j:2 * j + 2, :].rearrange("p c n -> p (c n)") for k in range(2))
                else:
                    hi, lo = (wo_s[:, par, k, j - 4, :] for k in range(2))
                nc.vector.scalar_tensor_tensor(lo, wst2[:, j % 2, :], WS, hi, ALU.mult, ALU.subtract
                                               ).then_inc(w_lo, 1)

            def rope_q(n, qbank):
                dve.wait_ge(q_done, n + 1)
                at_least(dve, q_lo, n)
                rope(bank[qbank], qa, qb, cos_q[:, :], sin_q[:, :], q_a, q_read, q_roped, n)

            def q_low(n):
                dve.wait_ge(q_hi, n + 1)
                nc.vector.tensor_tensor(q_s[:, 1, :], qa[:, :], q_s[:, 0, :], ALU.subtract).then_inc(q_lo, 1)

            def o_low(p, pb, ph):
                dve.wait_ge(o_hi, p + 1)
                nc.vector.scalar_tensor_tensor(o_s[:, pb, ph, 1, :], bank[5][:, :], OS / (PS * VS),
                                               o_s[:, pb, ph, 0, :], ALU.mult, ALU.subtract).then_inc(o_lo, 1)

            def add_y(s, yb, t, k, half):
                dve.wait_ge(y_done[k], s - LAG + 1)
                dve.wait_ge(y_in[yb], 16 * (1 + half))
                y_p = y[:, yb, t, 512 * k:512 * k + 512]
                nc.vector.scalar_tensor_tensor(y_p, bank[6 + k][:, :], gates[:, 4:5], y_p, ALU.mult, ALU.add
                                               ).then_inc(y_added[k], 1)

            for j in range(8):
                split_piece(j, j, 0)
            rope_q(0, 2)
            q_low(0)

            def steps(it, par, first=False, last=False):
                for u in range(SPI):
                    s = SPI * it + u
                    b_now, h = divmod(u, GQ)
                    lagged = not (first and u < GQ)
                    half = it // HK if b_now == 1 else ((it - 1) // HK if lagged else 0)
                    if not last:
                        split_piece(8 * it + 8 + u, u, 1 - par)
                    if not (first and u == 0):
                        o_low(s - 1, ((u - 1) % SPI) // GQ, (u - 1) % GQ)
                    if not (last and u == SPI - 1):
                        rope_q(s + 1, 2 + (u + 1) % 2)
                    if lagged:
                        add_y(s, 1 - b_now, h, 0, half)
                    if not (last and u == SPI - 1):
                        q_low(s + 1)
                    dve.wait_ge(den_done, s + 1)
                    nc.vector.transpose(den_t[:, :], bank[4][:, :]).then_inc(den_read, 1)
                    dve.wait_ge(den_read, s + 1)
                    nc.vector.reciprocal(rden_t[:, :], den_t[:, :].rearrange("p (c j) -> p c j", j=32)[:, :, 0]
                                         ).then_inc(rden_t_done, 1)
                    dve.wait_ge(rden_t_done, s + 1)
                    at_least(dve, weighted, 2 * s)
                    nc.vector.transpose(rden[:, :].rearrange("p (c j) -> p c j", j=32),
                                        rden_t[:, :].unsqueeze(2).broadcast_to([P, PAIR // 32, 32])
                                        ).then_inc(rden_done, 1)
                    dve.wait_ge(rden_done, s + 1)
                    for b in range(2):
                        dve.wait_ge(esum_done, 2 * s + b + 1)
                        nc.vector.tensor_tensor(e_t[:, b, :, :], e_t[:, b, :, :],
                                                rden[:, b * S:(b + 1) * S].unsqueeze(1).broadcast_to([P, 2, S]),
                                                ALU.mult).then_inc(weighted, 1)
                    for b in range(2):
                        dve.wait_ge(p_hi, 2 * s + b + 1)
                        nc.vector.tensor_tensor(w_s[:, 1, b, :, :], e_t[:, b, :, :], w_s[:, 0, b, :, :],
                                                ALU.subtract).then_inc(p_lo, 1)
                    if lagged:
                        add_y(s, 1 - b_now, h, 1, half)

            steps(0, 0, first=True)
            with dve.Fori(0, NIT // 2 - 1) as j:
                steps(2 * j + 1, 1)
                steps(2 * j + 2, 0)
            steps(NIT - 1, 1, last=True)
            o_low(NSTEP - 1, PAIRS_PER_HALF - 1, GQ - 1)
            for t in range(TP):
                for k in range(2):
                    add_y(NSTEP + t, PAIRS_PER_HALF - 1, t, k, 1)

            wait_phase2(dve)
            dve.wait_ge(b3_in, 32)
            nc.vector.tensor_scalar(bias_row[:, :], bias_row[:, :], gates[:, 3:4], None, ALU.mult
                                    ).then_inc(bias_set, 1)
            nc.vector.tensor_scalar(thr_bias[:, 1:2], thr_bias[:, 0:1], 0.5, None, ALU.mult).then_inc(bias_set, 1)

            def norm_tile(i, slot, par):
                dve.wait_ge(x1_in[slot], 16 * (i // NX + 1))
                at_least(dve, tr3_done, NTR3W + 2 * (i - 1) if not (isinstance(i, int) and i < 2) else 0)
                layernorm(ln3_stat, ln3_rstd, ln3, i, x1t[:, slot, :], xn2[:, par, :], stats3[:, :], mv3[:, :])

            def bank3_lo(n, dst, hi, src, scale=1.0):
                dve.wait_ge(tr3_hi, n + 1)
                nc.vector.scalar_tensor_tensor(dst, src, scale, hi, ALU.mult, ALU.subtract).then_inc(tr3_lo, 1)

            norm_tile(0, 0, 0)
            norm_tile(1, 1, 1)
            for n, hi, lo, src, scale in weight_banks():
                bank3_lo(n, lo, hi, src, scale)

            def xt_low(i, par):
                for f in range(2):
                    bank3_lo(NTR3W + 2 * i + f, xt_lo[:, par, 4 * f:4 * f + 4, :], xt_hi[:, par, 4 * f:4 * f + 4, :],
                             bank[4 + f][:, :].rearrange("p (c t) -> p c t", c=4))

            xt_low(0, 0)

            def output(i, slot, par):
                at_least(dve, out_out[par], 16 * (i // 2))
                dve.wait_ge(x1_biased, i + 1)
                for f in range(2):
                    dve.wait_ge(ffn_done, 2 * i + f + 1)
                    cols = slice(512 * f, 512 * f + 512)
                    nc.vector.scalar_tensor_tensor(out_t[:, par, cols], bank[2 * par + f][:, :], gates[:, 5:6],
                                                   x1t[:, slot, cols], ALU.mult, ALU.add).then_inc(out_set, 1)

            def tile(i, u, first=False, more=1):
                par = u % 2
                G = gsm[:, par, :]
                n = [6 * i]

                def gate(ins):
                    ins.then_inc(gate_step, 1)
                    n[0] = n[0] + 1
                    dve.wait_ge(gate_step, n[0])

                if not first:
                    output(i - 1, (u - 1) % NX, 1 - par)
                if more >= 1:
                    xt_low(i + 1, 1 - par)
                dve.wait_ge(hg_done, i + 1)
                gate(nc.vector.tensor_reduce(G[:, 8:9], bank[6][:, E * R:E * R + E], AX, ALU.max))
                nc.vector.tensor_scalar(G[:, 9:10], G[:, 8:9], -1.0 / WS, None, ALU.mult).then_inc(gmax, 1)
                dve.wait_ge(gexp, 2 * i + 2)
                nc.vector.tensor_scalar(G[:, 11:12], G[:, 10:11], 1.0 / 16, 1.0 / 16, ALU.mult, ALU.add)
                gate(nc.vector.tensor_reduce(G[:, 12:13], G[:, 0:E], AX, ALU.add))
                gate(nc.vector.reciprocal(G[:, 13:14], G[:, 12:13]))
                gate(nc.vector.tensor_scalar(G[:, 16:24], G[:, 0:E], G[:, 13:14], G[:, 11:12],
                                             ALU.mult, ALU.subtract))
                nc.vector.tensor_scalar(G[:, 24:32], G[:, 16:24], 0.0, None, ALU.max).then_inc(gate_step, 1)
                dve.wait_ge(gate_step, 6 * i + 5)
                nc.vector.tensor_reduce(G[:, 32:33], G[:, 24:32], AX, ALU.add).then_inc(gate_step, 1)
                dve.wait_ge(gate_step, 6 * i + 6)
                sum_chain(dve, G, i)
                nc.vector.tensor_tensor(hw[:, :].rearrange("p (e r) -> p e r", e=E),
                                        bank[6][:, 0:E * R].rearrange("p (e r) -> p e r", e=E),
                                        G[:, 40:48].unsqueeze(2).broadcast_to([P, E, R]), ALU.mult
                                        ).then_inc(hw_set, 1)
                if more >= 2:
                    norm_tile(i + 2, (u + 2) % NX, par)
                dve.wait_ge(hwt_hi, i + 1)
                nc.vector.tensor_tensor(hwt[:, 1, :], bank[7][:, 0:P], hwt[:, 0, :], ALU.subtract
                                        ).then_inc(hwt_lo, 1)

            def sum_chain(dve, G, i):
                nc.vector.tensor_scalar(G[:, 33:34], G[:, 32:33], 0.0, G[:, 32:33], ALU.is_equal, ALU.add
                                        ).then_inc(wsum_step, 1)
                dve.wait_ge(wsum_step, 3 * i + 1)
                nc.vector.reciprocal(G[:, 34:35], G[:, 33:34]).then_inc(wsum_step, 1)
                dve.wait_ge(wsum_step, 3 * i + 2)
                nc.vector.tensor_scalar(G[:, 40:48], G[:, 24:32], G[:, 34:35], HS / WS, ALU.mult, ALU.mult
                                        ).then_inc(wsum_step, 1)
                dve.wait_ge(wsum_step, 3 * i + 3)

            tile(0, 0, first=True, more=2)
            for u in range(1, NX):
                tile(u, u, more=2)
            with dve.Fori(1, NT // NX - 1) as j:
                for u in range(NX):
                    tile(j * NX + u, u, more=2)
            for u in range(NX):
                tile(NT - NX + u, u, more=min(2, NX - 1 - u))
            output(NT - 1, NX - 1, 1)

        @block.tensor
        def _(pe):
            mm = nc.tensor.matmul

            def three(dst, st_hi, st_lo, mv_hi, mv_lo, start, stop):
                mm(dst, st_hi, mv_hi, start=start, stop=False)
                mm(dst, st_hi, mv_lo, start=False, stop=False)
                return mm(dst, st_lo, mv_hi, start=False, stop=stop)

            def transpose4(done, dst, srcs):
                for k, src in enumerate(srcs):
                    i = nc.tensor.transpose(dst[:, k * P:(k + 1) * P], src, ident)
                i.then_inc(done, 1)

            pe.wait_ge(tab_in, 16)

            def ctx_bank(n, par, t, f):
                at_least(pe, tr_lo, n - 1)
                transpose4(tr_done, bank[par], [ctx_raw[:, t, (4 * f + k) * P:(4 * f + k + 1) * P] for k in range(4)])

            for m in range(DC):
                t, f = divmod(m, 2)
                pe.wait_ge(ctx_in[t], 16)
                ctx_bank(m, m % 2, t, f)
            pe.wait_ge(setup_dve, 10)
            for c in range(2):
                for k in range(2):
                    i = nc.tensor.transpose(bank[6][:, c * S + k * P:c * S + (k + 1) * P],
                                            mask_f[:, k, c * P:(c + 1) * P], ident)
            i.then_inc(mask_tr, 1)
            for k in range(2):
                i = nc.tensor.transpose(bank[7][:, k * P:(k + 1) * P], row_wide[:, k, :], ident)
            i.then_inc(mask_tr, 1)

            def pair(q, more):
                for g in range(HK):
                    if g == 0:
                        pe.wait_ge(ln1, TP * (q + 1))
                    n = DC + 16 * q + g
                    pe.wait_ge(tr_lo, n - 1)
                    transpose4(tr_done, bank[g % 2], [x_raw[:, t, g * P:(g + 1) * P] for t in range(TP)])
                    if g == 0:
                        pe.wait_ge(wk_lo_set, DC)
                        pe.wait_ge(tr_lo, DC + 16 * q)
                    at_least(pe, kr_read, HK * q + max(g - 1, 0))
                    for c in range(DC):
                        w = slice(g * DH, (g + 1) * DH)
                        i = three(bank[2 + g % 2][:, :], wk_hi[:, c, w], wk_lo[:, c, w], ct_hi[:, c, :],
                                  ct_lo[:, c, :], c == 0, c == DC - 1)
                    i.then_inc(k_done, 1)
                for v in range(2 * TP):
                    t, f = divmod(v, 2)
                    if more and t >= 1:
                        if f == 0:
                            pe.wait_ge(ctx_in[t - 1], 16 * (q + 2))
                        ctx_bank(DC + 16 * q + DC + v - 2, v % 2, t - 1, f)
                    if v == 0:
                        pe.wait_ge(wv_lo_set, DC)
                    at_least(pe, v_lo, 2 * TP * q + max(v - 1, 0))
                    for c in range(DC):
                        r, w = slice(t * P, (t + 1) * P), slice(f * 512, (f + 1) * 512)
                        i = three(bank[4 + v % 2][:, :], ct_hi[:, c, r], ct_lo[:, c, r], wv_hi[:, c, w],
                                  wv_lo[:, c, w], c == 0, c == DC - 1)
                    i.then_inc(v_done, 1)
                if more:
                    pe.wait_ge(ctx_in[TP - 1], 16 * (q + 2))
                    for f in range(2):
                        ctx_bank(DC + 16 * q + DC + 6 + f, f, TP - 1, f)

            pair(0, True)
            with pe.Fori(1, NP - 1) as q:
                pair(q, True)
            pair(NP - 1, False)

            wait_phase1(pe)
            pe.wait_ge(ones_set, 1)

            def q_part(n, qbank, par, b, h, part):
                if part == 0:
                    at_least(pe, q_read, n - 1)
                cols = slice(h * DH, (h + 1) * DH)
                for c in range(4 * part, 4 * part + 4):
                    i = three(bank[qbank][:, :], wq_s[:, par, 0, c, cols], wq_s[:, par, 1, c, cols],
                              xn[:, b, 0, c, :], xn[:, b, 1, c, :], c == 0, c == DC - 1)
                if part == 1:
                    i.then_inc(q_done, 1)

            def av(p, pb):
                at_least(pe, o_lo, p)
                for b in range(2):
                    pe.wait_ge(p_hi, 2 * p + b + 1)
                    pe.wait_ge(p_lo, 2 * p + b + 1)
                    for k in range(2):
                        t = 2 * b + k
                        i = three(bank[5][:, b * S:(b + 1) * S], vt[:, pb, t, 0, :], vt[:, pb, t, 1, :],
                                  w_s[:, 0, b, k, :], w_s[:, 1, b, k, :], k == 0, k == 1)
                i.then_inc(av_done, 1)

            def wo_part(s, ob, par, t, k):
                at_least(pe, y_added[k], s - LAG)
                rows, cols = slice(t * P, (t + 1) * P), slice(512 * k, 512 * k + 512)
                for h in range(GQ):
                    i = three(bank[6 + k][:, :], o_s[:, ob, h, 0, rows], o_s[:, ob, h, 1, rows],
                              wo_s[:, par, 0, h, cols], wo_s[:, par, 1, h, cols], h == 0, h == GQ - 1)
                i.then_inc(y_done[k], 1)

            pe.wait_ge(w_lo, 4)
            pe.wait_ge(xn_in[0], 16)
            q_part(0, 2, 0, 0, 0, 0)
            q_part(0, 2, 0, 0, 0, 1)

            def steps(it, par, first=False, last=False):
                for u in range(SPI):
                    s = SPI * it + u
                    b_now, h = divmod(u, GQ)
                    lagged = not (first and u < GQ)
                    ends = last and u == SPI - 1
                    if h == 0:
                        pe.wait_ge(kv_in[b_now], 32 * (it + 1))
                    pe.wait_ge(q_hi, s + 1)
                    pe.wait_ge(q_lo, s + 1)
                    for b in range(2):
                        at_least(pe, tanh_done, 2 * s - 1 + b if not (first and u == 0) else 0)
                        for k in range(2):
                            keys = slice(b * S + k * P, b * S + (k + 1) * P)
                            qs = slice(b * S, (b + 1) * S)
                            i = three(bank[b][:, k * S:(k + 1) * S], kt[:, b_now, 0, keys], kt[:, b_now, 1, keys],
                                      q_s[:, 0, qs], q_s[:, 1, qs], True, True)
                        i.then_inc(logits_done, 1)
                    nu = (u + 1) % SPI
                    nb, nh = divmod(nu, GQ)
                    npar = par if nu else 1 - par
                    if not ends:
                        if nu == 0:
                            pe.wait_ge(w_lo, 8 * it + 8 + 4)
                        if nh == 0:
                            pe.wait_ge(xn_in[nb], 16 * (1 + ((it + 1) // HK if nu == 0 else it // HK)))
                        q_part(s + 1, 2 + nu % 2, npar, nb, nh, 0)
                    if not (first and u == 0):
                        av(s - 1, ((u - 1) % SPI) // GQ)
                    if not ends:
                        q_part(s + 1, 2 + nu % 2, npar, nb, nh, 1)
                    wpar = par if b_now == 1 else 1 - par
                    if lagged:
                        if h == 0:
                            pe.wait_ge(w_lo, 8 * (it + 1) if b_now == 1 else 8 * it)
                            pe.wait_ge(o_lo, s)
                        wo_part(s, 1 - b_now, wpar, h, 0)
                    at_least(pe, den_read, s)
                    pe.wait_ge(esum_lo, s + 1)
                    for k in range(2):
                        i = mm(bank[4][:, :], ones_r[:, :], esum_r[:, k, :], start=k == 0, stop=k == 1)
                    i.then_inc(den_done, 1)
                    if lagged:
                        wo_part(s, 1 - b_now, wpar, h, 1)

            steps(0, 0, first=True)
            with pe.Fori(0, NIT // 2 - 1) as j:
                steps(2 * j + 1, 1)
                steps(2 * j + 2, 0)
            steps(NIT - 1, 1, last=True)
            av(NSTEP - 1, PAIRS_PER_HALF - 1)
            pe.wait_ge(o_lo, NSTEP)
            for t in range(TP):
                for k in range(2):
                    wo_part(NSTEP + t, PAIRS_PER_HALF - 1, 1, t, k)

            wait_phase2(pe)

            def free3(n):
                at_least(pe, tr3_lo, n - 1)

            n = 0
            pe.wait_ge(w3_in, 16 * DC)
            for c in range(DC):
                for f in range(2):
                    free3(n)
                    transpose4(tr3_done, bank[4 + n % 2],
                               [wb_raw[:, 4 * f + k, c * P:(c + 1) * P] for k in range(4)])
                    n += 1
            pe.wait_ge(g3_in, 16 * (3 + DC))
            for c in range(DC):
                free3(n)
                b = bank[4 + n % 2]
                nc.tensor.transpose(b[:, 0:P], a_raw[:, c * P:(c + 1) * P], ident)
                nc.tensor.transpose(b[:, P:HGW], gt_raw[0:NG, c * P:(c + 1) * P], ident[0:NG, 0:NG]
                                    ).then_inc(tr3_done, 1)
                n += 1
            for f in range(2):
                free3(n)
                transpose4(tr3_done, bank[4 + n % 2],
                           [b_raw[:, 4 * f + k, :, :].rearrange("p e r -> p (e r)") for k in range(4)])
                n += 1

            def xt_banks(i, par):
                pe.wait_ge(ln3, i + 1)
                for f in range(2):
                    free3(NTR3W + 2 * i + f)
                    transpose4(tr3_done, bank[4 + f], [xn2[:, par, (4 * f + k) * P:(4 * f + k + 1) * P]
                                                       for k in range(4)])

            xt_banks(0, 0)

            def tile(i, par, more):
                pe.wait_ge(tr3_lo, NTR3W + 2 * i + 2)
                at_least(pe, hw_set, i)
                for c in range(DC):
                    ins = three(bank[6][:, 0:HGW], xt_hi[:, par, c, :], xt_lo[:, par, c, :],
                                ag_hi[:, c, 0:HGW], ag_lo[:, c, 0:HGW], c == 0, c == DC - 1)
                ins.then_inc(hg_done, 1)
                if more:
                    xt_banks(i + 1, 1 - par)
                for f in range(2):
                    at_least(pe, out_set, 2 * i - 3 + f if not (isinstance(i, int) and i < 2) else 0)
                    cols = slice(512 * f, 512 * f + 512)
                    for c in range(DC):
                        three(bank[2 * par + f][:, :], xt_hi[:, par, c, :], xt_lo[:, par, c, :],
                              wb_hi[:, c, cols], wb_lo[:, c, cols], c == 0, False)
                pe.wait_ge(hw_set, i + 1)
                at_least(pe, hwt_lo, i)
                nc.tensor.transpose(bank[7][:, 0:P], hw[:, :], ident).then_inc(hwt_done, 1)
                pe.wait_ge(hwt_lo, i + 1)
                for f in range(2):
                    cols = slice(512 * f, 512 * f + 512)
                    three(bank[2 * par + f][:, :], hwt[:, 0, :], hwt[:, 1, :], bt_hi[:, cols], bt_lo[:, cols],
                          False, True).then_inc(ffn_done, 1)

            tile(0, 0, True)
            tile(1, 1, True)
            with pe.Fori(1, NT // 2 - 1) as j:
                tile(2 * j, 0, True)
                tile(2 * j + 1, 1, True)
            tile(NT - 2, 0, True)
            tile(NT - 1, 1, False)


def rope_tables():
    import numpy as np
    exponents = np.arange(0, DH, 2, dtype=np.float32)
    inv_freq = (np.float32(1.0) / np.float32(10000.0) ** (exponents / np.float32(DH))).astype(np.float32)
    phase = (np.arange(S, dtype=np.float32)[:, None] * inv_freq[None, :]).astype(np.float32).T
    cos = np.cos(phase).astype(np.float32) * np.float32(QS / WS)
    sin = np.sin(phase).astype(np.float32) * np.float32(QS / WS)
    return np.ascontiguousarray(np.concatenate([
        np.concatenate([cos, cos], 0), np.concatenate([sin, -sin], 0), np.eye(P, dtype=np.float32)], 1))


NAMES = ['x', 'ctx_4096', 'mask_1x1xSxS2_bk0', 'g_xattn', 'g_ffn', 'L0_xattn_Wq', 'L0_xattn_Wk', 'L0_xattn_Wv',
         'L0_xattn_Wo', 'L0_ffn_W_base', 'L0_ffn_b_base', 'L0_ffn_W_gate', 'L0_ffn_W_thr', 'L0_ffn_b_thr',
         'L0_ffn_A', 'L0_ffn_B']


def kernel(**inputs):
    import numpy as np
    import concourse.bacc as bacc
    from concourse.bass_utils import run_bass_kernel_spmd

    nc = bacc.Bacc("TRN2", target_bir_lowering=False, num_devices=1)
    arrays, args = {}, []

    def give(name, a):
        arrays[name] = a
        args.append(nc.dram_tensor(name, a.shape, mybir.dt.from_np(a.dtype), kind="ExternalInput").ap())

    for name in NAMES:
        give("in_" + name, np.ascontiguousarray(inputs[name]))
    give("tables", rope_tables())
    out = nc.dram_tensor("out_x", (NB, S, D), F32, kind="ExternalOutput").ap()
    build(nc, *args, out)
    r = run_bass_kernel_spmd(nc, [arrays], core_ids=[0])
    return r.results[0]["out_x"]
```

```python
import concourse.bass as bass
from concourse import mybir
from contextlib import ExitStack

F32 = mybir.dt.float32
F32R = mybir.dt.float32r
F16 = mybir.dt.float16
U8 = mybir.dt.uint8
ALU = mybir.AluOpType
ACT = mybir.ActivationFunctionType
AX = mybir.AxisListType.X

P = 128
NB, S, D = 8, 256, 1024
HQ, HK, DH = 32, 8, 128
GQ = HQ // HK
ROWS = NB * S
PAIR = 2 * S
NP = ROWS // PAIR
TP = PAIR // P
DC = D // P
E, R = 8, 16
NG = E + 1
HGW = E * R + NG
NT = ROWS // P
EPS = 1e-5
ATTN_MULT = 0.08838834764831845
MAX_ATTN = 30.0

WS = 64.0
QS = 4.0
VS = 4.0
PS = 1024.0
OS = 4.0
HS = 16.0
BS = 8.0

PAIRS_PER_HALF = 2
NIT = 2 * HK
SPI = PAIRS_PER_HALF * GQ
NSTEP = NIT * SPI
LAG = GQ


def at_least(eng, sem, value):
    if isinstance(value, int) and value <= 0:
        return
    eng.wait_ge(sem, value)


def build(nc, x, ctx, mask, g_xattn, g_ffn, wq, wk, wv, wo, w_base, b_base, w_gate, w_thr, b_thr, a_dn, b_up,
          tables, out):
    x_rows = x.rearrange("b s d -> (b s) d")
    ctx_rows = ctx.rearrange("b s d -> (b s) d")
    out_rows = out.rearrange("b s d -> (b s) d")
    mask_rows = mask.rearrange("a b t s -> (a b t) s").rearrange("(k p) s -> p k s", p=P)

    k_scr = nc.dram_tensor("k_scr", (HK, NP, P, 2 * PAIR), F16, kind="Internal").ap()
    v_scr = nc.dram_tensor("v_scr", (HK, NP, P, TP * 2 * DH), F16, kind="Internal").ap()
    xn_scr = nc.dram_tensor("xn_scr", (NP, P, 2 * DC * PAIR), F16, kind="Internal").ap()
    x1_scr = nc.dram_tensor("x1_scr", (ROWS, D), F32, kind="Internal").ap()

    with ExitStack() as whole:
        def sem(name):
            return whole.enter_context(nc.semaphore(name))

        def sb(stack, name, shape, dt):
            return stack.enter_context(nc.sbuf_tensor(name, shape, dt))

        bank = [whole.enter_context(nc.psum_tensor(f"bank{i}", [P, 512], F32)) for i in range(8)]

        tab = sb(whole, "tab", [P, 2 * S + P], F32)
        cos_k, sin_k, ident = tab[:, 0:S], tab[:, S:2 * S], tab[:, 2 * S:2 * S + P]
        cos_q = sb(whole, "cos_q", [P, S], F32)
        sin_q = sb(whole, "sin_q", [P, S], F32)
        mask_t = sb(whole, "mask_t", [P, 2 * S], F32)
        gates = sb(whole, "gates", [P, 8], F32)
        ones_r = sb(whole, "ones_r", [P, P], F32R)
        mhalf = sb(whole, "mhalf", [P, 1], F32)

        wst2 = sb(whole, "wst2", [P, 2, D], F32)
        wq_even = sb(whole, "wq_even", [P, 2, DC, GQ * DH], F16)

        ph1 = ExitStack()
        wk_hi = sb(ph1, "wk_hi", [P, DC, D], F16)
        wk_lo = sb(ph1, "wk_lo", [P, DC, D], F16)
        ctx_raw = sb(ph1, "ctx_raw", [P, TP, D], F32)
        x_raw = sb(ph1, "x_raw", [P, TP, D], F32)
        wv_hi = sb(ph1, "wv_hi", [P, DC, D], F16)
        wv_lo = sb(ph1, "wv_lo", [P, DC, D], F16)
        ct_hi = sb(ph1, "ct_hi", [P, DC, PAIR], F16)
        ct_lo = sb(ph1, "ct_lo", [P, DC, PAIR], F16)
        xst = sb(ph1, "xst", [P, 2, DC, PAIR], F16)
        NST1 = 3
        wst1 = sb(ph1, "wst1", [P, NST1, D], F32)
        kst = sb(ph1, "kst", [P, 2, 2, PAIR], F16)
        vst = sb(ph1, "vst", [P, HK, TP, 2, DH], F16)
        ka = sb(ph1, "ka", [P, PAIR], F32)
        kb = sb(ph1, "kb", [P, PAIR], F32)
        stats = sb(ph1, "stats", [P, TP, 12], F32)
        mv = sb(ph1, "mv", [P, TP, 16], F32)
        mask_u8 = sb(ph1, "mask_u8", [P, 2, S], U8)
        mask_f = sb(ph1, "mask_f", [P, 2, S], F32)
        row_any = sb(ph1, "row_any", [P, 2, 2], F32)
        row_wide = sb(ph1, "row_wide", [P, 2, P], F32)
        ones_w = sb(ph1, "ones_w", [P, P], F32)
        ph1.close()

        ph2 = ExitStack()
        xn = sb(ph2, "xn", [P, PAIRS_PER_HALF, 2, DC, PAIR], F16)
        wo_even = sb(ph2, "wo_even", [P, 2, GQ, D], F16)
        kt = sb(ph2, "kt", [P, PAIRS_PER_HALF, 2, PAIR], F16)
        vt = sb(ph2, "vt", [P, PAIRS_PER_HALF, TP, 2, DH], F16)
        q_s = sb(ph2, "q_s", [P, 2, PAIR], F16)
        qa = sb(ph2, "qa", [P, PAIR], F32)
        qb = sb(ph2, "qb", [P, PAIR], F32)
        esum = sb(ph2, "esum", [P, PAIR], F32)
        y = sb(ph2, "y", [P, PAIRS_PER_HALF, TP, D], F32)
        e_t = sb(ph2, "e_t", [P, 2, 2, S], F32)
        w_s = sb(ph2, "w_s", [P, 2, 2, 2, S], F16)
        esum_r = sb(ph2, "esum_r", [P, 2, PAIR], F32R)
        den_t = sb(ph2, "den_t", [P, PAIR], F32)
        rden = sb(ph2, "rden", [P, PAIR], F32)
        wo_odd = sb(ph2, "wo_odd", [P, 2, GQ, D], F16)
        wq_odd = sb(ph2, "wq_odd", [P, 2, DC, GQ * DH], F16)
        o_s = sb(ph2, "o_s", [P, PAIRS_PER_HALF, GQ, 2, PAIR], F16)
        rden_t = sb(ph2, "rden_t", [P, PAIR // 32], F32)
        wq_s, wo_s = (wq_even, wq_odd), (wo_even, wo_odd)
        ph2.close()

        ph3 = ExitStack()
        wb_raw = sb(ph3, "wb_raw", [P, DC, D], F32)
        sb(ph3, "gap_wo_even", [P, 2, GQ, D], F16)
        bias_row = sb(ph3, "bias_row", [P, D], F32)
        b_raw = sb(ph3, "b_raw", [P, DC, E, R], F32)
        gsm = sb(ph3, "gsm", [P, 2, 64], F32)
        hw = sb(ph3, "hw", [P, E * R], F32)
        hwt = sb(ph3, "hwt", [P, 2, P], F16)
        stats3 = sb(ph3, "stats3", [P, 2, 12], F32)
        mv3 = sb(ph3, "mv3", [P, 2, 16], F32)
        thr_bias = sb(ph3, "thr_bias", [P, 8], F32)
        sb(ph3, "gap_small", [P, 1600], F32)
        NX = 4
        x1t = sb(ph3, "x1t", [P, NX, D], F32)
        out_t = sb(ph3, "out_t", [P, 2, D], F32)
        sb(ph3, "gap_y", [P, 2, D], F32)
        ag_hi = sb(ph3, "ag_hi", [P, DC, HGW + 1], F16)
        ag_lo = sb(ph3, "ag_lo", [P, DC, HGW + 1], F16)
        bt_hi = sb(ph3, "bt_hi", [P, D], F16)
        bt_lo = sb(ph3, "bt_lo", [P, D], F16)
        sb(ph3, "gap_e", [P, 1968], F32)
        sb(ph3, "gap_wo_odd", [P, 2, GQ, D], F16)
        xn2 = sb(ph3, "xn2", [P, 2, D], F32)
        xt_hi = sb(ph3, "xt_hi", [P, 2, DC, P], F16)
        xt_lo = sb(ph3, "xt_lo", [P, 2, DC, P], F16)
        a_raw, gt_raw = wst2[:, 0, :], wst2[:, 1, :]
        wb_hi = wq_even[:, :, :, :].rearrange("p a c n -> p (a c n)").rearrange("p (c n) -> p c n", c=DC)
        wb_lo = wo_even[:, :, :, :].rearrange("p a h n -> p (a h n)").rearrange("p (c n) -> p c n", c=DC)
        ph3.close()

        tab_in = sem("tab_in")
        mask_in = sem("mask_in")
        g_in = sem("g_in")
        setup_dve = sem("setup_dve")
        ones_set = sem("ones_set")
        mask_tr = sem("mask_tr")
        tanh_g = sem("tanh_g")
        ctx_in = [sem(f"ctx_in{t}") for t in range(TP)]
        x_in = [sem(f"x_in{t}") for t in range(TP)]
        wst1_in = [sem(f"wst1_in{t}") for t in range(NST1)]
        wk_hi_set = sem("wk_hi_set")
        wk_lo_set = sem("wk_lo_set")
        wv_hi_set = sem("wv_hi_set")
        wv_scaled = sem("wv_scaled")
        wv_lo_set = sem("wv_lo_set")
        tr_done = sem("tr_done")
        tr_hi = sem("tr_hi")
        tr_lo = sem("tr_lo")
        k_done = sem("k_done")
        v_done = sem("v_done")
        kr_a = sem("kr_a")
        kr_read = sem("kr_read")
        k_roped = sem("k_roped")
        k_hi = sem("k_hi")
        k_lo = sem("k_lo")
        v_hi = sem("v_hi")
        v_lo = sem("v_lo")
        ln1_stat = sem("ln1_stat")
        ln1_rstd = sem("ln1_rstd")
        ln1 = sem("ln1")
        mhalf_set = sem("mhalf_set")
        k_out = [sem("k_out0"), sem("k_out1")]
        v_out = sem("v_out")
        xn_out = sem("xn_out")

        wst2_in = [sem("wst2_in0"), sem("wst2_in1")]
        w_hi = sem("w_hi")
        w_lo = sem("w_lo")
        kv_in = [sem("kv_in0"), sem("kv_in1")]
        xn_in = [sem("xn_in0"), sem("xn_in1")]
        y_in = [sem("y_in0"), sem("y_in1")]
        y_out = [sem("y_out0"), sem("y_out1")]
        q_done = sem("q_done")
        q_a = sem("q_a")
        q_read = sem("q_read")
        q_roped = sem("q_roped")
        q_hi = sem("q_hi")
        q_lo = sem("q_lo")
        logits_done = sem("logits_done")
        tanh_done = sem("tanh_done")
        exp_done = sem("exp_done")
        masked = sem("masked")
        esum_done = sem("esum_done")
        esum_hi = sem("esum_hi")
        esum_lo = sem("esum_lo")
        den_done = sem("den_done")
        den_read = sem("den_read")
        rden_t_done = sem("rden_t_done")
        rden_done = sem("rden_done")
        weighted = sem("weighted")
        p_hi = sem("p_hi")
        p_lo = sem("p_lo")
        av_done = sem("av_done")
        o_hi = sem("o_hi")
        o_lo = sem("o_lo")
        y_done = [sem("y_done0"), sem("y_done1")]
        y_added = [sem("y_added0"), sem("y_added1")]

        wb_in = [sem("wb_in0"), sem("wb_in1")]
        bup_in = sem("bup_in")
        g3_in = sem("g3_in")
        b3_in = sem("b3_in")
        x1_in = [sem(f"x1_in{t}") for t in range(NX)]
        tr3_done = sem("tr3_done")
        tr3_hi = sem("tr3_hi")
        tr3_lo = sem("tr3_lo")
        bias_set = sem("bias_set")
        ln3_stat = sem("ln3_stat")
        ln3_rstd = sem("ln3_rstd")
        ln3 = sem("ln3")
        x1_biased = sem("x1_biased")
        hg_done = sem("hg_done")
        gmax = sem("gmax")
        gexp = sem("gexp")
        gate_step = sem("gate_step")
        wsum_step = sem("wsum_step")
        hw_set = sem("hw_set")
        hwt_done = sem("hwt_done")
        hwt_hi = sem("hwt_hi")
        hwt_lo = sem("hwt_lo")
        ffn_done = sem("ffn_done")
        out_set = sem("out_set")
        out_out = [sem("out_out0"), sem("out_out1")]

        NTR1 = 2 * DC * NP

        def transposes(more):
            order = []
            for v in range(2 * TP):
                if more and v >= 2:
                    order.append((v, "ctx", v - 2))
                order.append((v, "x", v))
            if more:
                order += [(2 * TP, "ctx", 6), (2 * TP, "ctx", 7)]
            return list(enumerate(order))

        def after_bank(q, more, kind, which):
            return DC + 16 * q + 1 + [k for k, (_, a, b) in transposes(more) if (a, b) == (kind, which)][0]

        NTR3W = 2 * DC + DC + 2

        def weight_banks():
            n = 0
            for f in range(2):
                for c in range(DC):
                    yield (n, wb_hi[:, c, f * 512:(f + 1) * 512], wb_lo[:, c, f * 512:(f + 1) * 512],
                           bank[n % 2][:, :], WS)
                    n += 1
            for c in range(DC):
                yield n, ag_hi[:, c, 0:HGW], ag_lo[:, c, 0:HGW], bank[n % 2][:, 0:HGW], WS
                n += 1
            for f in range(2):
                yield (n, bt_hi[:, f * 512:(f + 1) * 512], bt_lo[:, f * 512:(f + 1) * 512],
                       bank[n % 2][:, :], BS)
                n += 1

        def beside(k):
            return range(3 * k + 3, min(3 * k + 6, NTR3W))

        block = whole.enter_context(nc.Block())

        @block.sync
        def _(sp):
            sp.dma_start(tab[:, :], tables).then_inc(tab_in, 16)
            for t in range(TP):
                sp.dma_start(ctx_raw[:, t, :], ctx_rows[t * P:(t + 1) * P, :]).then_inc(ctx_in[t], 16)
            sp.dma_start(mask_u8[:, :, :], mask_rows).then_inc(mask_in, 16)
            sp.dma_start(gates[:, 0:1], g_xattn.partition_broadcast(P)).then_inc(g_in, 16)
            sp.dma_start(gates[:, 1:2], g_ffn.partition_broadcast(P)).then_inc(g_in, 16)

            def load_w(n, src):
                f, j = divmod(n % 8, 4)
                if n >= NST1:
                    if n - NST1 < 8:
                        sp.wait_ge(wk_lo_set, n - NST1 + 1)
                    else:
                        sp.wait_ge(wv_lo_set, n - NST1 - 8 + 1)
                sp.dma_start(wst1[:, n % NST1, :].rearrange("p (c n) -> p c n", c=2),
                             src[2 * j * P:(2 * j + 2) * P, f * 512:(f + 1) * 512].rearrange(
                                 "(c p) n -> p c n", p=P)).then_inc(wst1_in[n % NST1], 16)

            for n in range(8):
                load_w(n, wk)
            for n in range(8, 8 + NST1):
                load_w(n, wv)
            for t in range(TP):
                sp.dma_start(x_raw[:, t, :], x_rows[t * P:(t + 1) * P, :]).then_inc(x_in[t], 16)
            for t in range(TP):
                sp.wait_ge(tr_done, 2 * (t + 1))
                sp.dma_start(ctx_raw[:, t, :], ctx_rows[PAIR + t * P:PAIR + (t + 1) * P, :]).then_inc(ctx_in[t], 16)

            def store_k(q, g):
                sp.wait_ge(k_hi, q * HK + g + 1)
                sp.wait_ge(k_lo, q * HK + g + 1)
                sp.dma_start(k_scr[g, q, :, :], kst[:, g % 2, :, :].rearrange("p a t -> p (a t)")
                             ).then_inc(k_out[g % 2], 16)

            def store_xn(q, more):
                sp.wait_ge(tr_lo, after_bank(q, more, "x", 7))
                sp.dma_start(xn_scr[q, :, :], xst[:, :, :, :].rearrange("p a c t -> p (a c t)")).then_inc(xn_out, 16)

            def store_v(q):
                sp.wait_ge(v_lo, (q + 1) * 2 * TP)
                sp.dma_start(v_scr[:, q, :, :].rearrange("g p n -> p g n"),
                             vst[:, :, :, :, :].rearrange("p g t a d -> p g (t a d)")).then_inc(v_out, 16)

            def pair_io(q, more_ctx):
                for g in range(HK):
                    store_k(q, g)
                    if isinstance(q, int) and q == 0 and 8 + NST1 + g < 16:
                        load_w(8 + NST1 + g, wv)
                for t in range(TP):
                    if t == TP - 1:
                        for r in range(TP):
                            sp.wait_ge(tr_done, after_bank(q, True, "x", 7))
                            sp.dma_start(x_raw[:, r, :], x_rows[bass.ds(q * PAIR + PAIR + r * P, P), :]
                                         ).then_inc(x_in[r], 16)
                    if more_ctx:
                        sp.wait_ge(tr_done, after_bank(q, True, "ctx", 2 * t + 1))
                        sp.dma_start(ctx_raw[:, t, :], ctx_rows[bass.ds(q * PAIR + 2 * PAIR + t * P, P), :]
                                     ).then_inc(ctx_in[t], 16)
                store_xn(q, True)
                store_v(q)

            pair_io(0, True)
            with sp.Fori(1, NP - 2) as q:
                pair_io(q, True)
            pair_io(NP - 2, False)
            for g in range(HK):
                store_k(NP - 1, g)


            def load_piece(n_first, n, g):
                j = n_first
                at_least(sp, w_lo, n - 1)
                if j < 4:
                    src = wq[2 * j * P:(2 * j + 2) * P, bass.ds(g * GQ * DH, GQ * DH)].rearrange(
                        "(c p) n -> p c n", p=P)
                    dst = wst2[:, j % 2, :].rearrange("p (c n) -> p c n", c=2)
                else:
                    src = wo[bass.ds(g * GQ * DH + (j - 4) * DH, P), :]
                    dst = wst2[:, j % 2, :]
                sp.dma_start(dst, src).then_inc(wst2_in[j % 2], 16)

            def load_kv(b, g, half):
                q = half * PAIRS_PER_HALF + b
                sp.dma_start(kt[:, b, :, :].rearrange("p a t -> p (a t)"), k_scr[g, q, :, :]).then_inc(kv_in[b], 16)
                sp.dma_start(vt[:, b, :, :, :].rearrange("p t a d -> p (t a d)"), v_scr[g, q, :, :]
                             ).then_inc(kv_in[b], 16)

            def load_xn(b, half):
                sp.dma_start(xn[:, b, :, :, :].rearrange("p a c t -> p (a c t)"),
                             xn_scr[half * PAIRS_PER_HALF + b, :, :]).then_inc(xn_in[b], 16)

            def y_rows(dram, b, half):
                r0 = (half * PAIRS_PER_HALF + b) * PAIR
                return dram[r0:r0 + PAIR, :].rearrange("(t p) d -> p t d", p=P)

            def load_y(b, half):
                sp.dma_start(y[:, b, :, :], y_rows(x_rows, b, half)).then_inc(y_in[b], 16)

            def store_y(b, half):
                sp.dma_start(y_rows(x1_scr, b, half), y[:, b, :, :]).then_inc(y_out[b], 16)

            sp.wait_ge(k_done, HK * NP)
            sp.wait_ge(xn_out, 32)
            for b in range(PAIRS_PER_HALF):
                load_xn(b, 0)
            for j in range(8):
                load_piece(j, j, 0)
            sp.wait_ge(tr_done, NTR1)
            for k in range(2):
                sp.wait_ge(k_out[k], 16 * HK * NP // 2)
            sp.wait_ge(v_out, 16 * (NP - 1))
            load_kv(0, 0, 0)
            store_v(NP - 1)
            load_kv(1, 0, 0)
            store_xn(NP - 1, False)
            sp.wait_ge(v_done, 2 * TP * NP)
            load_y(0, 0)
            load_y(1, 0)
            sp.wait_ge(xn_out, 16 * NP)
            sp.wait_ge(v_out, 16 * NP)

            def loads(it, half, g, turn=False, last=False):
                for u in range(SPI):
                    if not last:
                        load_piece(u, 8 * it + 8 + u, (g + 1) if not turn else 0)
                    if u == 1 and not (isinstance(it, int) and it == 0):
                        sp.wait_ge(av_done, 8 * it)
                        load_kv(1, g, half)
                    if u == 5 and not last:
                        sp.wait_ge(av_done, 8 * it + 4)
                        if turn:
                            load_kv(0, 0, 1)
                        else:
                            load_kv(0, g + 1, half)
                    if turn and u == 5:
                        sp.wait_ge(q_done, 8 * it + 4)
                        load_xn(0, 1)
                    if isinstance(it, int) and it == HK:
                        if u == 1:
                            sp.wait_ge(q_done, 8 * it)
                            load_xn(1, 1)
                            for k in range(2):
                                sp.wait_ge(y_added[k], 8 * it - LAG)
                            store_y(0, 0)
                        if u == 2:
                            sp.wait_ge(y_out[0], 16)
                            load_y(0, 1)
                        if u == 5:
                            for k in range(2):
                                sp.wait_ge(y_added[k], 8 * it)
                            store_y(1, 0)
                        if u == 6:
                            sp.wait_ge(y_out[1], 16)
                            load_y(1, 1)

            loads(0, 0, 0)
            with sp.Fori(1, HK - 1) as it:
                loads(it, 0, it)
            loads(HK - 1, 0, HK - 1, turn=True)
            loads(HK, 1, 0)
            with sp.Fori(HK + 1, NIT - 1) as it:
                loads(it, 1, it - HK)
            loads(NIT - 1, 1, HK - 1, last=True)
            def load_base(f):
                for o in range(4 * f, 4 * f + 4):
                    sp.dma_start(wb_raw[:, o, :], w_base[o * P:(o + 1) * P, :]).then_inc(wb_in[f], 16)

            def load_x1(i, slot):
                sp.dma_start(x1t[:, slot, :], x1_scr[bass.ds(i * P, P), :]).then_inc(x1_in[slot], 16)

            sp.wait_ge(w_lo, 8 * NIT)
            sp.wait_ge(q_done, NSTEP - GQ)
            load_base(0)
            sp.dma_start(a_raw, a_dn.rearrange("e r d -> (e r) d")).then_inc(g3_in, 16)
            sp.dma_start(gt_raw[0:E, :], w_gate).then_inc(g3_in, 16)
            sp.dma_start(gt_raw[E:NG, :], w_thr).then_inc(g3_in, 16)
            sp.wait_ge(q_done, NSTEP)
            load_base(1)
            for k in range(2):
                sp.wait_ge(y_added[k], NSTEP - LAG)
            store_y(0, 1)
            sp.wait_ge(av_done, NSTEP)
            b_by_o = b_up.rearrange("e (k p) r -> k p e r", p=P)
            for o in range(DC):
                sp.dma_start(b_raw[:, o, :, :], b_by_o[o, :, :, :]).then_inc(bup_in, 16)
            sp.dma_start(bias_row[:, :], b_base.partition_broadcast(P)).then_inc(b3_in, 16)
            sp.dma_start(thr_bias[:, 0:1], b_thr.partition_broadcast(P)).then_inc(b3_in, 16)
            sp.wait_ge(y_out[0], 32)
            for i in range(NX):
                load_x1(i, i)
            for k in range(2):
                sp.wait_ge(y_added[k], NSTEP)
            store_y(1, 1)
            sp.wait_ge(y_out[1], 32)

            def rows_io(i, u, more):
                if more:
                    sp.wait_ge(out_set, 2 * i + 2)
                    load_x1(i + NX, u)
                sp.wait_ge(out_set, 2 * i + 2)
                sp.dma_start(out_rows[bass.ds(i * P, P), :], out_t[:, u % 2, :]).then_inc(out_out[u % 2], 16)

            with sp.Fori(0, NT // NX - 1) as j:
                for u in range(NX):
                    rows_io(j * NX + u, u, True)
            for u in range(NX):
                rows_io(NT - NX + u, u, False)
            for k in range(2):
                sp.wait_ge(out_out[k], 16 * NT // 2)

        @block.gpsimd
        def _(pool):
            nc.gpsimd.memset(mhalf[:, :], -0.5).then_inc(mhalf_set, 1)
            pool.wait_ge(mhalf_set, 1)

            def inverse_std(stat, rstd, n, m):
                pool.wait_ge(stat, 8 * n + 8)
                nc.gpsimd.tensor_tensor(m[:, 3:4], m[:, 2:3], mhalf[:, :], ALU.pow).then_inc(rstd, 1)

            for n in range(8):
                f, j = divmod(n, 4)
                w = wst1[:, (8 + n) % NST1, :]
                cols = (slice(None), slice(2 * j, 2 * j + 2), slice(f * 512, (f + 1) * 512))
                pool.wait_ge(wv_hi_set, n + 1)
                nc.gpsimd.tensor_scalar(w, w, WS, 1.0, ALU.mult, ALU.mult).then_inc(wv_scaled, 1)
                pool.wait_ge(wv_scaled, n + 1)
                nc.gpsimd.tensor_tensor(wv_lo[cols], w.rearrange("p (c n) -> p c n", c=2), wv_hi[cols], ALU.subtract
                                        ).then_inc(wv_lo_set, 1)
                if n % 2 == 1:
                    inverse_std(ln1_stat, ln1_rstd, n // 2, mv[:, n // 2, :])

            with pool.Fori(1, NP) as q:
                for t in range(TP):
                    inverse_std(ln1_stat, ln1_rstd, TP * q + t, mv[:, t, :])

            pool.wait_ge(setup_dve, 11)

            def step(s):
                for b in range(2):
                    pool.wait_ge(exp_done, 2 * s + b + 1)
                    e_b = e_t[:, b, :, :].rearrange("p k t -> p (k t)")
                    nc.gpsimd.tensor_tensor(e_b, e_b, mask_t[:, :], ALU.mult).then_inc(masked, 1)
                    pool.wait_ge(masked, 2 * s + b + 1)
                    at_least(pool, esum_lo, s)
                    nc.gpsimd.tensor_tensor(esum[:, b * S:(b + 1) * S], e_t[:, b, 0, :], e_t[:, b, 1, :],
                                            ALU.add).then_inc(esum_done, 1)
                pool.wait_ge(esum_hi, s + 1)
                at_least(pool, den_done, s)
                nc.gpsimd.tensor_tensor(esum_r[:, 1, :], esum[:, :], esum_r[:, 0, :].bitcast(F32), ALU.subtract
                                        ).then_inc(esum_lo, 1)

            step(0)
            with pool.Fori(1, NSTEP) as s:
                step(s)

            for i in range(2):
                inverse_std(ln3_stat, ln3_rstd, i, mv3[:, i, :])
            pool.wait_ge(b3_in, 32)
            pool.wait_ge(bias_set, 2)

            def biased(i, u):
                pool.wait_ge(ln3, i + 1)
                nc.gpsimd.tensor_tensor(x1t[:, u, :], x1t[:, u, :], bias_row[:, :], ALU.add).then_inc(x1_biased, 1)

            with pool.Fori(0, NT // NX - 1) as j:
                for u in range(NX):
                    biased(j * NX + u, u)
                    inverse_std(ln3_stat, ln3_rstd, j * NX + u + 2, mv3[:, u % 2, :])
            for u in range(NX):
                biased(NT - NX + u, u)
                if u < NX - 2:
                    inverse_std(ln3_stat, ln3_rstd, NT - NX + u + 2, mv3[:, u % 2, :])

        @block.scalar
        def _(act):
            act.wait_ge(g_in, 32)
            nc.scalar.activation(gates[:, 2:4], gates[:, 0:2], ACT.Tanh).then_inc(tanh_g, 1)

            def bank_hi(n, par, dst):
                act.wait_ge(tr_done, n + 1)
                src = bank[par][:, :]
                if len(dst.shape) == 3:
                    src = src.rearrange("p (a b) -> p a b", a=dst.shape[1])
                nc.scalar.activation(dst, src, ACT.Copy).then_inc(tr_hi, 1)

            for m in range(DC):
                t, f = divmod(m, 2)
                bank_hi(m, m % 2, ct_hi[:, 4 * f:4 * f + 4, t * P:(t + 1) * P])
            def split_w1(n, dst, done):
                f, j = divmod(n % 8, 4)
                act.wait_ge(wst1_in[n % NST1], 16 * (n // NST1 + 1))
                nc.scalar.activation(dst[:, 2 * j:2 * j + 2, f * 512:(f + 1) * 512],
                                     wst1[:, n % NST1, :].rearrange("p (c n) -> p c n", c=2),
                                     ACT.Copy, scale=WS).then_inc(done, 1)

            for n in range(8):
                split_w1(n, wk_hi, wk_hi_set)

            def split_piece(n, j, par, it):
                act.wait_ge(wst2_in[j % 2], 16 * (n // 2 + 1))
                if j < 4:
                    at_least(act, q_done, 8 * it if not isinstance(it, int) or it > 0 else 0)
                    dst = wq_s[par][:, 0, 2 * j:2 * j + 2, :].rearrange("p c n -> p (c n)")
                else:
                    at_least(act, y_done[1], 8 * it if not isinstance(it, int) or it > 0 else 0)
                    dst = wo_s[par][:, 0, j - 4, :]
                nc.scalar.activation(dst, wst2[:, j % 2, :], ACT.Copy, scale=WS).then_inc(w_hi, 1)

            def pair(q, more):
                for g in range(HK):
                    act.wait_ge(k_roped, HK * q + g + 1)
                    at_least(act, k_out[g % 2], 16 * (4 * q + g // 2))
                    nc.scalar.activation(kst[:, g % 2, 0, :], ka[:, :], ACT.Copy).then_inc(k_hi, 1)
                    if isinstance(q, int) and q == 0:
                        split_w1(8 + g, wv_hi, wv_hi_set)
                for v in range(2 * TP + 1):
                    for k, (slot, kind, m) in transposes(more):
                        if slot != v:
                            continue
                        t, f = divmod(m, 2)
                        if kind == "ctx":
                            act.wait_ge(v_done, 2 * TP * q + 2 * (t + 1))
                            bank_hi(DC + 16 * q + k, k % 2, ct_hi[:, 4 * f:4 * f + 4, t * P:(t + 1) * P])
                        else:
                            at_least(act, xn_out, 16 * q)
                            bank_hi(DC + 16 * q + k, k % 2, xst[:, 0, m, :])
                    if v == 2 * TP:
                        continue
                    if not more:
                        split_piece(v, v, 0, 0)
                    t, f = divmod(v, 2)
                    act.wait_ge(v_done, 2 * TP * q + v + 1)
                    at_least(act, v_out, 16 * q)
                    nc.scalar.activation(vst[:, 4 * f:4 * f + 4, t, 0, :],
                                         bank[4 + v % 2][:, :].rearrange("p (g d) -> p g d", g=4),
                                         ACT.Copy, scale=VS / WS).then_inc(v_hi, 1)

            pair(0, True)
            with act.Fori(1, NP - 1) as q:
                pair(q, True)
            pair(NP - 1, False)

            def q_high(n):
                act.wait_ge(q_roped, n + 1)
                at_least(act, logits_done, 2 * n)
                nc.scalar.activation(q_s[:, 0, :], qa[:, :], ACT.Copy).then_inc(q_hi, 1)

            def o_high(p, pb, ph):
                act.wait_ge(av_done, p + 1)
                at_least(act, y_done[1], p + 1 - LAG)
                nc.scalar.activation(o_s[:, pb, ph, 0, :], bank[5][:, :], ACT.Copy, scale=OS / (PS * VS)
                                     ).then_inc(o_hi, 1)

            q_high(0)
            act.wait_ge(wv_lo_set, 8)
            for k in range(2):
                act.wait_ge(k_out[k], 16 * HK * NP // 2)

            def steps(it, par, first=False, last=False):
                for u in range(SPI):
                    s = SPI * it + u
                    for b in range(2):
                        act.wait_ge(logits_done, 2 * s + b + 1)
                        at_least(act, p_lo, 2 * s - 1 + b if not (first and u == 0) else 0)
                        e_b = e_t[:, b, :, :].rearrange("p k t -> p (k t)")
                        nc.scalar.activation(e_b, bank[b][:, :], ACT.Tanh,
                                             scale=ATTN_MULT / (MAX_ATTN * QS * QS)).then_inc(tanh_done, 1)
                    for b in range(2):
                        act.wait_ge(tanh_done, 2 * s + b + 1)
                        e_b = e_t[:, b, :, :].rearrange("p k t -> p (k t)")
                        nc.scalar.activation(e_b, e_b, ACT.Exp, scale=MAX_ATTN).then_inc(exp_done, 1)
                    if first and u == GQ:
                        act.wait_ge(xn_out, 16 * NP)
                    if not last:
                        split_piece(8 * it + 8 + u, u, 1 - par, it)
                    if first and u == 1:
                        act.wait_ge(v_out, 16 * NP)
                    if not (first and u == 0):
                        o_high(s - 1, ((u - 1) % SPI) // GQ, (u - 1) % GQ)
                    act.wait_ge(esum_done, 2 * s + 2)
                    at_least(act, den_done, s)
                    nc.scalar.activation(esum_r[:, 0, :], esum[:, :], ACT.Copy).then_inc(esum_hi, 1)
                    if not (last and u == SPI - 1):
                        q_high(s + 1)
                    for b in range(2):
                        act.wait_ge(weighted, 2 * s + b + 1)
                        at_least(act, av_done, s)
                        nc.scalar.activation(w_s[:, 0, b, :, :], e_t[:, b, :, :], ACT.Copy).then_inc(p_hi, 1)

            steps(0, 0, first=True)
            with act.Fori(0, NIT // 2 - 1) as j:
                steps(2 * j + 1, 1)
                steps(2 * j + 2, 0)
            steps(NIT - 1, 1, last=True)
            o_high(NSTEP - 1, PAIRS_PER_HALF - 1, GQ - 1)

            def bank3_hi(n, dst, src, scale=1.0):
                act.wait_ge(tr3_done, n + 1)
                nc.scalar.activation(dst, src, ACT.Copy, scale=scale).then_inc(tr3_hi, 1)

            act.wait_ge(q_done, NSTEP)
            for n, dst, _, src, scale in weight_banks():
                bank3_hi(n, dst, src, scale)

            def xt_high(i, par):
                for f in range(2):
                    at_least(act, hg_done, i - 1)
                    at_least(act, ffn_done, 2 * i - 2)
                    bank3_hi(NTR3W + 2 * i + f, xt_hi[:, par, 4 * f:4 * f + 4, :],
                             bank[4 + f][:, :].rearrange("p (c t) -> p c t", c=4))

            xt_high(0, 0)

            def tile(i, par, more):
                if more:
                    xt_high(i + 1, 1 - par)
                act.wait_ge(gmax, i + 1)
                nc.scalar.activation(gsm[:, par, 0:E], bank[6][:, E * R:E * R + E], ACT.Exp,
                                     bias=gsm[:, par, 9:10], scale=1.0 / WS).then_inc(gexp, 1)
                nc.scalar.activation(gsm[:, par, 10:11], bank[6][:, E * R + E:HGW], ACT.Tanh,
                                     bias=thr_bias[:, 1:2], scale=0.5 / WS).then_inc(gexp, 1)
                act.wait_ge(hwt_done, i + 1)
                at_least(act, ffn_done, 2 * i)
                nc.scalar.activation(hwt[:, 0, :], bank[7][:, 0:P], ACT.Copy).then_inc(hwt_hi, 1)

            tile(0, 0, True)
            tile(1, 1, True)
            with act.Fori(1, NT // 2 - 1) as j:
                tile(2 * j, 0, True)
                tile(2 * j + 1, 1, True)
            tile(NT - 2, 0, True)
            tile(NT - 1, 1, False)

        @block.vector
        def _(dve):
            setup = [0]

            def link(ins):
                setup[0] += 1
                ins.then_inc(setup_dve, 1)
                dve.wait_ge(setup_dve, setup[0])

            link(nc.vector.memset(ones_w[:, :], 1.0))
            nc.vector.tensor_scalar(ones_r[:, :], ones_w[:, :], 1.0 / PS, None, ALU.mult).then_inc(ones_set, 1)

            def bank_lo(n, par, dst, hi):
                dve.wait_ge(tr_hi, n + 1)
                src = bank[par][:, :]
                if len(dst.shape) == 3:
                    src = src.rearrange("p (a b) -> p a b", a=dst.shape[1])
                nc.vector.tensor_tensor(dst, src, hi, ALU.subtract).then_inc(tr_lo, 1)

            for m in range(DC):
                t, f = divmod(m, 2)
                cols = (slice(None), slice(4 * f, 4 * f + 4), slice(t * P, (t + 1) * P))
                bank_lo(m, m % 2, ct_lo[cols], ct_hi[cols])

            for n in range(8):
                f, j = divmod(n, 4)
                dve.wait_ge(wk_hi_set, n + 1)
                cols = (slice(None), slice(2 * j, 2 * j + 2), slice(f * 512, (f + 1) * 512))
                nc.vector.scalar_tensor_tensor(wk_lo[cols], wst1[:, n % NST1, :].rearrange("p (c n) -> p c n", c=2),
                                               WS, wk_hi[cols], ALU.mult, ALU.subtract).then_inc(wk_lo_set, 1)

            def split_piece(n, j, par):
                dve.wait_ge(w_hi, n + 1)
                if j < 4:
                    hi, lo = (wq_s[par][:, k, 2 * j:2 * j + 2, :].rearrange("p c n -> p (c n)") for k in range(2))
                else:
                    hi, lo = (wo_s[par][:, k, j - 4, :] for k in range(2))
                nc.vector.scalar_tensor_tensor(lo, wst2[:, j % 2, :], WS, hi, ALU.mult, ALU.subtract
                                               ).then_inc(w_lo, 1)

            dve.wait_ge(mask_in, 16)
            link(nc.vector.tensor_copy(mask_f[:, :, :], mask_u8[:, :, :]))
            for k in range(2):
                link(nc.vector.tensor_reduce(row_any[:, k, 0:1], mask_f[:, k, :], AX, ALU.max))
                link(nc.vector.tensor_scalar(row_any[:, k, 1:2], row_any[:, k, 0:1], -1.0, 1.0, ALU.mult, ALU.add))
                link(nc.vector.tensor_scalar(mask_f[:, k, :], mask_f[:, k, :], row_any[:, k, 1:2], None, ALU.max))
                link(nc.vector.tensor_scalar(row_wide[:, k, :], ones_w[:, :], row_any[:, k, 0:1], None, ALU.mult))

            def masks_and_gates():
                dve.wait_ge(mask_tr, 1)
                link(nc.vector.tensor_copy(mask_t[:, :], bank[6][:, :]))
                dve.wait_ge(mask_tr, 2)
                link(nc.vector.tensor_tensor(cos_q[:, :], bank[7][:, 0:S], cos_k, ALU.mult))
                link(nc.vector.tensor_tensor(sin_q[:, :], bank[7][:, 0:S], sin_k, ALU.mult))
                dve.wait_ge(tanh_g, 1)
                link(nc.vector.tensor_scalar(gates[:, 4:5], gates[:, 2:3], 1.0 / (OS * WS), None, ALU.mult))
                link(nc.vector.tensor_scalar(gates[:, 5:6], gates[:, 3:4], 1.0 / WS, None, ALU.mult))

            dve.wait_ge(tab_in, 16)

            def layernorm(stat, rstd, done, n, src, dst, st, m):
                for k in range(2):
                    i = nc.vector.bn_stats(st[:, 6 * k:6 * k + 6], src[:, 512 * k:512 * k + 512])
                i.then_inc(stat, 1)
                groups = st.rearrange("p (g k) -> p g k", k=3)
                dve.wait_ge(stat, 8 * n + 1)
                nc.vector.tensor_reduce(m[:, 1:2], groups[:, :, 1], AX, ALU.add).then_inc(stat, 1)
                dve.wait_ge(stat, 8 * n + 2)
                nc.vector.tensor_scalar(m[:, 0:1], m[:, 1:2], 0.25, None, ALU.mult).then_inc(stat, 1)
                dve.wait_ge(stat, 8 * n + 3)
                nc.vector.tensor_scalar(m[:, 4:8], groups[:, :, 1], m[:, 0:1], None, ALU.subtract).then_inc(stat, 1)
                dve.wait_ge(stat, 8 * n + 4)
                nc.vector.scalar_tensor_tensor(m[:, 8:12], m[:, 4:8], D / 4.0, m[:, 4:8], ALU.mult, ALU.mult
                                               ).then_inc(stat, 1)
                dve.wait_ge(stat, 8 * n + 5)
                nc.vector.tensor_tensor(m[:, 12:16], m[:, 8:12], groups[:, :, 2], ALU.add).then_inc(stat, 1)
                dve.wait_ge(stat, 8 * n + 6)
                nc.vector.tensor_reduce(m[:, 1:2], m[:, 12:16], AX, ALU.add).then_inc(stat, 1)
                dve.wait_ge(stat, 8 * n + 7)
                nc.vector.tensor_scalar(m[:, 2:3], m[:, 1:2], 1.0 / D, EPS, ALU.mult, ALU.add).then_inc(stat, 1)
                dve.wait_ge(rstd, n + 1)
                nc.vector.tensor_scalar(dst, src, m[:, 0:1], m[:, 3:4], ALU.subtract, ALU.mult).then_inc(done, 1)

            def norm_x(q, t):
                dve.wait_ge(x_in[t], 16 * (q + 1))
                layernorm(ln1_stat, ln1_rstd, ln1, TP * q + t, x_raw[:, t, :], x_raw[:, t, :], stats[:, t, :], mv[:, t, :])

            def rope(src, ra, rb, cos, sin, a_set, b_set, summed, n):
                two = "p (b t) -> p b t"
                wide = [P, 2, S]
                half = [P // 2, 2, S]
                lo, hi = slice(0, P // 2), slice(P // 2, P)
                nc.vector.tensor_tensor(ra[:, :].rearrange(two, b=2), src[:, :].rearrange(two, b=2),
                                        cos.unsqueeze(1).broadcast_to(wide), ALU.mult).then_inc(a_set, 1)
                nc.vector.tensor_tensor(rb[lo, :].rearrange(two, b=2), src[hi, :].rearrange(two, b=2),
                                        sin[hi, :].unsqueeze(1).broadcast_to(half), ALU.mult)
                nc.vector.tensor_tensor(rb[hi, :].rearrange(two, b=2), src[lo, :].rearrange(two, b=2),
                                        sin[lo, :].unsqueeze(1).broadcast_to(half), ALU.mult).then_inc(b_set, 1)
                dve.wait_ge(a_set, n + 1)
                dve.wait_ge(b_set, n + 1)
                nc.vector.tensor_tensor(ra[:, :], ra[:, :], rb[:, :], ALU.add).then_inc(summed, 1)

            def pair(q, more):
                for g in range(HK):
                    n = HK * q + g
                    dve.wait_ge(k_done, n + 1)
                    at_least(dve, k_lo, n)
                    rope(bank[2 + g % 2], ka, kb, cos_k, sin_k, kr_a, kr_read, k_roped, n)
                    dve.wait_ge(k_hi, n + 1)
                    at_least(dve, k_out[g % 2], 16 * (4 * q + g // 2))
                    nc.vector.tensor_tensor(kst[:, g % 2, 1, :], ka[:, :], kst[:, g % 2, 0, :], ALU.subtract
                                            ).then_inc(k_lo, 1)
                    if g % 2 == 1:
                        norm_x(q, g // 2)
                for v in range(2 * TP + 1):
                    for k, (slot, kind, m) in transposes(more):
                        if slot != v:
                            continue
                        t, f = divmod(m, 2)
                        cols = (slice(None), slice(4 * f, 4 * f + 4), slice(t * P, (t + 1) * P))
                        if kind == "ctx":
                            bank_lo(DC + 16 * q + k, k % 2, ct_lo[cols], ct_hi[cols])
                        else:
                            bank_lo(DC + 16 * q + k, k % 2, xst[:, 1, m, :], xst[:, 0, m, :])
                    if v == 2 * TP:
                        continue
                    if not more:
                        split_piece(v, v, 0)
                    t, f = divmod(v, 2)
                    dve.wait_ge(v_hi, 2 * TP * q + v + 1)
                    nc.vector.scalar_tensor_tensor(
                        vst[:, 4 * f:4 * f + 4, t, 1, :], bank[4 + v % 2][:, :].rearrange("p (g d) -> p g d", g=4),
                        VS / WS, vst[:, 4 * f:4 * f + 4, t, 0, :], ALU.mult, ALU.subtract).then_inc(v_lo, 1)

            pair(0, True)
            masks_and_gates()
            with dve.Fori(1, NP - 1) as q:
                pair(q, True)
            pair(NP - 1, False)

            def rope_q(n, qbank):
                dve.wait_ge(q_done, n + 1)
                at_least(dve, q_lo, n)
                rope(bank[qbank], qa, qb, cos_q[:, :], sin_q[:, :], q_a, q_read, q_roped, n)

            def q_low(n):
                dve.wait_ge(q_hi, n + 1)
                nc.vector.tensor_tensor(q_s[:, 1, :], qa[:, :], q_s[:, 0, :], ALU.subtract).then_inc(q_lo, 1)

            def o_low(p, pb, ph):
                dve.wait_ge(o_hi, p + 1)
                nc.vector.scalar_tensor_tensor(o_s[:, pb, ph, 1, :], bank[5][:, :], OS / (PS * VS),
                                               o_s[:, pb, ph, 0, :], ALU.mult, ALU.subtract).then_inc(o_lo, 1)

            def add_y(s, yb, t, k, half):
                dve.wait_ge(y_done[k], s - LAG + 1)
                dve.wait_ge(y_in[yb], 16 * (1 + half))
                y_p = y[:, yb, t, 512 * k:512 * k + 512]
                nc.vector.scalar_tensor_tensor(y_p, bank[6 + k][:, :], gates[:, 4:5], y_p, ALU.mult, ALU.add
                                               ).then_inc(y_added[k], 1)

            rope_q(0, 2)
            q_low(0)

            def steps(it, par, first=False, last=False):
                for u in range(SPI):
                    s = SPI * it + u
                    b_now, h = divmod(u, GQ)
                    lagged = not (first and u < GQ)
                    half = it // HK if b_now == 1 else ((it - 1) // HK if lagged else 0)
                    if not last:
                        split_piece(8 * it + 8 + u, u, 1 - par)
                    if not (first and u == 0):
                        o_low(s - 1, ((u - 1) % SPI) // GQ, (u - 1) % GQ)
                    if not (last and u == SPI - 1):
                        rope_q(s + 1, 2 + (u + 1) % 2)
                    if lagged:
                        add_y(s, 1 - b_now, h, 0, half)
                    if not (last and u == SPI - 1):
                        q_low(s + 1)
                    dve.wait_ge(den_done, s + 1)
                    nc.vector.transpose(den_t[:, :], bank[4][:, :]).then_inc(den_read, 1)
                    dve.wait_ge(den_read, s + 1)
                    nc.vector.reciprocal(rden_t[:, :], den_t[:, :].rearrange("p (c j) -> p c j", j=32)[:, :, 0]
                                         ).then_inc(rden_t_done, 1)
                    dve.wait_ge(rden_t_done, s + 1)
                    at_least(dve, weighted, 2 * s)
                    nc.vector.transpose(rden[:, :].rearrange("p (c j) -> p c j", j=32),
                                        rden_t[:, :].unsqueeze(2).broadcast_to([P, PAIR // 32, 32])
                                        ).then_inc(rden_done, 1)
                    dve.wait_ge(rden_done, s + 1)
                    for b in range(2):
                        dve.wait_ge(esum_done, 2 * s + b + 1)
                        nc.vector.tensor_tensor(e_t[:, b, :, :], e_t[:, b, :, :],
                                                rden[:, b * S:(b + 1) * S].unsqueeze(1).broadcast_to([P, 2, S]),
                                                ALU.mult).then_inc(weighted, 1)
                    for b in range(2):
                        dve.wait_ge(p_hi, 2 * s + b + 1)
                        nc.vector.tensor_tensor(w_s[:, 1, b, :, :], e_t[:, b, :, :], w_s[:, 0, b, :, :],
                                                ALU.subtract).then_inc(p_lo, 1)
                    if lagged:
                        add_y(s, 1 - b_now, h, 1, half)

            steps(0, 0, first=True)
            with dve.Fori(0, NIT // 2 - 1) as j:
                steps(2 * j + 1, 1)
                steps(2 * j + 2, 0)
            steps(NIT - 1, 1, last=True)
            o_low(NSTEP - 1, PAIRS_PER_HALF - 1, GQ - 1)

            def norm_tile(i, slot, par):
                dve.wait_ge(x1_in[slot], 16 * (i // NX + 1))
                at_least(dve, tr3_done, NTR3W + 2 * (i - 1) if not (isinstance(i, int) and i < 2) else 0)
                layernorm(ln3_stat, ln3_rstd, ln3, i, x1t[:, slot, :], xn2[:, par, :], stats3[:, par, :], mv3[:, par, :])

            def bank3_lo(n, dst, hi, src, scale=1.0):
                dve.wait_ge(tr3_hi, n + 1)
                nc.vector.scalar_tensor_tensor(dst, src, scale, hi, ALU.mult, ALU.subtract).then_inc(tr3_lo, 1)

            banks = list(weight_banks())

            def banks_beside(k):
                for i in beside(k):
                    n, hi, lo, src, scale = banks[i]
                    bank3_lo(n, lo, hi, src, scale)

            banks_beside(-1)
            for t in range(TP):
                for k in range(2):
                    add_y(NSTEP + t, PAIRS_PER_HALF - 1, t, k, 1)
                    banks_beside(2 * t + k)
                if t >= 2:
                    norm_tile(t - 2, t - 2, t - 2)
            dve.wait_ge(b3_in, 32)
            nc.vector.tensor_scalar(bias_row[:, :], bias_row[:, :], gates[:, 3:4], None, ALU.mult
                                    ).then_inc(bias_set, 1)
            nc.vector.tensor_scalar(thr_bias[:, 1:2], thr_bias[:, 0:1], 0.5, None, ALU.mult).then_inc(bias_set, 1)

            def xt_low(i, par):
                for f in range(2):
                    bank3_lo(NTR3W + 2 * i + f, xt_lo[:, par, 4 * f:4 * f + 4, :], xt_hi[:, par, 4 * f:4 * f + 4, :],
                             bank[4 + f][:, :].rearrange("p (c t) -> p c t", c=4))

            xt_low(0, 0)

            def output(i, slot, par):
                at_least(dve, out_out[par], 16 * (i // 2))
                dve.wait_ge(y_out[1], 32)
                dve.wait_ge(x1_biased, i + 1)
                for f in range(2):
                    dve.wait_ge(ffn_done, 2 * i + f + 1)
                    cols = slice(512 * f, 512 * f + 512)
                    nc.vector.scalar_tensor_tensor(out_t[:, par, cols], bank[2 * par + f][:, :], gates[:, 5:6],
                                                   x1t[:, slot, cols], ALU.mult, ALU.add).then_inc(out_set, 1)

            def tile(i, u, first=False, more=1):
                par = u % 2
                G = gsm[:, par, :]
                n = [6 * i]

                def gate(ins):
                    ins.then_inc(gate_step, 1)
                    n[0] = n[0] + 1
                    dve.wait_ge(gate_step, n[0])

                if not first:
                    output(i - 1, (u - 1) % NX, 1 - par)
                if more >= 1:
                    xt_low(i + 1, 1 - par)
                dve.wait_ge(hg_done, i + 1)
                gate(nc.vector.tensor_reduce(G[:, 8:9], bank[6][:, E * R:E * R + E], AX, ALU.max))
                nc.vector.tensor_scalar(G[:, 9:10], G[:, 8:9], -1.0 / WS, None, ALU.mult).then_inc(gmax, 1)
                dve.wait_ge(gexp, 2 * i + 2)
                nc.vector.tensor_scalar(G[:, 11:12], G[:, 10:11], 1.0 / 16, 1.0 / 16, ALU.mult, ALU.add)
                gate(nc.vector.tensor_reduce(G[:, 12:13], G[:, 0:E], AX, ALU.add))
                gate(nc.vector.reciprocal(G[:, 13:14], G[:, 12:13]))
                gate(nc.vector.tensor_scalar(G[:, 16:24], G[:, 0:E], G[:, 13:14], G[:, 11:12],
                                             ALU.mult, ALU.subtract))
                nc.vector.tensor_scalar(G[:, 24:32], G[:, 16:24], 0.0, None, ALU.max).then_inc(gate_step, 1)
                dve.wait_ge(gate_step, 6 * i + 5)
                nc.vector.tensor_reduce(G[:, 32:33], G[:, 24:32], AX, ALU.add).then_inc(gate_step, 1)
                dve.wait_ge(gate_step, 6 * i + 6)
                sum_chain(dve, G, i)
                nc.vector.tensor_tensor(hw[:, :].rearrange("p (e r) -> p e r", e=E),
                                        bank[6][:, 0:E * R].rearrange("p (e r) -> p e r", e=E),
                                        G[:, 40:48].unsqueeze(2).broadcast_to([P, E, R]), ALU.mult
                                        ).then_inc(hw_set, 1)
                if more >= 2:
                    norm_tile(i + 2, (u + 2) % NX, par)
                dve.wait_ge(hwt_hi, i + 1)
                nc.vector.tensor_tensor(hwt[:, 1, :], bank[7][:, 0:P], hwt[:, 0, :], ALU.subtract
                                        ).then_inc(hwt_lo, 1)

            def sum_chain(dve, G, i):
                nc.vector.tensor_scalar(G[:, 33:34], G[:, 32:33], 0.0, G[:, 32:33], ALU.is_equal, ALU.add
                                        ).then_inc(wsum_step, 1)
                dve.wait_ge(wsum_step, 3 * i + 1)
                nc.vector.reciprocal(G[:, 34:35], G[:, 33:34]).then_inc(wsum_step, 1)
                dve.wait_ge(wsum_step, 3 * i + 2)
                nc.vector.tensor_scalar(G[:, 40:48], G[:, 24:32], G[:, 34:35], HS / WS, ALU.mult, ALU.mult
                                        ).then_inc(wsum_step, 1)
                dve.wait_ge(wsum_step, 3 * i + 3)

            tile(0, 0, first=True, more=2)
            for u in range(1, NX):
                tile(u, u, more=2)
            with dve.Fori(1, NT // NX - 1) as j:
                for u in range(NX):
                    tile(j * NX + u, u, more=2)
            for u in range(NX):
                tile(NT - NX + u, u, more=min(2, NX - 1 - u))
            output(NT - 1, NX - 1, 1)

        @block.tensor
        def _(pe):
            mm = nc.tensor.matmul

            def three(dst, st_hi, st_lo, mv_hi, mv_lo, start, stop):
                mm(dst, st_hi, mv_hi, start=start, stop=False)
                mm(dst, st_hi, mv_lo, start=False, stop=False)
                return mm(dst, st_lo, mv_hi, start=False, stop=stop)

            def transpose4(done, dst, srcs):
                for k, src in enumerate(srcs):
                    i = nc.tensor.transpose(dst[:, k * P:(k + 1) * P], src, ident)
                i.then_inc(done, 1)

            pe.wait_ge(tab_in, 16)

            def ctx_bank(n, par, t, f):
                at_least(pe, tr_lo, n - 1)
                transpose4(tr_done, bank[par], [ctx_raw[:, t, (4 * f + k) * P:(4 * f + k + 1) * P] for k in range(4)])

            for m in range(DC):
                t, f = divmod(m, 2)
                pe.wait_ge(ctx_in[t], 16)
                ctx_bank(m, m % 2, t, f)

            def mask_banks():
                pe.wait_ge(setup_dve, 10)
                for c in range(2):
                    for k in range(2):
                        i = nc.tensor.transpose(bank[6][:, c * S + k * P:c * S + (k + 1) * P],
                                                mask_f[:, k, c * P:(c + 1) * P], ident)
                i.then_inc(mask_tr, 1)
                for k in range(2):
                    i = nc.tensor.transpose(bank[7][:, k * P:(k + 1) * P], row_wide[:, k, :], ident)
                i.then_inc(mask_tr, 1)

            def pair(q, more):
                for g in range(HK):
                    if g % 4 == 0:
                        pe.wait_ge(wk_lo_set, 4 + g)
                    if g == 0:
                        pe.wait_ge(tr_lo, DC + 16 * q)
                    at_least(pe, kr_read, HK * q + max(g - 1, 0))
                    for c in range(DC):
                        w = slice(g * DH, (g + 1) * DH)
                        i = three(bank[2 + g % 2][:, :], wk_hi[:, c, w], wk_lo[:, c, w], ct_hi[:, c, :],
                                  ct_lo[:, c, :], c == 0, c == DC - 1)
                    i.then_inc(k_done, 1)
                pe.wait_ge(ln1, TP * (q + 1))
                for v in range(2 * TP + 1):
                    for k, (slot, kind, m) in transposes(more):
                        if slot != v:
                            continue
                        t, f = divmod(m, 2)
                        n = DC + 16 * q + k
                        if kind == "ctx":
                            pe.wait_ge(ctx_in[t], 16 * (q + 2))
                            ctx_bank(n, k % 2, t, f)
                        else:
                            pe.wait_ge(tr_lo, n - 1)
                            transpose4(tr_done, bank[k % 2], [x_raw[:, t, m * P:(m + 1) * P] for t in range(TP)])
                    if v == 2 * TP:
                        continue
                    t, f = divmod(v, 2)
                    if v < 2:
                        pe.wait_ge(wv_lo_set, 4 + 4 * v)
                    at_least(pe, v_lo, 2 * TP * q + max(v - 1, 0))
                    for c in range(DC):
                        r, w = slice(t * P, (t + 1) * P), slice(f * 512, (f + 1) * 512)
                        i = three(bank[4 + v % 2][:, :], ct_hi[:, c, r], ct_lo[:, c, r], wv_hi[:, c, w],
                                  wv_lo[:, c, w], c == 0, c == DC - 1)
                    i.then_inc(v_done, 1)

            pair(0, True)
            mask_banks()
            with pe.Fori(1, NP - 1) as q:
                pair(q, True)
            pair(NP - 1, False)

            def q_part(n, qbank, par, b, h, part):
                if part == 0:
                    at_least(pe, q_read, n - 1)
                cols = slice(h * DH, (h + 1) * DH)
                for c in range(4 * part, 4 * part + 4):
                    i = three(bank[qbank][:, :], wq_s[par][:, 0, c, cols], wq_s[par][:, 1, c, cols],
                              xn[:, b, 0, c, :], xn[:, b, 1, c, :], c == 0, c == DC - 1)
                if part == 1:
                    i.then_inc(q_done, 1)

            def av(p, pb):
                at_least(pe, o_lo, p)
                for b in range(2):
                    pe.wait_ge(p_hi, 2 * p + b + 1)
                    pe.wait_ge(p_lo, 2 * p + b + 1)
                    for k in range(2):
                        t = 2 * b + k
                        i = three(bank[5][:, b * S:(b + 1) * S], vt[:, pb, t, 0, :], vt[:, pb, t, 1, :],
                                  w_s[:, 0, b, k, :], w_s[:, 1, b, k, :], k == 0, k == 1)
                i.then_inc(av_done, 1)

            def wo_part(s, ob, par, t, k):
                at_least(pe, y_added[k], s - LAG)
                rows, cols = slice(t * P, (t + 1) * P), slice(512 * k, 512 * k + 512)
                for h in range(GQ):
                    i = three(bank[6 + k][:, :], o_s[:, ob, h, 0, rows], o_s[:, ob, h, 1, rows],
                              wo_s[par][:, 0, h, cols], wo_s[par][:, 1, h, cols], h == 0, h == GQ - 1)
                i.then_inc(y_done[k], 1)

            pe.wait_ge(w_lo, 4)
            pe.wait_ge(xn_in[0], 16)
            pe.wait_ge(kr_read, HK * NP)
            q_part(0, 2, 0, 0, 0, 0)
            q_part(0, 2, 0, 0, 0, 1)
            pe.wait_ge(tr_lo, NTR1)
            pe.wait_ge(v_lo, 2 * TP * NP)
            pe.wait_ge(setup_dve, 13)
            pe.wait_ge(ones_set, 1)

            def steps(it, par, first=False, last=False):
                for u in range(SPI):
                    s = SPI * it + u
                    b_now, h = divmod(u, GQ)
                    lagged = not (first and u < GQ)
                    ends = last and u == SPI - 1
                    if h == 0:
                        pe.wait_ge(kv_in[b_now], 32 * (it + 1))
                    pe.wait_ge(q_hi, s + 1)
                    pe.wait_ge(q_lo, s + 1)
                    for b in range(2):
                        at_least(pe, tanh_done, 2 * s - 1 + b if not (first and u == 0) else 0)
                        for k in range(2):
                            keys = slice(b * S + k * P, b * S + (k + 1) * P)
                            qs = slice(b * S, (b + 1) * S)
                            i = three(bank[b][:, k * S:(k + 1) * S], kt[:, b_now, 0, keys], kt[:, b_now, 1, keys],
                                      q_s[:, 0, qs], q_s[:, 1, qs], True, True)
                        i.then_inc(logits_done, 1)
                    nu = (u + 1) % SPI
                    nb, nh = divmod(nu, GQ)
                    npar = par if nu else 1 - par
                    if not ends:
                        if nu == 0:
                            pe.wait_ge(w_lo, 8 * it + 8 + 4)
                        if nh == 0:
                            pe.wait_ge(xn_in[nb], 16 * (1 + ((it + 1) // HK if nu == 0 else it // HK)))
                        q_part(s + 1, 2 + nu % 2, npar, nb, nh, 0)
                    if not (first and u == 0):
                        av(s - 1, ((u - 1) % SPI) // GQ)
                    if not ends:
                        q_part(s + 1, 2 + nu % 2, npar, nb, nh, 1)
                    wpar = par if b_now == 1 else 1 - par
                    if lagged:
                        if h == 0:
                            pe.wait_ge(w_lo, 8 * (it + 1) if b_now == 1 else 8 * it)
                            pe.wait_ge(o_lo, s)
                        wo_part(s, 1 - b_now, wpar, h, 0)
                    at_least(pe, den_read, s)
                    pe.wait_ge(esum_lo, s + 1)
                    for k in range(2):
                        i = mm(bank[4][:, :], ones_r[:, :], esum_r[:, k, :], start=k == 0, stop=k == 1)
                    i.then_inc(den_done, 1)
                    if lagged:
                        wo_part(s, 1 - b_now, wpar, h, 1)

            steps(0, 0, first=True)
            with pe.Fori(0, NIT // 2 - 1) as j:
                steps(2 * j + 1, 1)
                steps(2 * j + 2, 0)
            steps(NIT - 1, 1, last=True)
            av(NSTEP - 1, PAIRS_PER_HALF - 1)

            def free3(n):
                at_least(pe, tr3_lo, n - 1)

            def banks_beside(j):
                for n in beside(j):
                    free3(n)
                    b = bank[n % 2]
                    if n < 2 * DC:
                        f, c = divmod(n, DC)
                        if c == 0:
                            pe.wait_ge(wb_in[f], 16 * 4)
                        transpose4(tr3_done, b, [wb_raw[:, 4 * f + k, c * P:(c + 1) * P] for k in range(4)])
                    elif n < 3 * DC:
                        c = n - 2 * DC
                        pe.wait_ge(g3_in, 16 * 3)
                        nc.tensor.transpose(b[:, 0:P], a_raw[:, c * P:(c + 1) * P], ident)
                        nc.tensor.transpose(b[:, P:HGW], gt_raw[0:NG, c * P:(c + 1) * P], ident[0:NG, 0:NG]
                                            ).then_inc(tr3_done, 1)
                    else:
                        f = n - 3 * DC
                        pe.wait_ge(bup_in, 16 * DC)
                        transpose4(tr3_done, b,
                                   [b_raw[:, 4 * f + k, :, :].rearrange("p e r -> p (e r)") for k in range(4)])

            pe.wait_ge(tanh_done, 2 * NSTEP)
            banks_beside(-1)
            pe.wait_ge(o_lo, NSTEP)
            for t in range(TP):
                for k in range(2):
                    wo_part(NSTEP + t, PAIRS_PER_HALF - 1, 1, t, k)
                    banks_beside(2 * t + k)

            def xt_banks(i, par):
                pe.wait_ge(ln3, i + 1)
                for f in range(2):
                    free3(NTR3W + 2 * i + f)
                    transpose4(tr3_done, bank[4 + f], [xn2[:, par, (4 * f + k) * P:(4 * f + k + 1) * P]
                                                       for k in range(4)])

            xt_banks(0, 0)
            pe.wait_ge(y_added[0], NSTEP)
            pe.wait_ge(y_added[1], NSTEP)

            def tile(i, par, more):
                pe.wait_ge(tr3_lo, NTR3W + 2 * i + 2)
                at_least(pe, hw_set, i)
                for c in range(DC):
                    ins = three(bank[6][:, 0:HGW], xt_hi[:, par, c, :], xt_lo[:, par, c, :],
                                ag_hi[:, c, 0:HGW], ag_lo[:, c, 0:HGW], c == 0, c == DC - 1)
                ins.then_inc(hg_done, 1)
                if more:
                    xt_banks(i + 1, 1 - par)
                for f in range(2):
                    at_least(pe, out_set, 2 * i - 3 + f if not (isinstance(i, int) and i < 2) else 0)
                    cols = slice(512 * f, 512 * f + 512)
                    for c in range(DC):
                        three(bank[2 * par + f][:, :], xt_hi[:, par, c, :], xt_lo[:, par, c, :],
                              wb_hi[:, c, cols], wb_lo[:, c, cols], c == 0, False)
                    if f == 0:
                        pe.wait_ge(hw_set, i + 1)
                        at_least(pe, hwt_lo, i)
                        nc.tensor.transpose(bank[7][:, 0:P], hw[:, :], ident).then_inc(hwt_done, 1)
                pe.wait_ge(hwt_lo, i + 1)
                for f in range(2):
                    cols = slice(512 * f, 512 * f + 512)
                    three(bank[2 * par + f][:, :], hwt[:, 0, :], hwt[:, 1, :], bt_hi[:, cols], bt_lo[:, cols],
                          False, True).then_inc(ffn_done, 1)

            tile(0, 0, True)
            tile(1, 1, True)
            with pe.Fori(1, NT // 2 - 1) as j:
                tile(2 * j, 0, True)
                tile(2 * j + 1, 1, True)
            tile(NT - 2, 0, True)
            tile(NT - 1, 1, False)


def rope_tables():
    import numpy as np
    exponents = np.arange(0, DH, 2, dtype=np.float32)
    inv_freq = (np.float32(1.0) / np.float32(10000.0) ** (exponents / np.float32(DH))).astype(np.float32)
    phase = (np.arange(S, dtype=np.float32)[:, None] * inv_freq[None, :]).astype(np.float32).T
    cos = np.cos(phase).astype(np.float32) * np.float32(QS / WS)
    sin = np.sin(phase).astype(np.float32) * np.float32(QS / WS)
    return np.ascontiguousarray(np.concatenate([
        np.concatenate([cos, cos], 0), np.concatenate([sin, -sin], 0), np.eye(P, dtype=np.float32)], 1))


NAMES = ['x', 'ctx_4096', 'mask_1x1xSxS2_bk0', 'g_xattn', 'g_ffn', 'L0_xattn_Wq', 'L0_xattn_Wk', 'L0_xattn_Wv',
         'L0_xattn_Wo', 'L0_ffn_W_base', 'L0_ffn_b_base', 'L0_ffn_W_gate', 'L0_ffn_W_thr', 'L0_ffn_b_thr',
         'L0_ffn_A', 'L0_ffn_B']


def kernel(**inputs):
    import numpy as np
    import concourse.bacc as bacc
    from concourse.bass_utils import run_bass_kernel_spmd

    nc = bacc.Bacc("TRN2", target_bir_lowering=False, num_devices=1)
    arrays, args = {}, []

    def give(name, a):
        arrays[name] = a
        args.append(nc.dram_tensor(name, a.shape, mybir.dt.from_np(a.dtype), kind="ExternalInput").ap())

    for name in NAMES:
        give("in_" + name, np.ascontiguousarray(inputs[name]))
    give("tables", rope_tables())
    out = nc.dram_tensor("out_x", (NB, S, D), F32, kind="ExternalOutput").ap()
    build(nc, *args, out)
    r = run_bass_kernel_spmd(nc, [arrays], core_ids=[0])
    return r.results[0]["out_x"]
```

```python
import concourse.bass as bass
from concourse import mybir
from contextlib import ExitStack

F32 = mybir.dt.float32
F32R = mybir.dt.float32r
F16 = mybir.dt.float16
U8 = mybir.dt.uint8
ALU = mybir.AluOpType
ACT = mybir.ActivationFunctionType
AX = mybir.AxisListType.X

P = 128
NB, S, D = 8, 256, 1024
HQ, HK, DH = 32, 8, 128
GQ = HQ // HK
ROWS = NB * S
PAIR = 2 * S
NP = ROWS // PAIR
TP = PAIR // P
DC = D // P
E, R = 8, 16
NG = E + 1
HGW = E * R + NG
NT = ROWS // P
GROUPS = (2, 0, 1, 3)
EPS = 1e-5
ATTN_MULT = 0.08838834764831845
MAX_ATTN = 30.0

WS = 64.0
QS = 4.0
VS = 4.0
PS = 1024.0
OS = 4.0
HS = 16.0
BS = 8.0

PAIRS_PER_HALF = 2
NIT = 2 * HK
SPI = PAIRS_PER_HALF * GQ
NSTEP = NIT * SPI
FIRST_Q = 2 * TP - 1
FIRST_W1 = 3
FIRST_XT = 4
EARLY_W1 = 7
MASKS = 5
LAG = GQ


def at_least(eng, sem, value):
    if isinstance(value, int) and value <= 0:
        return
    eng.wait_ge(sem, value)


def build(nc, x, ctx, mask, g_xattn, g_ffn, wq, wk, wv, wo, w_base, b_base, w_gate, w_thr, b_thr, a_dn, b_up,
          tables, out):
    x_rows = x.rearrange("b s d -> (b s) d")
    ctx_rows = ctx.rearrange("b s d -> (b s) d")
    out_rows = out.rearrange("b s d -> (b s) d")
    mask_rows = mask.rearrange("a b t s -> (a b t) s").rearrange("(k p) s -> p k s", p=P)

    k_scr = nc.dram_tensor("k_scr", (HK, NP, P, 2 * PAIR), F16, kind="Internal").ap()
    v_scr = nc.dram_tensor("v_scr", (HK, NP, P, TP * 2 * DH), F16, kind="Internal").ap()
    xn_scr = nc.dram_tensor("xn_scr", (NP, P, 2 * DC * PAIR), F16, kind="Internal").ap()
    x1_scr = nc.dram_tensor("x1_scr", (ROWS, D), F32, kind="Internal").ap()

    with ExitStack() as whole:
        def sem(name):
            return whole.enter_context(nc.semaphore(name))

        def sb(stack, name, shape, dt):
            return stack.enter_context(nc.sbuf_tensor(name, shape, dt))

        bank = [whole.enter_context(nc.psum_tensor(f"bank{i}", [P, 512], F32)) for i in range(8)]

        tab = sb(whole, "tab", [P, 2 * S + P], F32)
        cos_k, sin_k, ident = tab[:, 0:S], tab[:, S:2 * S], tab[:, 2 * S:2 * S + P]
        cos_q = sb(whole, "cos_q", [P, S], F32)
        sin_q = sb(whole, "sin_q", [P, S], F32)
        mask_t = sb(whole, "mask_t", [P, 2 * S], F32)
        gates = sb(whole, "gates", [P, 8], F32)
        ones_r = sb(whole, "ones_r", [P, P], F32R)
        mhalf = sb(whole, "mhalf", [P, 1], F32)

        wst2 = sb(whole, "wst2", [P, 2, D], F32)
        wq_even = sb(whole, "wq_even", [P, 2, DC, GQ * DH], F16)

        ph1 = ExitStack()
        wk_hi = sb(ph1, "wk_hi", [P, DC, D], F16)
        wk_lo = sb(ph1, "wk_lo", [P, DC, D], F16)
        ctx_raw = sb(ph1, "ctx_raw", [P, TP, D], F32)
        x_raw = sb(ph1, "x_raw", [P, TP, D], F32)
        wv_hi = sb(ph1, "wv_hi", [P, DC, D], F16)
        wv_lo = sb(ph1, "wv_lo", [P, DC, D], F16)
        ct_hi = sb(ph1, "ct_hi", [P, DC, PAIR], F16)
        ct_lo = sb(ph1, "ct_lo", [P, DC, PAIR], F16)
        xst = sb(ph1, "xst", [P, 2, DC, PAIR], F16)
        wst1 = sb(ph1, "wst1", [P, 3, D], F32)
        wst1_s = [wst1[:, k, :] for k in range(3)] + [wst2[:, k, :] for k in range(2)]
        NST1 = len(wst1_s)
        kst = sb(ph1, "kst", [P, 2, 2, PAIR], F16)
        vst = sb(ph1, "vst", [P, HK, TP, 2, DH], F16)
        ka = sb(ph1, "ka", [P, 2, PAIR], F32)
        kb = sb(ph1, "kb", [P, PAIR], F32)
        stats = sb(ph1, "stats", [P, TP, 12], F32)
        mv = sb(ph1, "mv", [P, TP, 16], F32)
        mask_u8 = sb(ph1, "mask_u8", [P, 2, S], U8)
        mask_f = sb(ph1, "mask_f", [P, 2, S], F32)
        row_any = sb(ph1, "row_any", [P, 2, 2], F32)
        row_wide = sb(ph1, "row_wide", [P, 2, P], F32)
        ones_w = sb(ph1, "ones_w", [P, P], F32)
        ph1.close()

        ph2 = ExitStack()
        xn = sb(ph2, "xn", [P, PAIRS_PER_HALF, 2, DC, PAIR], F16)
        wo_even = sb(ph2, "wo_even", [P, 2, GQ, D], F16)
        kt = sb(ph2, "kt", [P, PAIRS_PER_HALF, 2, PAIR], F16)
        vt = sb(ph2, "vt", [P, PAIRS_PER_HALF, TP, 2, DH], F16)
        q_s = sb(ph2, "q_s", [P, 2, PAIR], F16)
        qa = sb(ph2, "qa", [P, PAIR], F32)
        qb = sb(ph2, "qb", [P, PAIR], F32)
        esum = sb(ph2, "esum", [P, PAIR], F32)
        y = sb(ph2, "y", [P, PAIRS_PER_HALF, TP, D], F32)
        e_even = sb(ph2, "e_even", [P, 2, 2, S], F32)
        w_s = sb(ph2, "w_s", [P, 2, 2, 2, S], F16)
        esum_r = sb(ph2, "esum_r", [P, 2, PAIR], F32R)
        den_t = sb(ph2, "den_t", [P, PAIR], F32)
        rden = sb(ph2, "rden", [P, PAIR], F32)
        wo_odd = sb(ph2, "wo_odd", [P, 2, GQ, D], F16)
        wq_odd = sb(ph2, "wq_odd", [P, 2, DC, GQ * DH], F16)
        o_s = sb(ph2, "o_s", [P, PAIRS_PER_HALF, GQ, 2, PAIR], F16)
        rden_t = sb(ph2, "rden_t", [P, PAIR // 32], F32)
        e_odd = sb(ph2, "e_odd", [P, 2, 2, S], F32)
        e_s = (e_even, e_odd)
        wq_s, wo_s = (wq_even, wq_odd), (wo_even, wo_odd)
        ph2.close()

        ph3 = ExitStack()
        wb_raw = sb(ph3, "wb_raw", [P, DC, D], F32)
        sb(ph3, "gap_wo_even", [P, 2, GQ, D], F16)
        bias_row = sb(ph3, "bias_row", [P, D], F32)
        b_raw = sb(ph3, "b_raw", [P, DC, E, R], F32)
        gsm = sb(ph3, "gsm", [P, 2, 64], F32)
        hw = sb(ph3, "hw", [P, E * R], F32)
        hwt = sb(ph3, "hwt", [P, 2, P], F16)
        stats3 = sb(ph3, "stats3", [P, 2, 12], F32)
        mv3 = sb(ph3, "mv3", [P, 2, 16], F32)
        thr_bias = sb(ph3, "thr_bias", [P, 8], F32)
        sb(ph3, "gap_small", [P, 1600], F32)
        NX = TP
        x1t = y[:, 0, :, :]
        sb(ph3, "gap_y", [P, PAIRS_PER_HALF, TP, D], F32)
        ag_hi = sb(ph3, "ag_hi", [P, DC, HGW + 1], F16)
        ag_lo = sb(ph3, "ag_lo", [P, DC, HGW + 1], F16)
        bt_hi = sb(ph3, "bt_hi", [P, D], F16)
        bt_lo = sb(ph3, "bt_lo", [P, D], F16)
        sb(ph3, "gap_e", [P, 1968], F32)
        out_t = sb(ph3, "out_t", [P, 2, D], F32)
        sb(ph3, "gap_wo_odd", [P, 2, D], F32)
        xn2 = sb(ph3, "xn2", [P, 2, D], F32)
        xt_hi = sb(ph3, "xt_hi", [P, 2, DC, P], F16)
        xt_lo = sb(ph3, "xt_lo", [P, 2, DC, P], F16)
        a_raw, gt_raw = wst2[:, 0, :], wst2[:, 1, :]
        wb_hi = wq_even[:, :, :, :].rearrange("p a c n -> p (a c n)").rearrange("p (c n) -> p c n", c=DC)
        wb_lo = wo_even[:, :, :, :].rearrange("p a h n -> p (a h n)").rearrange("p (c n) -> p c n", c=DC)
        ph3.close()

        ident_in = sem("ident_in")
        tab_in = sem("tab_in")
        mask_in = sem("mask_in")
        g_in = sem("g_in")
        setup_dve = sem("setup_dve")
        ones_set = sem("ones_set")
        mask_tr = sem("mask_tr")
        tanh_g = sem("tanh_g")
        ctx_in = [sem(f"ctx_in{t}") for t in range(TP)]
        x_in = [sem(f"x_in{t}") for t in range(TP)]
        wst1_in = [sem(f"wst1_in{t}") for t in range(NST1)]
        wk_hi_set = sem("wk_hi_set")
        wk_lo_set = sem("wk_lo_set")
        wv_hi_set = sem("wv_hi_set")
        wv_lo_set = sem("wv_lo_set")
        tr_done = sem("tr_done")
        tr_hi = sem("tr_hi")
        tr_lo = sem("tr_lo")
        k_done = sem("k_done")
        v_done = sem("v_done")
        kr_a = sem("kr_a")
        kr_read = sem("kr_read")
        k_roped = sem("k_roped")
        k_hi = sem("k_hi")
        k_lo = sem("k_lo")
        v_hi = sem("v_hi")
        v_lo = sem("v_lo")
        ln1_stat = sem("ln1_stat")
        ln1_rstd = sem("ln1_rstd")
        ln1 = sem("ln1")
        mhalf_set = sem("mhalf_set")
        k_out = [sem("k_out0"), sem("k_out1")]
        v_out = sem("v_out")
        xn_out = sem("xn_out")

        wst2_in = [sem("wst2_in0"), sem("wst2_in1")]
        w_hi = sem("w_hi")
        w_lo = sem("w_lo")
        kv_in = [sem("kv_in0"), sem("kv_in1")]
        xn_in = [sem("xn_in0"), sem("xn_in1")]
        y_in = [sem("y_in0"), sem("y_in1")]
        y_out = [sem("y_out0"), sem("y_out1")]
        q_done = sem("q_done")
        q_a = sem("q_a")
        q_read = sem("q_read")
        q_roped = sem("q_roped")
        q_hi = sem("q_hi")
        q_lo = sem("q_lo")
        logits_done = sem("logits_done")
        tanh_done = sem("tanh_done")
        exp_done = sem("exp_done")
        masked = sem("masked")
        esum_done = sem("esum_done")
        esum_hi = sem("esum_hi")
        esum_lo = sem("esum_lo")
        den_done = sem("den_done")
        den_read = sem("den_read")
        rden_t_done = sem("rden_t_done")
        rden_done = sem("rden_done")
        weighted = sem("weighted")
        p_hi = sem("p_hi")
        p_lo = sem("p_lo")
        av_done = sem("av_done")
        o_hi = sem("o_hi")
        o_lo = sem("o_lo")
        y_done = [sem("y_done0"), sem("y_done1")]
        y_added = [sem("y_added0"), sem("y_added1")]

        wb_in = [sem("wb_in0"), sem("wb_in1")]
        bup_in = sem("bup_in")
        g3_in = sem("g3_in")
        b3_in = sem("b3_in")
        x1_in = [sem(f"x1_in{t}") for t in range(NX)]
        tr3_done = sem("tr3_done")
        tr3_hi = sem("tr3_hi")
        tr3_lo = sem("tr3_lo")
        bias_set = sem("bias_set")
        ln3_stat = sem("ln3_stat")
        ln3_rstd = sem("ln3_rstd")
        ln3 = sem("ln3")
        x1_biased = sem("x1_biased")
        hg_done = sem("hg_done")
        gmax = sem("gmax")
        gexp = sem("gexp")
        gate_step = sem("gate_step")
        wsum_step = sem("wsum_step")
        hw_set = sem("hw_set")
        hwt_done = sem("hwt_done")
        hwt_hi = sem("hwt_hi")
        hwt_lo = sem("hwt_lo")
        ffn_done = sem("ffn_done")
        out_set = sem("out_set")
        out_out = [sem("out_out0"), sem("out_out1")]

        NTR1 = 2 * DC * NP

        TR_BANKS = (0, 1, 6, 7)

        def transposes(more):
            order = []
            for v in range(2 * TP):
                if more and v >= 2:
                    order.append((v, "ctx", v - 2))
                beside = range(3 * (v - 5), min(3 * (v - 4), DC)) if more else range(2 * v, min(2 * v + 2, DC))
                order += [(v, "x", m) for m in beside if m >= 0]
            if more:
                order += [(2 * TP, "ctx", 6), (2 * TP, "ctx", 7)]
            return list(enumerate(order))

        def first_pieces(g):
            ends = (EARLY_W1, 8, 10, 11, 12, 14, 15, 16, 16)
            return range(ends[g], ends[g + 1])

        def after_bank(q, more, kind, which):
            return DC + 16 * q + 1 + [k for k, (_, a, b) in transposes(more) if (a, b) == (kind, which)][0]

        NTR3W = 2 * DC + DC + 2

        W_BANKS = (2, 3, 0, 1)

        def weight_banks():
            n = 0
            for f in range(2):
                for c in range(DC):
                    yield (n, wb_hi[:, c, f * 512:(f + 1) * 512], wb_lo[:, c, f * 512:(f + 1) * 512],
                           bank[W_BANKS[n % 4]][:, :], WS)
                    n += 1
            for c in range(DC):
                yield n, ag_hi[:, c, 0:HGW], ag_lo[:, c, 0:HGW], bank[W_BANKS[n % 4]][:, 0:HGW], WS
                n += 1
            for f in range(2):
                yield (n, bt_hi[:, f * 512:(f + 1) * 512], bt_lo[:, f * 512:(f + 1) * 512],
                       bank[W_BANKS[n % 4]][:, :], BS)
                n += 1

        def beside(k):
            return range(4 * k, min(4 * k + 4, NTR3W))

        block = whole.enter_context(nc.Block())

        @block.sync
        def _(sp):
            def load_w(n):
                f, j = divmod(n % 8, 4)
                if n >= NST1:
                    if n - NST1 < 8:
                        sp.wait_ge(wk_lo_set, n - NST1 + 1)
                    else:
                        sp.wait_ge(wv_lo_set, n - NST1 - 8 + 1)
                if n < 8:
                    src, c = wk[:, n * DH:(n + 1) * DH], DC
                else:
                    src, c = wv[2 * j * P:(2 * j + 2) * P, f * 512:(f + 1) * 512], 2
                sp.dma_start(wst1_s[n % NST1].rearrange("p (c n) -> p c n", c=c),
                             src.rearrange("(c p) n -> p c n", p=P)).then_inc(wst1_in[n % NST1], 16)

            sp.dma_start(ident, tables[:, 2 * S:2 * S + P]).then_inc(ident_in, 16)

            def load_ctx(tiles):
                for t in tiles:
                    sp.dma_start(ctx_raw[:, t, :], ctx_rows[t * P:(t + 1) * P, :]).then_inc(ctx_in[t], 16)

            load_ctx(range(2))
            load_w(0)
            load_ctx(range(2, TP))
            for n in range(1, NST1):
                load_w(n)
            sp.dma_start(tab[:, 0:2 * S], tables[:, 0:2 * S]).then_inc(tab_in, 16)
            sp.dma_start(mask_u8[:, :, :], mask_rows).then_inc(mask_in, 16)
            sp.dma_start(gates[:, 0:1], g_xattn.partition_broadcast(P)).then_inc(g_in, 16)
            sp.dma_start(gates[:, 1:2], g_ffn.partition_broadcast(P)).then_inc(g_in, 16)

            for n in range(NST1, EARLY_W1 + NST1):
                load_w(n)

            def store_k(q, g):
                sp.wait_ge(k_hi, q * HK + g + 1)
                sp.wait_ge(k_lo, q * HK + g + 1)
                sp.dma_start(k_scr[g, q, :, :], kst[:, g % 2, :, :].rearrange("p a t -> p (a t)")
                             ).then_inc(k_out[g % 2], 16)

            def store_xn(q, more):
                sp.wait_ge(tr_lo, after_bank(q, more, "x", 7))
                sp.dma_start(xn_scr[q, :, :], xst[:, :, :, :].rearrange("p a c t -> p (a c t)")).then_inc(xn_out, 16)

            def store_v(q):
                sp.wait_ge(v_lo, (q + 1) * 2 * TP)
                sp.dma_start(v_scr[:, q, :, :].rearrange("g p n -> p g n"),
                             vst[:, :, :, :, :].rearrange("p g t a d -> p g (t a d)")).then_inc(v_out, 16)

            def load_first(g):
                for n in first_pieces(g):
                    if n + NST1 < 16:
                        load_w(n + NST1)
                if g in (2, 3, 4, 5):
                    t = g - 2
                    sp.dma_start(x_raw[:, t, :], x_rows[t * P:(t + 1) * P, :]).then_inc(x_in[t], 16)
                if g == 6:
                    sp.wait_ge(tr_done, DC)
                    for r in range(TP):
                        sp.dma_start(ctx_raw[:, r, :], ctx_rows[PAIR + r * P:PAIR + (r + 1) * P, :]
                                     ).then_inc(ctx_in[r], 16)

            def pair_io(q, more_ctx):
                for g in range(HK):
                    store_k(q, g)
                    if isinstance(q, int) and q == 0:
                        load_first(g)
                for t in range(TP):
                    if t == TP - 1:
                        for r in range(TP):
                            sp.wait_ge(tr_done, after_bank(q, True, "x", 7))
                            sp.dma_start(x_raw[:, r, :], x_rows[bass.ds(q * PAIR + PAIR + r * P, P), :]
                                         ).then_inc(x_in[r], 16)
                    if more_ctx:
                        sp.wait_ge(tr_done, after_bank(q, True, "ctx", 2 * t + 1))
                        sp.dma_start(ctx_raw[:, t, :], ctx_rows[bass.ds(q * PAIR + 2 * PAIR + t * P, P), :]
                                     ).then_inc(ctx_in[t], 16)
                store_xn(q, True)
                store_v(q)

            def load_piece(j, n, g):
                at_least(sp, w_lo, n - 1)
                if j < 4:
                    src = wq[2 * j * P:(2 * j + 2) * P, bass.ds(g * GQ * DH, GQ * DH)].rearrange(
                        "(c p) n -> p c n", p=P)
                    dst = wst2[:, j % 2, :].rearrange("p (c n) -> p c n", c=2)
                else:
                    src = wo[bass.ds(g * GQ * DH + (j - 4) * DH, P), :]
                    dst = wst2[:, j % 2, :]
                sp.dma_start(dst, src).then_inc(wst2_in[j % 2], 16)

            pair_io(0, True)
            with sp.Fori(1, NP - 2) as q:
                pair_io(q, True)
            pair_io(NP - 2, False)
            for g in range(HK):
                if g >= HK - 2:
                    sp.wait_ge(wv_lo_set, 8)
                    load_piece(g - HK + 2, g - HK + 2, 0)
                store_k(NP - 1, g)

            sp.wait_ge(v_out, 16 * (NP - 1))

            def store_v_tile(t):
                sp.wait_ge(v_lo, (NP - 1) * 2 * TP + 2 * (t + 1))
                sp.dma_start(v_scr[:, NP - 1, :, t * 2 * DH:(t + 1) * 2 * DH].rearrange("g p n -> p g n"),
                             vst[:, :, t, :, :].rearrange("p g a d -> p g (a d)")).then_inc(v_out, 16)


            def load_kv(b, g, half):
                q = half * PAIRS_PER_HALF + b
                sp.dma_start(kt[:, b, :, :].rearrange("p a t -> p (a t)"), k_scr[g, q, :, :]).then_inc(kv_in[b], 16)
                sp.dma_start(vt[:, b, :, :, :].rearrange("p t a d -> p (t a d)"), v_scr[g, q, :, :]
                             ).then_inc(kv_in[b], 16)

            def load_xn(b, half):
                sp.dma_start(xn[:, b, :, :, :].rearrange("p a c t -> p (a c t)"),
                             xn_scr[half * PAIRS_PER_HALF + b, :, :]).then_inc(xn_in[b], 16)

            def y_rows(dram, b, half):
                r0 = (half * PAIRS_PER_HALF + b) * PAIR
                return dram[r0:r0 + PAIR, :].rearrange("(t p) d -> p t d", p=P)

            def load_y(b, half):
                sp.dma_start(y[:, b, :, :], y_rows(x_rows, b, half)).then_inc(y_in[b], 16)

            def store_y(b, half):
                sp.dma_start(y_rows(x1_scr, b, half), y[:, b, :, :]).then_inc(y_out[b], 16)

            sp.wait_ge(k_done, HK * NP)
            sp.wait_ge(xn_out, 32)
            for b in range(PAIRS_PER_HALF):
                load_xn(b, 0)
                load_piece(2 + b, 2 + b, 0)
            store_v_tile(0)
            load_piece(4, 4, 0)
            store_xn(NP - 1, False)
            sp.wait_ge(tr_done, NTR1)
            for k in range(2):
                sp.wait_ge(k_out[k], 16 * HK * NP // 2)
            load_kv(0, 0, 0)
            store_v_tile(1)
            load_piece(5, 5, 0)
            load_kv(1, 0, 0)
            load_piece(6, 6, 0)
            store_v_tile(2)
            for n in range(7, 9):
                load_piece(n % 8, n, n // 8)
            store_v_tile(3)
            load_piece(1, 9, 1)
            sp.wait_ge(v_done, 2 * TP * NP)
            load_y(0, 0)

            def loads(it, half, g, turn=False, last=False):
                for u in range(SPI):
                    if not last and not (isinstance(it, int) and it == 0 and u < 2):
                        load_piece(u, 8 * it + 8 + u, (g + 1) if not turn else 0)
                    if isinstance(it, int) and it == 0 and u == 4:
                        load_y(1, 0)
                    if u == 1 and not (isinstance(it, int) and it == 0):
                        sp.wait_ge(av_done, 8 * it)
                        load_kv(1, g, half)
                    if u == 5 and not last:
                        sp.wait_ge(av_done, 8 * it + 4)
                        if turn:
                            sp.wait_ge(xn_out, 16 * NP)
                            sp.wait_ge(v_out, 16 * (NP - 1 + TP))
                            load_kv(0, 0, 1)
                        else:
                            load_kv(0, g + 1, half)
                    if turn and u == 5:
                        sp.wait_ge(q_done, 8 * it + 4)
                        load_xn(0, 1)
                    if isinstance(it, int) and it == HK:
                        if u == 1:
                            sp.wait_ge(q_done, 8 * it)
                            load_xn(1, 1)
                            for k in range(2):
                                sp.wait_ge(y_added[k], 8 * it - LAG)
                            store_y(0, 0)
                        if u == 2:
                            sp.wait_ge(y_out[0], 16)
                            load_y(0, 1)
                        if u == 5:
                            for k in range(2):
                                sp.wait_ge(y_added[k], 8 * it)
                            store_y(1, 0)
                        if u == 6:
                            sp.wait_ge(y_out[1], 16)
                            load_y(1, 1)

            loads(0, 0, 0)
            with sp.Fori(1, HK - 1) as it:
                loads(it, 0, it)
            loads(HK - 1, 0, HK - 1, turn=True)
            loads(HK, 1, 0)
            with sp.Fori(HK + 1, NIT - 1) as it:
                loads(it, 1, it - HK)
            loads(NIT - 1, 1, HK - 1, last=True)
            def load_base(f):
                for o in range(4 * f, 4 * f + 4):
                    sp.dma_start(wb_raw[:, o, :], w_base[o * P:(o + 1) * P, :]).then_inc(wb_in[f], 16)

            sp.wait_ge(w_lo, 8 * NIT)
            sp.wait_ge(q_done, NSTEP - GQ)
            load_base(0)
            sp.dma_start(a_raw, a_dn.rearrange("e r d -> (e r) d")).then_inc(g3_in, 16)
            sp.dma_start(gt_raw[0:E, :], w_gate).then_inc(g3_in, 16)
            sp.dma_start(gt_raw[E:NG, :], w_thr).then_inc(g3_in, 16)
            sp.wait_ge(q_done, NSTEP)
            load_base(1)
            sp.wait_ge(av_done, NSTEP)
            b_by_o = b_up.rearrange("e (k p) r -> k p e r", p=P)
            for o in range(DC):
                sp.dma_start(b_raw[:, o, :, :], b_by_o[o, :, :, :]).then_inc(bup_in, 16)
            sp.dma_start(bias_row[:, :], b_base.partition_broadcast(P)).then_inc(b3_in, 16)
            sp.dma_start(thr_bias[:, 0:1], b_thr.partition_broadcast(P)).then_inc(b3_in, 16)
            for k in range(2):
                sp.wait_ge(y_added[k], NSTEP)
            store_y(1, 1)

            def rows_io(i, u, row, next_row):
                sp.wait_ge(out_set, 2 * i + 2)
                if next_row is not None:
                    sp.dma_start(x1t[:, u, :], x1_scr[next_row * P:(next_row + 1) * P, :]).then_inc(x1_in[u], 16)
                sp.dma_start(out_rows[row * P:(row + 1) * P, :], out_t[:, u % 2, :]).then_inc(out_out[u % 2], 16)

            for k, group in enumerate(GROUPS):
                if k == len(GROUPS) - 2:
                    sp.wait_ge(y_out[1], 32)
                for u in range(NX):
                    rows_io(k * NX + u, u, group * NX + u,
                            GROUPS[k + 1] * NX + u if k + 1 < len(GROUPS) else None)
            for k in range(2):
                sp.wait_ge(out_out[k], 16 * NT // 2)

        @block.gpsimd
        def _(pool):
            nc.gpsimd.memset(mhalf[:, :], -0.5).then_inc(mhalf_set, 1)
            pool.wait_ge(mhalf_set, 1)

            def inverse_std(stat, rstd, n, m):
                pool.wait_ge(stat, 8 * n + 8)
                nc.gpsimd.tensor_tensor(m[:, 3:4], m[:, 2:3], mhalf[:, :], ALU.pow).then_inc(rstd, 1)

            def pair(q, more):
                for g in range(HK):
                    if not more and g % 2 == 0:
                        inverse_std(ln1_stat, ln1_rstd, TP * q + g // 2, mv[:, g // 2, :])
                    pool.wait_ge(k_hi, HK * q + g + 1)
                    at_least(pool, k_out[g % 2], 16 * (4 * q + g // 2))
                    nc.gpsimd.tensor_tensor(kst[:, g % 2, 1, :], ka[:, g % 2, :], kst[:, g % 2, 0, :], ALU.subtract
                                            ).then_inc(k_lo, 1)
                if more:
                    for t in range(TP):
                        inverse_std(ln1_stat, ln1_rstd, TP * q + t, mv[:, t, :])

            pair(0, True)
            with pool.Fori(1, NP - 1) as q:
                pair(q, True)
            pair(NP - 1, False)

            pool.wait_ge(setup_dve, 11)

            def step(s, par):
                for b in range(2):
                    pool.wait_ge(exp_done, 2 * s + b + 1)
                    e_b = e_s[par][:, b, :, :].rearrange("p k t -> p (k t)")
                    nc.gpsimd.tensor_tensor(e_b, e_b, mask_t[:, :], ALU.mult).then_inc(masked, 1)
                    pool.wait_ge(masked, 2 * s + b + 1)
                    at_least(pool, esum_lo, s)
                    nc.gpsimd.tensor_tensor(esum[:, b * S:(b + 1) * S], e_s[par][:, b, 0, :], e_s[par][:, b, 1, :],
                                            ALU.add).then_inc(esum_done, 1)
                pool.wait_ge(esum_hi, s + 1)
                at_least(pool, den_done, s)
                nc.gpsimd.tensor_tensor(esum_r[:, 1, :], esum[:, :], esum_r[:, 0, :].bitcast(F32), ALU.subtract
                                        ).then_inc(esum_lo, 1)

            step(0, 0)
            step(1, 1)
            with pool.Fori(1, NSTEP // 2) as j:
                step(2 * j, 0)
                step(2 * j + 1, 1)

            for i in range(2):
                inverse_std(ln3_stat, ln3_rstd, i, mv3[:, i, :])
            pool.wait_ge(b3_in, 32)
            pool.wait_ge(bias_set, 2)

            def biased(i, u):
                pool.wait_ge(ln3, i + 1)
                nc.gpsimd.tensor_tensor(x1t[:, u, :], x1t[:, u, :], bias_row[:, :], ALU.add).then_inc(x1_biased, 1)

            with pool.Fori(0, NT // NX - 1) as j:
                for u in range(NX):
                    biased(j * NX + u, u)
                    inverse_std(ln3_stat, ln3_rstd, j * NX + u + 2, mv3[:, u % 2, :])
            for u in range(NX):
                biased(NT - NX + u, u)
                if u < NX - 2:
                    inverse_std(ln3_stat, ln3_rstd, NT - NX + u + 2, mv3[:, u % 2, :])

        @block.scalar
        def _(act):
            def bank_hi(first, n, dst):
                act.wait_ge(tr_done, first + n + 1)
                src = bank[TR_BANKS[n % 4]][:, :]
                if len(dst.shape) == 3:
                    src = src.rearrange("p (a b) -> p a b", a=dst.shape[1])
                nc.scalar.activation(dst, src, ACT.Copy).then_inc(tr_hi, 1)

            def split_w1(n):
                f, j = divmod(n % 8, 4)
                act.wait_ge(wst1_in[n % NST1], 16 * (n // NST1 + 1))
                if n < 8:
                    dst, c, done = wk_hi[:, :, n * DH:(n + 1) * DH], DC, wk_hi_set
                else:
                    dst, c, done = wv_hi[:, 2 * j:2 * j + 2, f * 512:(f + 1) * 512], 2, wv_hi_set
                nc.scalar.activation(dst, wst1_s[n % NST1].rearrange("p (c n) -> p c n", c=c),
                                     ACT.Copy, scale=WS).then_inc(done, 1)

            for m in range(DC):
                t, f = divmod(m, 2)
                bank_hi(0, m, ct_hi[:, 4 * f:4 * f + 4, t * P:(t + 1) * P])
                if m == FIRST_W1:
                    split_w1(0)
            for n in range(1, EARLY_W1):
                split_w1(n)
            act.wait_ge(g_in, 32)
            nc.scalar.activation(gates[:, 2:4], gates[:, 0:2], ACT.Tanh).then_inc(tanh_g, 1)

            def split_piece(n, j, par, it):
                act.wait_ge(wst2_in[j % 2], 16 * (n // 2 + 1))
                if j < 4:
                    at_least(act, q_done, 8 * it if not isinstance(it, int) or it > 0 else 0)
                    dst = wq_s[par][:, 0, 2 * j:2 * j + 2, :].rearrange("p c n -> p (c n)")
                else:
                    at_least(act, y_done[1], 8 * it if not isinstance(it, int) or it > 0 else 0)
                    dst = wo_s[par][:, 0, j - 4, :]
                nc.scalar.activation(dst, wst2[:, j % 2, :], ACT.Copy, scale=WS).then_inc(w_hi, 1)

            def q_high(n):
                act.wait_ge(q_roped, n + 1)
                at_least(act, logits_done, 2 * n)
                nc.scalar.activation(q_s[:, 0, :], qa[:, :], ACT.Copy).then_inc(q_hi, 1)

            def pair(q, more):
                for g in range(HK):
                    act.wait_ge(k_roped, HK * q + g + 1)
                    at_least(act, k_out[g % 2], 16 * (4 * q + g // 2))
                    nc.scalar.activation(kst[:, g % 2, 0, :], ka[:, g % 2, :], ACT.Copy).then_inc(k_hi, 1)
                    if isinstance(q, int) and q == 0:
                        for n in first_pieces(g):
                            split_w1(n)
                for v in range(2 * TP + 1):
                    if not more and v == FIRST_Q:
                        q_high(0)
                    for k, (slot, kind, m) in transposes(more):
                        if slot != v:
                            continue
                        t, f = divmod(m, 2)
                        if kind == "ctx":
                            act.wait_ge(v_done, 2 * TP * q + 2 * (t + 1))
                            bank_hi(DC + 16 * q, k, ct_hi[:, 4 * f:4 * f + 4, t * P:(t + 1) * P])
                        else:
                            at_least(act, xn_out, 16 * q)
                            bank_hi(DC + 16 * q, k, xst[:, 0, m, :])
                    if v == 2 * TP:
                        continue
                    if not more:
                        split_piece(v, v, 0, 0)
                    t, f = divmod(v, 2)
                    act.wait_ge(v_done, 2 * TP * q + v + 1)
                    at_least(act, v_out, 16 * q)
                    nc.scalar.activation(vst[:, 4 * f:4 * f + 4, t, 0, :],
                                         bank[4 + v % 2][:, :].rearrange("p (g d) -> p g d", g=4),
                                         ACT.Copy, scale=VS / WS).then_inc(v_hi, 1)

            pair(0, True)
            with act.Fori(1, NP - 1) as q:
                pair(q, True)
            pair(NP - 1, False)

            def o_high(p, pb, ph):
                act.wait_ge(av_done, p + 1)
                at_least(act, y_done[1], p + 1 - LAG)
                nc.scalar.activation(o_s[:, pb, ph, 0, :], bank[5][:, :], ACT.Copy, scale=OS / (PS * VS)
                                     ).then_inc(o_hi, 1)

            act.wait_ge(wv_lo_set, 8)
            for k in range(2):
                act.wait_ge(k_out[k], 16 * HK * NP // 2)

            def bank3_hi(n, dst, src, scale=1.0):
                act.wait_ge(tr3_done, n + 1)
                nc.scalar.activation(dst, src, ACT.Copy, scale=scale).then_inc(tr3_hi, 1)

            banks = list(weight_banks())

            def banks_beside(k):
                for i in beside(k):
                    n, dst, _, src, scale = banks[i]
                    bank3_hi(n, dst, src, scale)

            def steps(it, par, first=False, last=False):
                for u in range(SPI):
                    s = SPI * it + u
                    for b in range(2):
                        act.wait_ge(logits_done, 2 * s + b + 1)
                        at_least(act, p_lo, 2 * s - 3 + b if not (first and u < 2) else 0)
                        e_b = e_s[u % 2][:, b, :, :].rearrange("p k t -> p (k t)")
                        nc.scalar.activation(e_b, bank[b][:, :], ACT.Tanh,
                                             scale=ATTN_MULT / (MAX_ATTN * QS * QS)).then_inc(tanh_done, 1)
                        act.wait_ge(tanh_done, 2 * s + b + 1)
                        nc.scalar.activation(e_b, e_b, ACT.Exp, scale=MAX_ATTN).then_inc(exp_done, 1)
                    if first and u == 1:
                        act.wait_ge(v_out, 16 * (NP - 1 + TP))
                    lagged = not (first and u < GQ)
                    if lagged:
                        o_high(s - 1, ((u - 1) % SPI) // GQ, (u - 1) % GQ)
                    act.wait_ge(esum_done, 2 * s + 2)
                    at_least(act, den_done, s)
                    nc.scalar.activation(esum_r[:, 0, :], esum[:, :], ACT.Copy).then_inc(esum_hi, 1)
                    if not lagged and u > 0:
                        o_high(s - 1, 0, u - 1)
                    if not (last and u == SPI - 1):
                        q_high(s + 1)
                    else:
                        act.wait_ge(q_done, NSTEP)
                        banks_beside(0)
                    if first and u == GQ:
                        act.wait_ge(xn_out, 16 * NP)
                    if not last:
                        split_piece(8 * it + 8 + u, u, 1 - par, it)
                    for b in range(2):
                        act.wait_ge(weighted, 2 * s + b + 1)
                        at_least(act, av_done, s)
                        nc.scalar.activation(w_s[:, 0, b, :, :], e_s[u % 2][:, b, :, :], ACT.Copy).then_inc(p_hi, 1)

            steps(0, 0, first=True)
            with act.Fori(0, NIT // 2 - 1) as j:
                steps(2 * j + 1, 1)
                steps(2 * j + 2, 0)
            steps(NIT - 1, 1, last=True)
            banks_beside(1)
            o_high(NSTEP - 1, PAIRS_PER_HALF - 1, GQ - 1)

            banks_beside(2)

            def xt_high(i, par):
                for f in range(2):
                    at_least(act, hg_done, i - 1)
                    at_least(act, ffn_done, 2 * i - 2)
                    bank3_hi(NTR3W + 2 * i + f, xt_hi[:, par, 4 * f:4 * f + 4, :],
                             bank[4 + f][:, :].rearrange("p (c t) -> p c t", c=4))

            for k in range(3, 3 + 2 * TP):
                banks_beside(k)
            xt_high(0, 0)

            def tile(i, par, more):
                if more:
                    xt_high(i + 1, 1 - par)
                act.wait_ge(gmax, i + 1)
                nc.scalar.activation(gsm[:, par, 0:E], bank[6][:, E * R:E * R + E], ACT.Exp,
                                     bias=gsm[:, par, 9:10], scale=1.0 / WS).then_inc(gexp, 1)
                nc.scalar.activation(gsm[:, par, 10:11], bank[6][:, E * R + E:HGW], ACT.Tanh,
                                     bias=thr_bias[:, 1:2], scale=0.5 / WS).then_inc(gexp, 1)
                act.wait_ge(hwt_done, i + 1)
                at_least(act, ffn_done, 2 * i)
                nc.scalar.activation(hwt[:, 0, :], bank[7][:, 0:P], ACT.Copy).then_inc(hwt_hi, 1)

            tile(0, 0, True)
            tile(1, 1, True)
            with act.Fori(1, NT // 2 - 1) as j:
                tile(2 * j, 0, True)
                tile(2 * j + 1, 1, True)
            tile(NT - 2, 0, True)
            tile(NT - 1, 1, False)

        @block.vector
        def _(dve):
            setup = [0]

            def link(ins):
                setup[0] += 1
                ins.then_inc(setup_dve, 1)
                dve.wait_ge(setup_dve, setup[0])

            link(nc.vector.memset(ones_w[:, :], 1.0))
            nc.vector.tensor_scalar(ones_r[:, :], ones_w[:, :], 1.0 / PS, None, ALU.mult).then_inc(ones_set, 1)

            def bank_lo(first, n, dst, hi):
                dve.wait_ge(tr_hi, first + n + 1)
                src = bank[TR_BANKS[n % 4]][:, :]
                if len(dst.shape) == 3:
                    src = src.rearrange("p (a b) -> p a b", a=dst.shape[1])
                nc.vector.tensor_tensor(dst, src, hi, ALU.subtract).then_inc(tr_lo, 1)

            def w1_low(n):
                if n < 8:
                    cols, c = (slice(None), slice(None), slice(n * DH, (n + 1) * DH)), DC
                    hi, lo, hi_set, lo_set = wk_hi, wk_lo, wk_hi_set, wk_lo_set
                else:
                    f, j = divmod(n - 8, 4)
                    cols, c = (slice(None), slice(2 * j, 2 * j + 2), slice(f * 512, (f + 1) * 512)), 2
                    hi, lo, hi_set, lo_set = wv_hi, wv_lo, wv_hi_set, wv_lo_set
                dve.wait_ge(hi_set, n % 8 + 1)
                nc.vector.scalar_tensor_tensor(lo[cols], wst1_s[n % NST1].rearrange("p (c n) -> p c n", c=c),
                                               WS, hi[cols], ALU.mult, ALU.subtract).then_inc(lo_set, 1)

            for m in range(DC):
                t, f = divmod(m, 2)
                cols = (slice(None), slice(4 * f, 4 * f + 4), slice(t * P, (t + 1) * P))
                bank_lo(0, m, ct_lo[cols], ct_hi[cols])
                if m == FIRST_W1:
                    w1_low(0)
            for n in range(1, EARLY_W1):
                w1_low(n)

            def split_piece(n, j, par):
                dve.wait_ge(w_hi, n + 1)
                if j < 4:
                    hi, lo = (wq_s[par][:, k, 2 * j:2 * j + 2, :].rearrange("p c n -> p (c n)") for k in range(2))
                else:
                    hi, lo = (wo_s[par][:, k, j - 4, :] for k in range(2))
                nc.vector.scalar_tensor_tensor(lo, wst2[:, j % 2, :], WS, hi, ALU.mult, ALU.subtract
                                               ).then_inc(w_lo, 1)

            def mask_rows_kept():
                dve.wait_ge(mask_in, 16)
                link(nc.vector.tensor_copy(mask_f[:, :, :], mask_u8[:, :, :]))
                for k in range(2):
                    link(nc.vector.tensor_reduce(row_any[:, k, 0:1], mask_f[:, k, :], AX, ALU.max))
                    link(nc.vector.tensor_scalar(row_any[:, k, 1:2], row_any[:, k, 0:1], -1.0, 1.0, ALU.mult, ALU.add))
                    link(nc.vector.tensor_scalar(mask_f[:, k, :], mask_f[:, k, :], row_any[:, k, 1:2], None, ALU.max))
                    link(nc.vector.tensor_scalar(row_wide[:, k, :], ones_w[:, :], row_any[:, k, 0:1], None, ALU.mult))

            def masks_and_gates():
                dve.wait_ge(mask_tr, 1)
                link(nc.vector.tensor_copy(mask_t[:, :], bank[2][:, :]))
                dve.wait_ge(mask_tr, 2)
                link(nc.vector.tensor_tensor(cos_q[:, :], bank[3][:, 0:S], cos_k, ALU.mult))
                link(nc.vector.tensor_tensor(sin_q[:, :], bank[3][:, 0:S], sin_k, ALU.mult))
                dve.wait_ge(tanh_g, 1)
                link(nc.vector.tensor_scalar(gates[:, 4:5], gates[:, 2:3], 1.0 / (OS * WS), None, ALU.mult))
                link(nc.vector.tensor_scalar(gates[:, 5:6], gates[:, 3:4], 1.0 / WS, None, ALU.mult))

            dve.wait_ge(tab_in, 16)

            def statistics(stat, n, src, st, m):
                for k in range(2):
                    i = nc.vector.bn_stats(st[:, 6 * k:6 * k + 6], src[:, 512 * k:512 * k + 512])
                i.then_inc(stat, 1)
                groups = st.rearrange("p (g k) -> p g k", k=3)
                dve.wait_ge(stat, 8 * n + 1)
                nc.vector.tensor_reduce(m[:, 1:2], groups[:, :, 1], AX, ALU.add).then_inc(stat, 1)
                dve.wait_ge(stat, 8 * n + 2)
                nc.vector.tensor_scalar(m[:, 0:1], m[:, 1:2], 0.25, None, ALU.mult).then_inc(stat, 1)
                dve.wait_ge(stat, 8 * n + 3)
                nc.vector.tensor_scalar(m[:, 4:8], groups[:, :, 1], m[:, 0:1], None, ALU.subtract).then_inc(stat, 1)
                dve.wait_ge(stat, 8 * n + 4)
                nc.vector.scalar_tensor_tensor(m[:, 8:12], m[:, 4:8], D / 4.0, m[:, 4:8], ALU.mult, ALU.mult
                                               ).then_inc(stat, 1)
                dve.wait_ge(stat, 8 * n + 5)
                nc.vector.tensor_tensor(m[:, 12:16], m[:, 8:12], groups[:, :, 2], ALU.add).then_inc(stat, 1)
                dve.wait_ge(stat, 8 * n + 6)
                nc.vector.tensor_reduce(m[:, 1:2], m[:, 12:16], AX, ALU.add).then_inc(stat, 1)
                dve.wait_ge(stat, 8 * n + 7)
                nc.vector.tensor_scalar(m[:, 2:3], m[:, 1:2], 1.0 / D, EPS, ALU.mult, ALU.add).then_inc(stat, 1)

            def normalise(rstd, done, n, src, dst, m):
                dve.wait_ge(rstd, n + 1)
                nc.vector.tensor_scalar(dst, src, m[:, 0:1], m[:, 3:4], ALU.subtract, ALU.mult).then_inc(done, 1)

            def x_statistics(q, t):
                dve.wait_ge(x_in[t], 16 * (q + 1))
                statistics(ln1_stat, TP * q + t, x_raw[:, t, :], stats[:, t, :], mv[:, t, :])

            def x_normalise(q, t):
                normalise(ln1_rstd, ln1, TP * q + t, x_raw[:, t, :], x_raw[:, t, :], mv[:, t, :])

            def rope(src, ra, rb, cos, sin, a_set, b_set, summed, n):
                two = "p (b t) -> p b t"
                wide = [P, 2, S]
                half = [P // 2, 2, S]
                lo, hi = slice(0, P // 2), slice(P // 2, P)
                nc.vector.tensor_tensor(ra[:, :].rearrange(two, b=2), src[:, :].rearrange(two, b=2),
                                        cos.unsqueeze(1).broadcast_to(wide), ALU.mult).then_inc(a_set, 1)
                nc.vector.tensor_tensor(rb[lo, :].rearrange(two, b=2), src[hi, :].rearrange(two, b=2),
                                        sin[hi, :].unsqueeze(1).broadcast_to(half), ALU.mult)
                nc.vector.tensor_tensor(rb[hi, :].rearrange(two, b=2), src[lo, :].rearrange(two, b=2),
                                        sin[lo, :].unsqueeze(1).broadcast_to(half), ALU.mult).then_inc(b_set, 1)
                dve.wait_ge(a_set, n + 1)
                dve.wait_ge(b_set, n + 1)
                nc.vector.tensor_tensor(ra[:, :], ra[:, :], rb[:, :], ALU.add).then_inc(summed, 1)

            def rope_q(n, qbank):
                dve.wait_ge(q_done, n + 1)
                at_least(dve, q_lo, n)
                rope(bank[qbank], qa, qb, cos_q[:, :], sin_q[:, :], q_a, q_read, q_roped, n)

            def q_low(n):
                dve.wait_ge(q_hi, n + 1)
                nc.vector.tensor_tensor(q_s[:, 1, :], qa[:, :], q_s[:, 0, :], ALU.subtract).then_inc(q_lo, 1)

            def first_q():
                rope_q(0, 2)
                q_low(0)

            def pair(q, more):
                for g in range(HK):
                    n = HK * q + g
                    if not more:
                        if g % 2 == 0:
                            x_statistics(q, g // 2)
                        else:
                            x_normalise(q, g // 2)
                    dve.wait_ge(k_done, n + 1)
                    at_least(dve, k_lo, HK * q + g - 1)
                    at_least(dve, k_roped, n)
                    rope(bank[2 + g % 2], ka[:, g % 2, :], kb, cos_k, sin_k, kr_a, kr_read, k_roped, n)
                    if isinstance(q, int) and q == 0:
                        for m in first_pieces(g):
                            w1_low(m)
                for v in range(2 * TP + 1):
                    if not more and v == FIRST_Q:
                        first_q()
                    if isinstance(q, int) and q == 0 and v == MASKS - 1:
                        mask_rows_kept()
                    if isinstance(q, int) and q == 0 and v == MASKS:
                        masks_and_gates()
                    if more and v < TP:
                        x_statistics(q, v)
                    for k, (slot, kind, m) in transposes(more):
                        if slot != v:
                            continue
                        t, f = divmod(m, 2)
                        cols = (slice(None), slice(4 * f, 4 * f + 4), slice(t * P, (t + 1) * P))
                        if kind == "ctx":
                            bank_lo(DC + 16 * q, k, ct_lo[cols], ct_hi[cols])
                        else:
                            bank_lo(DC + 16 * q, k, xst[:, 1, m, :], xst[:, 0, m, :])
                    if v == 2 * TP:
                        continue
                    if not more:
                        split_piece(v, v, 0)
                    t, f = divmod(v, 2)
                    dve.wait_ge(v_hi, 2 * TP * q + v + 1)
                    nc.vector.scalar_tensor_tensor(
                        vst[:, 4 * f:4 * f + 4, t, 1, :], bank[4 + v % 2][:, :].rearrange("p (g d) -> p g d", g=4),
                        VS / WS, vst[:, 4 * f:4 * f + 4, t, 0, :], ALU.mult, ALU.subtract).then_inc(v_lo, 1)
                    if more and v < TP:
                        x_normalise(q, v)

            pair(0, True)
            with dve.Fori(1, NP - 1) as q:
                pair(q, True)
            pair(NP - 1, False)

            def o_low(p, pb, ph):
                dve.wait_ge(o_hi, p + 1)
                nc.vector.scalar_tensor_tensor(o_s[:, pb, ph, 1, :], bank[5][:, :], OS / (PS * VS),
                                               o_s[:, pb, ph, 0, :], ALU.mult, ALU.subtract).then_inc(o_lo, 1)

            def add_y(s, yb, t, k, half):
                dve.wait_ge(y_done[k], s - LAG + 1)
                dve.wait_ge(y_in[yb], 16 * (1 + half))
                y_p = y[:, yb, t, 512 * k:512 * k + 512]
                nc.vector.scalar_tensor_tensor(y_p, bank[6 + k][:, :], gates[:, 4:5], y_p, ALU.mult, ALU.add
                                               ).then_inc(y_added[k], 1)

            def bank3_lo(n, dst, hi, src, scale=1.0):
                dve.wait_ge(tr3_hi, n + 1)
                nc.vector.scalar_tensor_tensor(dst, src, scale, hi, ALU.mult, ALU.subtract).then_inc(tr3_lo, 1)

            banks = list(weight_banks())

            def banks_beside(k):
                for i in beside(k):
                    n, hi, lo, src, scale = banks[i]
                    bank3_lo(n, lo, hi, src, scale)

            def steps(it, par, first=False, last=False):
                for u in range(SPI):
                    s = SPI * it + u
                    b_now, h = divmod(u, GQ)
                    lagged = not (first and u < GQ)
                    half = it // HK if b_now == 1 else ((it - 1) // HK if lagged else 0)
                    if lagged:
                        o_low(s - 1, ((u - 1) % SPI) // GQ, (u - 1) % GQ)
                    if not (last and u == SPI - 1):
                        rope_q(s + 1, 2 + (u + 1) % 2)
                    if not lagged and u > 0:
                        o_low(s - 1, 0, u - 1)
                    if lagged:
                        add_y(s, 1 - b_now, h, 0, half)
                    if not (last and u == SPI - 1):
                        q_low(s + 1)
                    else:
                        banks_beside(0)
                    dve.wait_ge(den_done, s + 1)
                    nc.vector.transpose(den_t[:, :], bank[4][:, :]).then_inc(den_read, 1)
                    dve.wait_ge(den_read, s + 1)
                    nc.vector.reciprocal(rden_t[:, :], den_t[:, :].rearrange("p (c j) -> p c j", j=32)[:, :, 0]
                                         ).then_inc(rden_t_done, 1)
                    dve.wait_ge(rden_t_done, s + 1)
                    at_least(dve, weighted, 2 * s)
                    nc.vector.transpose(rden[:, :].rearrange("p (c j) -> p c j", j=32),
                                        rden_t[:, :].unsqueeze(2).broadcast_to([P, PAIR // 32, 32])
                                        ).then_inc(rden_done, 1)
                    dve.wait_ge(rden_done, s + 1)
                    for b in range(2):
                        dve.wait_ge(esum_done, 2 * s + b + 1)
                        nc.vector.tensor_tensor(e_s[u % 2][:, b, :, :], e_s[u % 2][:, b, :, :],
                                                rden[:, b * S:(b + 1) * S].unsqueeze(1).broadcast_to([P, 2, S]),
                                                ALU.mult).then_inc(weighted, 1)
                    for b in range(2):
                        dve.wait_ge(p_hi, 2 * s + b + 1)
                        nc.vector.tensor_tensor(w_s[:, 1, b, :, :], e_s[u % 2][:, b, :, :], w_s[:, 0, b, :, :],
                                                ALU.subtract).then_inc(p_lo, 1)
                    if lagged:
                        add_y(s, 1 - b_now, h, 1, half)
                    if not last:
                        split_piece(8 * it + 8 + u, u, 1 - par)

            steps(0, 0, first=True)
            with dve.Fori(0, NIT // 2 - 1) as j:
                steps(2 * j + 1, 1)
                steps(2 * j + 2, 0)
            steps(NIT - 1, 1, last=True)
            banks_beside(1)
            o_low(NSTEP - 1, PAIRS_PER_HALF - 1, GQ - 1)

            def norm_tile(i, slot, par, x1_loads=0):
                if not (isinstance(i, int) and i < NX):
                    dve.wait_ge(x1_in[slot], 16 * x1_loads)
                at_least(dve, tr3_done, NTR3W + 2 * (i - 1) if not (isinstance(i, int) and i < 2) else 0)
                statistics(ln3_stat, i, x1t[:, slot, :], stats3[:, par, :], mv3[:, par, :])
                normalise(ln3_rstd, ln3, i, x1t[:, slot, :], xn2[:, par, :], mv3[:, par, :])

            def xt_low(i, par):
                for f in range(2):
                    bank3_lo(NTR3W + 2 * i + f, xt_lo[:, par, 4 * f:4 * f + 4, :], xt_hi[:, par, 4 * f:4 * f + 4, :],
                             bank[4 + f][:, :].rearrange("p (c t) -> p c t", c=4))

            banks_beside(2)
            for k in range(2):
                dve.wait_ge(y_added[k], NSTEP - LAG)
            for t in range(TP):
                for k in range(2):
                    add_y(NSTEP + t, PAIRS_PER_HALF - 1, t, k, 1)
                    banks_beside(3 + 2 * t + k)
                    if 2 * t + k == FIRST_XT:
                        xt_low(0, 0)
                if t < 2:
                    norm_tile(t, t, t)
            dve.wait_ge(b3_in, 32)
            nc.vector.tensor_scalar(bias_row[:, :], bias_row[:, :], gates[:, 3:4], None, ALU.mult
                                    ).then_inc(bias_set, 1)
            nc.vector.tensor_scalar(thr_bias[:, 1:2], thr_bias[:, 0:1], 0.5, None, ALU.mult).then_inc(bias_set, 1)

            def output(i, slot, par):
                at_least(dve, out_out[par], 16 * (i // 2))
                dve.wait_ge(x1_biased, i + 1)
                for f in range(2):
                    dve.wait_ge(ffn_done, 2 * i + f + 1)
                    cols = slice(512 * f, 512 * f + 512)
                    nc.vector.scalar_tensor_tensor(out_t[:, par, cols], bank[2 * par + f][:, :], gates[:, 5:6],
                                                   x1t[:, slot, cols], ALU.mult, ALU.add).then_inc(out_set, 1)

            def tile(i, u, first=False, more=1):
                par = u % 2
                G = gsm[:, par, :]
                n = [6 * i]

                def gate(ins):
                    ins.then_inc(gate_step, 1)
                    n[0] = n[0] + 1
                    dve.wait_ge(gate_step, n[0])

                if not first:
                    output(i - 1, (u - 1) % NX, 1 - par)
                if more >= 1:
                    xt_low(i + 1, 1 - par)
                dve.wait_ge(hg_done, i + 1)
                gate(nc.vector.tensor_reduce(G[:, 8:9], bank[6][:, E * R:E * R + E], AX, ALU.max))
                nc.vector.tensor_scalar(G[:, 9:10], G[:, 8:9], -1.0 / WS, None, ALU.mult).then_inc(gmax, 1)
                dve.wait_ge(gexp, 2 * i + 2)
                nc.vector.tensor_scalar(G[:, 11:12], G[:, 10:11], 1.0 / 16, 1.0 / 16, ALU.mult, ALU.add)
                gate(nc.vector.tensor_reduce(G[:, 12:13], G[:, 0:E], AX, ALU.add))
                gate(nc.vector.reciprocal(G[:, 13:14], G[:, 12:13]))
                gate(nc.vector.tensor_scalar(G[:, 16:24], G[:, 0:E], G[:, 13:14], G[:, 11:12],
                                             ALU.mult, ALU.subtract))
                nc.vector.tensor_scalar(G[:, 24:32], G[:, 16:24], 0.0, None, ALU.max).then_inc(gate_step, 1)
                dve.wait_ge(gate_step, 6 * i + 5)
                nc.vector.tensor_reduce(G[:, 32:33], G[:, 24:32], AX, ALU.add).then_inc(gate_step, 1)
                dve.wait_ge(gate_step, 6 * i + 6)
                sum_chain(dve, G, i)
                nc.vector.tensor_tensor(hw[:, :].rearrange("p (e r) -> p e r", e=E),
                                        bank[6][:, 0:E * R].rearrange("p (e r) -> p e r", e=E),
                                        G[:, 40:48].unsqueeze(2).broadcast_to([P, E, R]), ALU.mult
                                        ).then_inc(hw_set, 1)
                if more >= 2:
                    norm_tile(i + 2, (u + 2) % NX, par, (i + 2) // NX)
                dve.wait_ge(hwt_hi, i + 1)
                nc.vector.tensor_tensor(hwt[:, 1, :], bank[7][:, 0:P], hwt[:, 0, :], ALU.subtract
                                        ).then_inc(hwt_lo, 1)

            def sum_chain(dve, G, i):
                nc.vector.tensor_scalar(G[:, 33:34], G[:, 32:33], 0.0, G[:, 32:33], ALU.is_equal, ALU.add
                                        ).then_inc(wsum_step, 1)
                dve.wait_ge(wsum_step, 3 * i + 1)
                nc.vector.reciprocal(G[:, 34:35], G[:, 33:34]).then_inc(wsum_step, 1)
                dve.wait_ge(wsum_step, 3 * i + 2)
                nc.vector.tensor_scalar(G[:, 40:48], G[:, 24:32], G[:, 34:35], HS / WS, ALU.mult, ALU.mult
                                        ).then_inc(wsum_step, 1)
                dve.wait_ge(wsum_step, 3 * i + 3)

            tile(0, 0, first=True, more=2)
            for u in range(1, NX):
                tile(u, u, more=2)
            with dve.Fori(1, NT // NX - 1) as j:
                for u in range(NX):
                    tile(j * NX + u, u, more=2)
            for u in range(NX):
                tile(NT - NX + u, u, more=min(2, NX - 1 - u))
            output(NT - 1, NX - 1, 1)

        @block.tensor
        def _(pe):
            mm = nc.tensor.matmul

            def three(dst, st_hi, st_lo, mv_hi, mv_lo, start, stop):
                mm(dst, st_hi, mv_hi, start=start, stop=False)
                mm(dst, st_hi, mv_lo, start=False, stop=False)
                return mm(dst, st_lo, mv_hi, start=False, stop=stop)

            def transpose4(done, dst, srcs):
                for k, src in enumerate(srcs):
                    i = nc.tensor.transpose(dst[:, k * P:(k + 1) * P], src, ident)
                i.then_inc(done, 1)

            pe.wait_ge(ident_in, 16)

            def ctx_bank(first, n, t, f):
                at_least(pe, tr_lo, first + n - 3)
                transpose4(tr_done, bank[TR_BANKS[n % 4]], [ctx_raw[:, t, (4 * f + k) * P:(4 * f + k + 1) * P] for k in range(4)])

            for m in range(DC):
                t, f = divmod(m, 2)
                pe.wait_ge(ctx_in[t], 16)
                ctx_bank(0, m, t, f)

            def mask_banks():
                pe.wait_ge(setup_dve, 10)
                pe.wait_ge(kr_read, HK)
                for c in range(2):
                    for k in range(2):
                        i = nc.tensor.transpose(bank[2][:, c * S + k * P:c * S + (k + 1) * P],
                                                mask_f[:, k, c * P:(c + 1) * P], ident)
                i.then_inc(mask_tr, 1)
                for k in range(2):
                    i = nc.tensor.transpose(bank[3][:, k * P:(k + 1) * P], row_wide[:, k, :], ident)
                i.then_inc(mask_tr, 1)

            def q_part(n, qbank, par, b, h, part):
                if part == 0:
                    at_least(pe, q_read, n - 1)
                cols = slice(h * DH, (h + 1) * DH)
                for c in range(4 * part, 4 * part + 4):
                    i = three(bank[qbank][:, :], wq_s[par][:, 0, c, cols], wq_s[par][:, 1, c, cols],
                              xn[:, b, 0, c, :], xn[:, b, 1, c, :], c == 0, c == DC - 1)
                if part == 1:
                    i.then_inc(q_done, 1)

            def first_q():
                pe.wait_ge(w_lo, 4)
                pe.wait_ge(xn_in[0], 16)
                pe.wait_ge(kr_read, HK * NP)
                q_part(0, 2, 0, 0, 0, 0)
                q_part(0, 2, 0, 0, 0, 1)

            def pair(q, more):
                for g in range(HK):
                    if isinstance(q, int) and q == 0:
                        pe.wait_ge(wk_lo_set, g + 1)
                    at_least(pe, kr_read, HK * q + max(g - 1, 0))
                    for c in range(DC):
                        if g == 0 and c % 4 == 0:
                            pe.wait_ge(tr_lo, DC + 16 * q - 1 + c // 4)
                        w = slice(g * DH, (g + 1) * DH)
                        i = three(bank[2 + g % 2][:, :], wk_hi[:, c, w], wk_lo[:, c, w], ct_hi[:, c, :],
                                  ct_lo[:, c, :], c == 0, c == DC - 1)
                    i.then_inc(k_done, 1)
                for v in range(2 * TP + 1):
                    if not more and v == FIRST_Q:
                        first_q()
                    if isinstance(q, int) and q == 0 and v == MASKS:
                        mask_banks()
                    for k, (slot, kind, m) in transposes(more):
                        if slot != v:
                            continue
                        t, f = divmod(m, 2)
                        if kind == "ctx":
                            pe.wait_ge(ctx_in[t], 16 * (q + 2))
                            ctx_bank(DC + 16 * q, k, t, f)
                        else:
                            pe.wait_ge(tr_lo, DC + 16 * q + k - 3)
                            pe.wait_ge(ln1, TP * (q + 1))
                            transpose4(tr_done, bank[TR_BANKS[k % 4]], [x_raw[:, t, m * P:(m + 1) * P] for t in range(TP)])
                    if v == 2 * TP:
                        continue
                    t, f = divmod(v, 2)
                    if v < 2:
                        pe.wait_ge(wv_lo_set, 4 + 4 * v)
                    at_least(pe, v_lo, 2 * TP * q + max(v - 1, 0))
                    for c in range(DC):
                        r, w = slice(t * P, (t + 1) * P), slice(f * 512, (f + 1) * 512)
                        i = three(bank[4 + v % 2][:, :], ct_hi[:, c, r], ct_lo[:, c, r], wv_hi[:, c, w],
                                  wv_lo[:, c, w], c == 0, c == DC - 1)
                    i.then_inc(v_done, 1)

            pair(0, True)
            pe.wait_ge(setup_dve, 13)
            with pe.Fori(1, NP - 1) as q:
                pair(q, True)
            pair(NP - 1, False)

            def av(p, pb):
                at_least(pe, o_lo, p)
                for b in range(2):
                    pe.wait_ge(p_hi, 2 * p + b + 1)
                    pe.wait_ge(p_lo, 2 * p + b + 1)
                    for k in range(2):
                        t = 2 * b + k
                        i = three(bank[5][:, b * S:(b + 1) * S], vt[:, pb, t, 0, :], vt[:, pb, t, 1, :],
                                  w_s[:, 0, b, k, :], w_s[:, 1, b, k, :], k == 0, k == 1)
                i.then_inc(av_done, 1)

            def wo_part(s, ob, par, t, k, heads=range(GQ)):
                if heads[0] == 0:
                    at_least(pe, y_added[k], s - LAG)
                rows, cols = slice(t * P, (t + 1) * P), slice(512 * k, 512 * k + 512)
                for h in heads:
                    i = three(bank[6 + k][:, :], o_s[:, ob, h, 0, rows], o_s[:, ob, h, 1, rows],
                              wo_s[par][:, 0, h, cols], wo_s[par][:, 1, h, cols], h == 0, h == GQ - 1)
                if heads[-1] == GQ - 1:
                    i.then_inc(y_done[k], 1)

            pe.wait_ge(tr_lo, NTR1)

            def banks_beside(j):
                for n in beside(j):
                    if n == 0:
                        pe.wait_ge(q_read, NSTEP)
                    if n == 2:
                        pe.wait_ge(tanh_done, 2 * NSTEP)
                    at_least(pe, tr3_lo, n - 3)
                    b = bank[W_BANKS[n % 4]]
                    if n < 2 * DC:
                        f, c = divmod(n, DC)
                        if c == 0:
                            pe.wait_ge(wb_in[f], 16 * 4)
                        transpose4(tr3_done, b, [wb_raw[:, 4 * f + k, c * P:(c + 1) * P] for k in range(4)])
                    elif n < 3 * DC:
                        c = n - 2 * DC
                        pe.wait_ge(g3_in, 16 * 3)
                        nc.tensor.transpose(b[:, 0:P], a_raw[:, c * P:(c + 1) * P], ident)
                        nc.tensor.transpose(b[:, P:HGW], gt_raw[0:NG, c * P:(c + 1) * P], ident[0:NG, 0:NG]
                                            ).then_inc(tr3_done, 1)
                    else:
                        f = n - 3 * DC
                        pe.wait_ge(bup_in, 16 * DC)
                        transpose4(tr3_done, b,
                                   [b_raw[:, 4 * f + k, :, :].rearrange("p e r -> p (e r)") for k in range(4)])

            def steps(it, par, first=False, last=False):
                for u in range(SPI):
                    s = SPI * it + u
                    b_now, h = divmod(u, GQ)
                    lagged = not (first and u < GQ)
                    ends = last and u == SPI - 1
                    if h == 0:
                        pe.wait_ge(kv_in[b_now], 32 * (it + 1))
                    pe.wait_ge(q_hi, s + 1)
                    pe.wait_ge(q_lo, s + 1)
                    for b in range(2):
                        at_least(pe, tanh_done, 2 * s - 1 + b if not (first and u == 0) else 0)
                        for k in range(2):
                            keys = slice(b * S + k * P, b * S + (k + 1) * P)
                            qs = slice(b * S, (b + 1) * S)
                            i = three(bank[b][:, k * S:(k + 1) * S], kt[:, b_now, 0, keys], kt[:, b_now, 1, keys],
                                      q_s[:, 0, qs], q_s[:, 1, qs], True, True)
                        i.then_inc(logits_done, 1)
                    nu = (u + 1) % SPI
                    nb, nh = divmod(nu, GQ)
                    npar = par if nu else 1 - par
                    if not ends:
                        if nu == 0:
                            pe.wait_ge(w_lo, 8 * it + 8 + 4)
                        if nh == 0:
                            pe.wait_ge(xn_in[nb], 16 * (1 + ((it + 1) // HK if nu == 0 else it // HK)))
                        q_part(s + 1, 2 + nu % 2, npar, nb, nh, 0)
                    wpar = par if b_now == 1 else 1 - par
                    if ends:
                        wo_part(s, 1 - b_now, wpar, h, 0)
                    if not lagged:
                        q_part(s + 1, 2 + nu % 2, npar, nb, nh, 1)
                    if not (first and u == 0):
                        av(s - 1, ((u - 1) % SPI) // GQ)
                    if lagged and not ends:
                        q_part(s + 1, 2 + nu % 2, npar, nb, nh, 1)
                    if lagged:
                        if h == 0:
                            pe.wait_ge(w_lo, 8 * (it + 1) if b_now == 1 else 8 * it)
                            pe.wait_ge(o_lo, s)
                        if not ends:
                            wo_part(s, 1 - b_now, wpar, h, 0)
                        wo_part(s, 1 - b_now, wpar, h, 1, range(1))
                    if first and u == 0:
                        pe.wait_ge(v_lo, 2 * TP * NP)
                        pe.wait_ge(ones_set, 1)
                    if ends:
                        banks_beside(0)
                    at_least(pe, den_read, s)
                    pe.wait_ge(esum_lo, s + 1)
                    for k in range(2):
                        i = mm(bank[4][:, :], ones_r[:, :], esum_r[:, k, :], start=k == 0, stop=k == 1)
                    i.then_inc(den_done, 1)
                    if lagged:
                        wo_part(s, 1 - b_now, wpar, h, 1, range(1, GQ))

            steps(0, 0, first=True)
            with pe.Fori(0, NIT // 2 - 1) as j:
                steps(2 * j + 1, 1)
                steps(2 * j + 2, 0)
            steps(NIT - 1, 1, last=True)
            banks_beside(1)
            av(NSTEP - 1, PAIRS_PER_HALF - 1)
            banks_beside(2)

            def xt_banks(i, par):
                pe.wait_ge(ln3, i + 1)
                at_least(pe, tr3_lo, NTR3W + 2 * i if not (isinstance(i, int) and i == 0) else 0)
                for f in range(2):
                    transpose4(tr3_done, bank[4 + f], [xn2[:, par, (4 * f + k) * P:(4 * f + k + 1) * P]
                                                       for k in range(4)])

            pe.wait_ge(o_lo, NSTEP)
            for t in range(TP):
                for k in range(2):
                    wo_part(NSTEP + t, PAIRS_PER_HALF - 1, 1, t, k)
                    banks_beside(3 + 2 * t + k)
                    if 2 * t + k == FIRST_XT:
                        pe.wait_ge(den_read, NSTEP)
                        xt_banks(0, 0)
            pe.wait_ge(y_added[0], NSTEP)
            pe.wait_ge(y_added[1], NSTEP)

            def tile(i, par, more):
                pe.wait_ge(tr3_lo, NTR3W + 2 * i + 2)
                at_least(pe, hw_set, i)
                for c in range(DC):
                    ins = three(bank[6][:, 0:HGW], xt_hi[:, par, c, :], xt_lo[:, par, c, :],
                                ag_hi[:, c, 0:HGW], ag_lo[:, c, 0:HGW], c == 0, c == DC - 1)
                ins.then_inc(hg_done, 1)
                if more:
                    xt_banks(i + 1, 1 - par)
                for f in range(2):
                    at_least(pe, out_set, 2 * i - 3 + f if not (isinstance(i, int) and i < 2) else 0)
                    cols = slice(512 * f, 512 * f + 512)
                    for c in range(DC):
                        three(bank[2 * par + f][:, :], xt_hi[:, par, c, :], xt_lo[:, par, c, :],
                              wb_hi[:, c, cols], wb_lo[:, c, cols], c == 0, False)
                    if f == 0:
                        pe.wait_ge(hw_set, i + 1)
                        at_least(pe, hwt_lo, i)
                        nc.tensor.transpose(bank[7][:, 0:P], hw[:, :], ident).then_inc(hwt_done, 1)
                pe.wait_ge(hwt_lo, i + 1)
                for f in range(2):
                    cols = slice(512 * f, 512 * f + 512)
                    three(bank[2 * par + f][:, :], hwt[:, 0, :], hwt[:, 1, :], bt_hi[:, cols], bt_lo[:, cols],
                          False, True).then_inc(ffn_done, 1)

            tile(0, 0, True)
            tile(1, 1, True)
            with pe.Fori(1, NT // 2 - 1) as j:
                tile(2 * j, 0, True)
                tile(2 * j + 1, 1, True)
            tile(NT - 2, 0, True)
            tile(NT - 1, 1, False)


def rope_tables():
    import numpy as np
    exponents = np.arange(0, DH, 2, dtype=np.float32)
    inv_freq = (np.float32(1.0) / np.float32(10000.0) ** (exponents / np.float32(DH))).astype(np.float32)
    phase = (np.arange(S, dtype=np.float32)[:, None] * inv_freq[None, :]).astype(np.float32).T
    cos = np.cos(phase).astype(np.float32) * np.float32(QS / WS)
    sin = np.sin(phase).astype(np.float32) * np.float32(QS / WS)
    return np.ascontiguousarray(np.concatenate([
        np.concatenate([cos, cos], 0), np.concatenate([sin, -sin], 0), np.eye(P, dtype=np.float32)], 1))


NAMES = ['x', 'ctx_4096', 'mask_1x1xSxS2_bk0', 'g_xattn', 'g_ffn', 'L0_xattn_Wq', 'L0_xattn_Wk', 'L0_xattn_Wv',
         'L0_xattn_Wo', 'L0_ffn_W_base', 'L0_ffn_b_base', 'L0_ffn_W_gate', 'L0_ffn_W_thr', 'L0_ffn_b_thr',
         'L0_ffn_A', 'L0_ffn_B']


def kernel(**inputs):
    import numpy as np
    import concourse.bacc as bacc
    from concourse.bass_utils import run_bass_kernel_spmd

    nc = bacc.Bacc("TRN2", target_bir_lowering=False, num_devices=1)
    arrays, args = {}, []

    def give(name, a):
        arrays[name] = a
        args.append(nc.dram_tensor(name, a.shape, mybir.dt.from_np(a.dtype), kind="ExternalInput").ap())

    for name in NAMES:
        give("in_" + name, np.ascontiguousarray(inputs[name]))
    give("tables", rope_tables())
    out = nc.dram_tensor("out_x", (NB, S, D), F32, kind="ExternalOutput").ap()
    build(nc, *args, out)
    r = run_bass_kernel_spmd(nc, [arrays], core_ids=[0])
    return r.results[0]["out_x"]
```
